# Optimizing a Trainium2 kernel written in Bass

```python
import numpy as np
import jax
import jax.numpy as jnp

def _softmax(x, axis=-1):
    return jax.nn.softmax(x, axis=axis)

def _gelu(x):
    return jax.nn.gelu(x, approximate=True)

def _silu(x):
    return jax.nn.silu(x)

def _sigmoid(x):
    return jax.nn.sigmoid(x)

def _layernorm(x, axis=-1, eps=1e-05):
    m = jnp.mean(x, axis=axis, keepdims=True)
    v = jnp.var(x, axis=axis, keepdims=True)
    return (x - m) / jnp.sqrt(v + eps)

def _scatter_add(tgt, idx, src, axis=0):
    return tgt.at[idx].add(src)

def _segment_sum(src, seg, n):
    return jax.ops.segment_sum(src, seg, n)
kernel_name = 'mk_seq_postln_d2_jaxref_r4_b70db3'

def setup_inputs(seed: int=0):
    np.random.seed(seed)
    _w = jnp.asarray

    def _L0_attn_setup():
        import jax, jax.numpy as jnp
        import numpy as np
        E = 256
        H = 16
        HD = E // H
        MAX_REL = 20
        key = jax.random.key(seed)
        ks = jax.random.split(key, 12)
        B, S = (4, 256)

        def lin_w(k):
            return jax.random.normal(k, (E, E), dtype=jnp.float32) * (1.0 / np.sqrt(E))
        return {'hidden_states': jax.random.normal(ks[0], (B, S, E), dtype=jnp.float32), 'Wq': lin_w(ks[1]), 'bq': jnp.zeros((E,), jnp.float32), 'Wk': lin_w(ks[2]), 'bk': jnp.zeros((E,), jnp.float32), 'Wv': lin_w(ks[3]), 'bv': jnp.zeros((E,), jnp.float32), 'Wo': lin_w(ks[4]), 'bo': jnp.zeros((E,), jnp.float32), 'rel_k': jax.random.uniform(ks[5], (2 * MAX_REL + 1, HD), jnp.float32, -0.24, 0.24), 'rel_v': jax.random.uniform(ks[6], (2 * MAX_REL + 1, HD), jnp.float32, -0.24, 0.24)}
    _L0_attn_in = _L0_attn_setup()

    def _L0_ffn_setup():
        import jax, jax.numpy as jnp
        import numpy as np
        B, S, H, R, F, E, K = (4, 512, 256, 64, 1024, 8, 2)
        key = jax.random.key(seed)
        k = jax.random.split(key, 7)
        s = 0.02
        return {'x': jax.random.normal(k[0], (B, S, H), dtype=jnp.float32), 'router_w': jax.random.normal(k[1], (H, E), dtype=jnp.float32) * s, 'router_b': jnp.zeros((E,), dtype=jnp.float32), 'w1': jax.random.normal(k[2], (E, H, R), dtype=jnp.float32) * s, 'w2': jax.random.normal(k[3], (E, R, F), dtype=jnp.float32) * s, 'lin2_w': jax.random.normal(k[4], (F, H), dtype=jnp.float32) * s, 'lin2_b': jnp.zeros((H,), dtype=jnp.float32)}
    _L0_ffn_in = _L0_ffn_setup()

    def _L1_attn_setup():
        import jax, jax.numpy as jnp
        import numpy as np
        DIM = 256
        HEADS = 16
        DIM_HEAD = 64
        INNER = HEADS * DIM_HEAD
        EPS = 1e-06

        def elu_feature_map(t):
            return jnp.where(t > 0, t + 1.0, jnp.exp(t))
        key = jax.random.key(seed)
        k1, k2, k3, k4 = jax.random.split(key, 4)
        B, N = (4, 2048)
        x = jax.random.normal(k1, (B, N, DIM), dtype=jnp.float32)
        s_in = 1.0 / np.sqrt(DIM)
        s_out = 1.0 / np.sqrt(INNER)
        Wqkv = jax.random.uniform(k2, (DIM, 3 * INNER), dtype=jnp.float32, minval=-s_in, maxval=s_in)
        Wout = jax.random.uniform(k3, (INNER, DIM), dtype=jnp.float32, minval=-s_out, maxval=s_out)
        bout = jax.random.uniform(k4, (DIM,), dtype=jnp.float32, minval=-s_out, maxval=s_out)
        return {'x': x, 'Wqkv': Wqkv, 'Wout': Wout, 'bout': bout}
    _L1_attn_in = _L1_attn_setup()

    def _L1_ffn_setup():
        import jax, jax.numpy as jnp
        import numpy as np
        D, H, O, E, K = (256, 512, 256, 8, 2)
        B, S = (4, 256)
        key = jax.random.key(seed)
        ks = jax.random.split(key, 8)
        scale = 0.02
        return {'hidden_states': jax.random.normal(ks[0], (B, S, D), jnp.float32), 'router_w': jax.random.normal(ks[1], (E, D), jnp.float32) * scale, 'sg': jax.random.normal(ks[2], (H, D), jnp.float32) * scale, 'su': jax.random.normal(ks[3], (H, D), jnp.float32) * scale, 'sd': jax.random.normal(ks[4], (O, H), jnp.float32) * scale, 'eg': jax.random.normal(ks[5], (E, H, D), jnp.float32) * scale, 'eu': jax.random.normal(ks[6], (E, H, D), jnp.float32) * scale, 'ed': jax.random.normal(ks[7], (E, O, H), jnp.float32) * scale}
    _L1_ffn_in = _L1_ffn_setup()
    _d = {'L0_attn_hidden_states': _L0_attn_in['hidden_states'], 'L0_attn_Wq': _L0_attn_in['Wq'], 'L0_attn_bq': _L0_attn_in['bq'], 'L0_attn_Wk': _L0_attn_in['Wk'], 'L0_attn_bk': _L0_attn_in['bk'], 'L0_attn_Wv': _L0_attn_in['Wv'], 'L0_attn_bv': _L0_attn_in['bv'], 'L0_attn_Wo': _L0_attn_in['Wo'], 'L0_attn_bo': _L0_attn_in['bo'], 'L0_attn_rel_k': _L0_attn_in['rel_k'], 'L0_attn_rel_v': _L0_attn_in['rel_v'], 'L0_ffn_router_w': _L0_ffn_in['router_w'], 'L0_ffn_router_b': _L0_ffn_in['router_b'], 'L0_ffn_w1': _L0_ffn_in['w1'], 'L0_ffn_w2': _L0_ffn_in['w2'], 'L0_ffn_lin2_w': _L0_ffn_in['lin2_w'], 'L0_ffn_lin2_b': _L0_ffn_in['lin2_b'], 'L1_attn_Wqkv': _L1_attn_in['Wqkv'], 'L1_attn_Wout': _L1_attn_in['Wout'], 'L1_attn_bout': _L1_attn_in['bout'], 'L1_ffn_router_w': _L1_ffn_in['router_w'], 'L1_ffn_sg': _L1_ffn_in['sg'], 'L1_ffn_su': _L1_ffn_in['su'], 'L1_ffn_sd': _L1_ffn_in['sd'], 'L1_ffn_eg': _L1_ffn_in['eg'], 'L1_ffn_eu': _L1_ffn_in['eu'], 'L1_ffn_ed': _L1_ffn_in['ed']}
    _x0 = _d['L0_attn_hidden_states']
    _d['L0_attn_hidden_states'] = jax.random.normal(jax.random.fold_in(jax.random.key(seed), 1), (2, 2048, 256), dtype=_x0.dtype)
    del _x0
    return _d

def reference(L0_attn_hidden_states, L0_attn_Wq, L0_attn_bq, L0_attn_Wk, L0_attn_bk, L0_attn_Wv, L0_attn_bv, L0_attn_Wo, L0_attn_bo, L0_attn_rel_k, L0_attn_rel_v, L0_ffn_router_w, L0_ffn_router_b, L0_ffn_w1, L0_ffn_w2, L0_ffn_lin2_w, L0_ffn_lin2_b, L1_attn_Wqkv, L1_attn_Wout, L1_attn_bout, L1_ffn_router_w, L1_ffn_sg, L1_ffn_su, L1_ffn_sd, L1_ffn_eg, L1_ffn_eu, L1_ffn_ed):

    def _L0_attn_ref(hidden_states, Wq, bq, Wk, bk, Wv, bv, Wo, bo, rel_k, rel_v):
        import jax, jax.numpy as jnp
        import numpy as np
        E = 256
        H = 16
        HD = E // H
        MAX_REL = 20
        B, S, _ = hidden_states.shape
        scale = jnp.sqrt(jnp.float32(HD))

        def proj(W, b):
            return (hidden_states @ W.T + b).reshape(B, S, H, HD).transpose(0, 2, 1, 3)
        q = proj(Wq, bq)
        k = proj(Wk, bk)
        v = proj(Wv, bv)
        pos = jnp.arange(S)
        idx = jnp.clip(pos[None, :] - pos[:, None], -MAX_REL, MAX_REL) + MAX_REL
        rk2 = rel_k[idx]
        rv2 = rel_v[idx]
        attn1 = jnp.einsum('bhqd,bhkd->bhqk', q, k)
        attn2 = jnp.einsum('bhqd,qkd->bhqk', q, rk2)
        attn = jax.nn.softmax((attn1 + attn2) / scale, axis=-1)
        w1 = jnp.einsum('bhqk,bhkd->bhqd', attn, v)
        w2 = jnp.einsum('bhqk,qkd->bhqd', attn, rv2)
        x = (w1 + w2).transpose(0, 2, 1, 3).reshape(B, S, E)
        out = x @ Wo.T + bo
        return out

    def _L0_ffn_ref(x, router_w, router_b, w1, w2, lin2_w, lin2_b):
        import jax, jax.numpy as jnp
        import numpy as np
        B, S, H, R, F, E, K = (4, 512, 256, 64, 1024, 8, 2)
        logits = jnp.einsum('bsh,he->bse', x, router_w) + router_b
        routing_weights = jax.nn.softmax(logits, axis=-1)
        _, topk_idx = jax.lax.top_k(routing_weights, K)
        mask = jnp.sum(jax.nn.one_hot(topk_idx, E, dtype=x.dtype), axis=-2)
        mw = routing_weights * mask
        t = jnp.einsum('bsh,ehr->bser', x, w1)
        t = t * mw[..., None]
        mixed = jnp.einsum('bser,erf->bsf', t, w2)
        h = jax.nn.gelu(mixed, approximate=False)
        out = jnp.einsum('bsf,fh->bsh', h, lin2_w) + lin2_b
        return out

    def _L1_attn_ref(x, Wqkv, Wout, bout):
        import jax, jax.numpy as jnp
        import numpy as np
        DIM = 256
        HEADS = 16
        DIM_HEAD = 64
        INNER = HEADS * DIM_HEAD
        EPS = 1e-06

        def elu_feature_map(t):
            return jnp.where(t > 0, t + 1.0, jnp.exp(t))
        B, N, D = x.shape
        qkv = x @ Wqkv
        q, k, v = jnp.split(qkv, 3, axis=-1)
        resh = lambda t: t.reshape(B, N, HEADS, DIM_HEAD).transpose(0, 2, 1, 3)
        q, k, v = (resh(q), resh(k), resh(v))
        q = elu_feature_map(q)
        k = elu_feature_map(k)
        kv = jnp.einsum('bhnd,bhnf->bhdf', k, v)
        k_sum = k.sum(axis=-2)
        qkv_out = jnp.einsum('bhnd,bhdf->bhnf', q, kv)
        q_k_sum = jnp.einsum('bhnd,bhd->bhn', q, k_sum)
        out = qkv_out / (q_k_sum[..., None] + EPS)
        out = out.transpose(0, 2, 1, 3).reshape(B, N, INNER)
        return out @ Wout + bout

    def _L1_ffn_ref(hidden_states, router_w, sg, su, sd, eg, eu, ed):
        import jax, jax.numpy as jnp
        import numpy as np
        D, H, O, E, K = (256, 512, 256, 8, 2)
        B, S = (4, 256)
        b, s, d = hidden_states.shape
        shared_out = jnp.einsum('bsh,oh->bso', jax.nn.silu(jnp.einsum('bsd,hd->bsh', hidden_states, sg)) * jnp.einsum('bsd,hd->bsh', hidden_states, su), sd)
        flat = hidden_states.reshape(-1, d)
        T = flat.shape[0]
        logits = flat @ router_w.T
        probs = jax.nn.softmax(logits.astype(jnp.float32), axis=-1)
        topk_w, topk_idx = jax.lax.top_k(probs, K)
        topk_w = topk_w / jnp.sum(topk_w, axis=-1, keepdims=True)
        topk_w = topk_w.astype(hidden_states.dtype)
        combine = jnp.zeros((T, probs.shape[-1]), hidden_states.dtype)
        combine = combine.at[jnp.arange(T)[:, None], topk_idx].add(topk_w)
        gate = jnp.einsum('td,ehd->teh', flat, eg)
        up = jnp.einsum('td,ehd->teh', flat, eu)
        eout = jnp.einsum('teh,eoh->teo', jax.nn.silu(gate) * up, ed)
        routed = jnp.einsum('teo,te->to', eout, combine)
        return shared_out + routed.reshape(b, s, -1)
    x = L0_attn_hidden_states
    x = _layernorm(x + _L0_attn_ref(x, L0_attn_Wq, L0_attn_bq, L0_attn_Wk, L0_attn_bk, L0_attn_Wv, L0_attn_bv, L0_attn_Wo, L0_attn_bo, L0_attn_rel_k, L0_attn_rel_v), axis=-1)
    x = _layernorm(x + _L0_ffn_ref(x, L0_ffn_router_w, L0_ffn_router_b, L0_ffn_w1, L0_ffn_w2, L0_ffn_lin2_w, L0_ffn_lin2_b), axis=-1)
    x = _layernorm(x + _L1_attn_ref(x, L1_attn_Wqkv, L1_attn_Wout, L1_attn_bout), axis=-1)
    x = _layernorm(x + _L1_ffn_ref(x, L1_ffn_router_w, L1_ffn_sg, L1_ffn_su, L1_ffn_sd, L1_ffn_eg, L1_ffn_eu, L1_ffn_ed), axis=-1)
    return x

_drawn_inputs = setup_inputs


def setup_inputs(seed=0):
    import zlib

    import numpy as np

    out = dict(_drawn_inputs(seed))
    spreads = {'L0_attn_bq': (0.0, 0.8),
     'L0_attn_bk': (0.0, 2.0),
     'L0_attn_bv': (0.0, 0.1),
     'L0_attn_bo': (0.0, 0.1),
     'L0_ffn_router_b': (0.0, 0.8),
     'L0_ffn_lin2_b': (0.0, 0.1)}
    factors = {'L0_attn_rel_k': 7.449,
     'L0_ffn_router_w': 8.0,
     'L0_ffn_w1': 8.0,
     'L0_ffn_w2': 8.0,
     'L0_ffn_lin2_w': 8.0,
     'L1_attn_bout': 3.344,
     'L1_ffn_router_w': 3.818,
     'L1_ffn_eg': 3.368,
     'L1_ffn_eu': 3.334,
     'L1_ffn_ed': 3.331,
     'L1_ffn_sg': 3.012,
     'L1_ffn_su': 2.938,
     'L1_ffn_sd': 2.962}
    for name, (base, spread) in spreads.items():
        noise = np.random.default_rng([zlib.crc32(name.encode()), seed]).standard_normal(out[name].shape)
        drawn = base * np.exp(spread * noise) if base else spread * noise
        out[name] = jnp.asarray(drawn.astype(out[name].dtype))
    for name, factor in factors.items():
        out[name] = (out[name] * factor).astype(out[name].dtype)
    return out
```

```python
from contextlib import ExitStack

import numpy as np

import concourse.bass as bass
from concourse import mybir

F32 = mybir.dt.float32
F32R = mybir.dt.float32r
BF16 = mybir.dt.bfloat16
ALU = mybir.AluOpType
ACT = mybir.ActivationFunctionType
AX = mybir.AxisListType
RMAX = bass.bass_isa.ReduceOp.max

P = 128
B, S, E = 2, 2048, 256
T = B * S
H, HD = 16, 16
REL = 20
NREL = 2 * REL + 1
EK2 = E // P
CH = 512
NCH = T // CH
CPB = S // CH
KT = S // P
PAD = REL - 1
W = P + 2 * PAD
HALF = 1024
NH = B * H
NHP = NH + 4
VC = 50
EPS = 1e-5


def semaphores(nc, ctx, stage):
    mine = []

    def end():
        nc.clear_and_free_semaphores(mine)
        nc.all_engine_barrier()

    def sem(name):
        mine.append(nc.alloc_semaphore(name=f"{stage}_{name}"))
        return mine[-1]
    ctx.callback(end)
    return sem


def project_qkv(nc, t, scratch):
    qs, kh, kl, vs = scratch
    with ExitStack() as ctx:
        sb = lambda n, s, d: ctx.enter_context(nc.sbuf_tensor("qkv_" + n, s, d))
        ps = lambda n, s: ctx.enter_context(nc.psum_tensor("qkv_" + n, s, F32))
        sem = semaphores(nc, ctx, "qkv")
        wts = sb("wts", [P, 3, EK2, E], F32)
        cols = sb("cols", [P, EK2, 4], F32)
        kbias = sb("kbias", [P, EK2, 2], F32)
        rows = sb("rows", [P, 3, E], F32)
        vrow = sb("vrow", [P, 2, E], F32)
        xc = [sb(f"xc{i}", [P, EK2, CH], F32) for i in range(2)]
        full = [sb(f"full{i}", [P, CH], F32) for i in range(2)]
        rest = [sb(f"rest{i}", [P, CH], F32) for i in range(2)]
        part = [sb(f"part{i}", [P, 3, CH], BF16) for i in range(4)]
        vfull = [sb(f"vfull{i}", [P, 4 * E], F32) for i in range(2)]
        vrest = [sb(f"vrest{i}", [P, 4 * E], F32) for i in range(2)]
        vst = sb("vst", [P, 2, H, KT, VC], BF16)
        acc = [ps(f"acc{i}", [P, CH]) for i in range(4)]
        vacc = ps("vacc", [P, 4 * E])
        w_in, x_in0, x_in1 = sem("w_in"), sem("x_in0"), sem("x_in1")
        x_in = [x_in0, x_in1]
        prep, qk_mm, v_mm = sem("prep"), sem("qk_mm"), sem("v_mm")
        f_rdy, p1_rdy, r_rdy, p2_rdy, p3_rdy = (sem(n) for n in ("f_rdy", "p1_rdy", "r_rdy", "p2_rdy", "p3_rdy"))
        vf_rdy, v1_rdy, vr_rdy, v2_rdy, v3_rdy = (sem(n) for n in ("vf_rdy", "v1_rdy", "vr_rdy", "v2_rdy", "v3_rdy"))
        part_out = [sem(f"part_out{i}") for i in range(4)]
        v_out, pad_out = sem("v_out"), sem("pad_out")
        units = [(0, ("q", 0), qs, 0), (1, ("q", 1), qs, 1), (2, (0, 0), kh, 0), (2, (0, 1), kl, 0),
                 (3, (1, 0), kh, 1), (3, (1, 1), kl, 1)]
        NU = len(units)
        NUB = NU * CPB

        def bias_of(key):
            return cols[:, key[1], 0:1] if key[0] == "q" else kbias[:, key[0], key[1]:key[1] + 1]

        def v_view(buf):
            return buf[:].rearrange("p (t h d) -> p h t d", t=4, h=H)

        def v_part(hl, c, n):
            return vst[:, hl, :, 4 * c:4 * c + 4, n * HD:(n + 1) * HD]

        def s_slot(c, s):
            return (c * NU + s) % 4

        with nc.Block() as block:
            @block.sync
            def _(sp):
                sp.dma_start(wts[:], t["wqkv"].rearrange("w (k p) n -> p w k n", p=P)).then_inc(w_in, 16)
                sp.dma_start(cols[:], t["cols"].rearrange("(k p) n -> p k n", p=P)).then_inc(w_in, 16)
                sp.dma_start(rows[:], t["rows"]).then_inc(w_in, 16)
                with sp.Fori(0, B) as b:
                    for c in range(CPB):
                        if c >= 2:
                            sp.wait_ge(v_mm, b * CPB + c - 1)
                        else:
                            sp.wait_ge(v_mm, b * CPB)
                        sp.dma_start(xc[c % 2][:], t["xt"].rearrange("(k p) n -> p k n", p=P)[
                            :, :, bass.ds(b * S + c * CH, CH)]).then_inc(x_in[c % 2], 16)
                        for s, (_, _, dst, e) in enumerate(units):
                            sp.wait_ge(p3_rdy, b * NUB + c * NU + s + 1)
                            sp.dma_start(dst.rearrange("a r n -> r a n")[
                                bass.ds(b * E + e * P, P), :, c * CH:(c + 1) * CH],
                                part[s_slot(c, s)][:]).then_inc(part_out[s_slot(c, s)], 16)
                    sp.wait_ge(v3_rdy, b * 2 * CPB + 2 * CPB)
                    for l in range(2):
                        sp.dma_start(vs.rearrange("h l p c -> p h l c")[:, bass.ds(b * H, H), l],
                                     vst[:, l].rearrange("p h t c -> p h (t c)")).then_inc(v_out, 16)
                for i in range(4):
                    sp.wait_ge(part_out[i], 16 * B * NUB // 4)
                sp.wait_ge(v_out, 32 * B)
                for dst in (qs, kh, kl):
                    sp.dma_start(dst[:, NH * HD:NHP * HD], dst[:, 0:4 * HD]).then_inc(pad_out, 16)
                sp.dma_start(vs[NH:NHP], vs[0:4]).then_inc(pad_out, 16)
                sp.wait_ge(pad_out, 64)

            @block.tensor
            def _(pe):
                pe.wait_ge(w_in, 48)
                with pe.Fori(0, B) as b:
                    for c in range(CPB):
                        x = xc[c % 2]
                        pe.wait_ge(x_in[c % 2], b * 32 + 16 * (c // 2) + 16)
                        pe.wait_ge(p1_rdy, b * NUB + c * NU)
                        for a, (w, e) in enumerate(((0, 0), (0, 1), (1, 0), (1, 1))):
                            for k in range(EK2):
                                mm = nc.tensor.matmul(acc[a][:], wts[:, w, k, e * P:(e + 1) * P], x[:, k, :],
                                                      start=(k == 0), stop=(k == 1))
                            mm.then_inc(qk_mm, 1)
                        pe.wait_ge(vf_rdy, b * 2 * CPB + 2 * c)
                        for i in range(4):
                            for k in range(EK2):
                                mm = nc.tensor.matmul(vacc[:, i * E:(i + 1) * E], x[:, k, i * P:(i + 1) * P],
                                                      wts[:, 2, k, :], start=(k == 0), stop=(k == 1))
                        mm.then_inc(v_mm, 1)

            @block.scalar
            def _(act):
                act.wait_ge(prep, 6)
                with act.Fori(0, B) as b:
                    for c in range(CPB):
                        for s, (a, key, _, _) in enumerate(units):
                            n = c * NU + s
                            act.wait_ge(qk_mm, b * 4 * CPB + 4 * c + a + 1)
                            act.wait_ge(r_rdy, b * NUB + max(n - 1, 0))
                            nc.scalar.activation(full[n % 2][:], acc[a][:], ACT.Identity,
                                                 bias=bias_of(key)).then_inc(f_rdy, 1)
                            act.wait_ge(part_out[n % 4], b * (16 * NUB // 4) + 16 * (n // 4))
                            nc.scalar.activation(part[n % 4][:, 0, :], acc[a][:], ACT.Identity,
                                                 bias=bias_of(key)).then_inc(p1_rdy, 1)
                            act.wait_ge(r_rdy, b * NUB + n + 1)
                            nc.scalar.activation(part[n % 4][:, 1, :], rest[n % 2][:], ACT.Copy).then_inc(p2_rdy, 1)
                        for l in range(2):
                            m = 2 * c + l
                            act.wait_ge(vf_rdy, b * 2 * CPB + m + 1)
                            if c == 0:
                                act.wait_ge(v_out, b * 32)
                            nc.scalar.activation(v_part(l, c, 0), v_view(vfull[l]), ACT.Copy).then_inc(v1_rdy, 1)
                            act.wait_ge(vr_rdy, b * 2 * CPB + m + 1)
                            nc.scalar.activation(v_part(l, c, 1), v_view(vrest[l]), ACT.Copy).then_inc(v2_rdy, 1)

            @block.vector
            def _(dve):
                nc.vector.memset(vst[:, :, :, :, 3 * HD:VC], 1.0).then_inc(prep, 1)
                dve.wait_ge(w_in, 48)
                for e in range(EK2):
                    for l in range(2):
                        nc.vector.tensor_tensor(kbias[:, e, l:l + 1], cols[:, e, 1:2], cols[:, e, 2 + l:3 + l],
                                                ALU.add).then_inc(prep, 1)
                for l in range(2):
                    op = nc.vector.tensor_tensor(vrow[:, l, :], rows[:, 0, :], rows[:, 1 + l, :], ALU.add)
                    if l == 1:
                        op.then_inc(prep, 1)
                dve.wait_ge(prep, 6)
                with dve.Fori(0, B) as b:
                    for c in range(CPB):
                        for s in range(NU):
                            n = c * NU + s
                            dve.wait_ge(f_rdy, b * NUB + n + 1)
                            dve.wait_ge(p1_rdy, b * NUB + n + 1)
                            dve.wait_ge(p3_rdy, b * NUB + max(n - 1, 0))
                            nc.vector.tensor_tensor(rest[n % 2][:], full[n % 2][:], part[n % 4][:, 0, :],
                                                    ALU.subtract).then_inc(r_rdy, 1)
                            dve.wait_ge(p2_rdy, b * NUB + n + 1)
                            dve.wait_ge(r_rdy, b * NUB + n + 1)
                            nc.vector.tensor_tensor(part[n % 4][:, 2, :], rest[n % 2][:], part[n % 4][:, 1, :],
                                                    ALU.subtract).then_inc(p3_rdy, 1)
                        dve.wait_ge(v_mm, b * CPB + c + 1)
                        for l in range(2):
                            dve.wait_ge(v3_rdy, b * 2 * CPB + max(2 * c + l - 1, 0))
                            nc.vector.tensor_tensor(
                                vfull[l][:].rearrange("p (t n) -> p t n", t=4),
                                vacc[:].rearrange("p (t n) -> p t n", t=4),
                                vrow[:, l:l + 1, :].to_broadcast([P, 4, E]), ALU.add).then_inc(vf_rdy, 1)
                        for l in range(2):
                            m = 2 * c + l
                            dve.wait_ge(v1_rdy, b * 2 * CPB + m + 1)
                            nc.vector.tensor_tensor(v_view(vrest[l]), v_view(vfull[l]), v_part(l, c, 0),
                                                    ALU.subtract).then_inc(vr_rdy, 1)
                            dve.wait_ge(v2_rdy, b * 2 * CPB + m + 1)
                            dve.wait_ge(vr_rdy, b * 2 * CPB + m + 1)
                            nc.vector.tensor_tensor(v_part(l, c, 2), v_view(vrest[l]), v_part(l, c, 1),
                                                    ALU.subtract).then_inc(v3_rdy, 1)


NPT = 6
KS = NPT * HD
Q_PARTS, K_PARTS = (0, 0, 0, 1, 1, 2), (0, 1, 2, 0, 1, 0)
TAB = P + W - 1
HEADS = 4
STEPS = 2 * KT
WI = 32
GUARD_LAG = 7
GUARD = KS


def window(half, kt):
    q0, q1 = max(P * kt - PAD, HALF * half), min(P * kt - PAD + W, HALF * (half + 1))
    return (q0, q1, q0 - (P * kt - PAD)) if q1 > q0 else None


def segments(half, kt):
    out = []
    for q0 in range(HALF * half, HALF * (half + 1), CH):
        cut = min(max(P * kt, q0), q0 + CH)
        out += [(a, b, early) for a, b, early in ((q0, cut, 0), (cut, q0 + CH, 1)) if b > a]
    return out


BAND_ITEMS = [(w, min(w + WI, W)) for w in range(0, W, WI)]
CENTRE_ITEMS = [(w, w + WI) for w in range(PAD, PAD + P, WI)]
SIDE_ITEMS = [(0, PAD), (PAD + P, W)]


def attention_plan():
    steps, n = [], 0
    for u in range(HEADS):
        for s in range(STEPS):
            shared = [("max", s // KT, s % KT)]
            if u % 2 == 0 and s % 5 == 4:
                shared.append(("band", s // 5))
            f = u * STEPS + s
            last = u % 2 == 1 and s == STEPS - 1
            first = 2 * STEPS * (u // 2)
            values = [g for g in ([f - 2, f - 1, f] if last else [f - 2]) if g >= first]
            if last:
                shared_after = [("centre", i) for i in range(len(CENTRE_ITEMS))]
                shared_after += [("side", i) for i in range(len(SIDE_ITEMS))]
            else:
                shared_after = []
            steps.append((u, s // KT, s % KT, shared, values, shared_after))
    return steps


def attention(nc, t, scratch, outs):
    qs, kh, kl, vs = scratch
    os_, os2, den = outs
    late_early = (kh, kl)
    with ExitStack() as ctx:
        sb = lambda n, s, d: ctx.enter_context(nc.sbuf_tensor("att_" + n, s, d))
        sem = semaphores(nc, ctx, "att")
        ktab = [sb(f"ktab{l}", [KS, TAB], BF16) for l in range(2)]
        vtab = sb("vtab", [P, W, 3 * HD], BF16)
        with ExitStack() as tctx:
            tb = lambda n, s, d: tctx.enter_context(nc.sbuf_tensor("tab_" + n, s, d))
            tsem = semaphores(nc, tctx, "tab")
            rk, rkb, msk = tb("rk", [KS, TAB], F32), tb("rkb", [KS, 2], F32), tb("msk", [KS, 3], F32)
            kf, kr = tb("kf", [KS, TAB], F32), tb("kr", [KS, TAB], F32)
            kp = [tb(f"kp{i}", [KS, TAB], BF16) for i in range(3)]
            rv, rvb = tb("rv", [P, W, HD], F32), tb("rvb", [P, 2, HD], F32)
            vf, vr = tb("vf", [P, W, HD], F32), tb("vr", [P, W, HD], F32)
            tin, step = tsem("in"), tsem("step")
            with nc.Block() as block:
                @block.sync
                def _(sp):
                    for dst, name in ((rk, "rk"), (rkb, "rkb"), (msk, "msk"), (rv, "rv"), (rvb, "rvb")):
                        sp.dma_start(dst[:], t[name]).then_inc(tin, 16)

                @block.vector
                def _(dve):
                    dve.wait_ge(tin, 80)
                    n = 0
                    for l in range(2):
                        dve.wait_ge(step, n)
                        nc.vector.tensor_scalar(kf[:], rk[:], rkb[:, l:l + 1], None, ALU.subtract).then_inc(step, 1)
                        dve.wait_ge(step, n + 1)
                        nc.vector.tensor_copy(kp[0][:], kf[:]).then_inc(step, 1)
                        dve.wait_ge(step, n + 2)
                        nc.vector.tensor_tensor(kr[:], kf[:], kp[0][:], ALU.subtract).then_inc(step, 1)
                        dve.wait_ge(step, n + 3)
                        nc.vector.tensor_copy(kp[1][:], kr[:]).then_inc(step, 1)
                        dve.wait_ge(step, n + 4)
                        nc.vector.tensor_tensor(kp[2][:], kr[:], kp[1][:], ALU.subtract).then_inc(step, 1)
                        dve.wait_ge(step, n + 5)
                        nc.vector.tensor_scalar(kf[:], kp[0][:], msk[:, 0:1], None, ALU.mult).then_inc(step, 1)
                        dve.wait_ge(step, n + 6)
                        nc.vector.scalar_tensor_tensor(out=kr[:], in0=kp[1][:], scalar=msk[:, 1:2], in1=kf[:],
                                                       op0=ALU.mult, op1=ALU.add).then_inc(step, 1)
                        dve.wait_ge(step, n + 7)
                        nc.vector.scalar_tensor_tensor(out=ktab[l][:], in0=kp[2][:], scalar=msk[:, 2:3], in1=kr[:],
                                                       op0=ALU.mult, op1=ALU.add).then_inc(step, 1)
                        n += 8
                    for l, (a, b) in enumerate(((0, PAD), (PAD, W))):
                        nc.vector.tensor_tensor(vf[:, a:b, :], rv[:, a:b, :],
                                                rvb[:, l:l + 1, :].to_broadcast([P, b - a, HD]),
                                                ALU.subtract).then_inc(step, 1)
                    n += 2
                    dve.wait_ge(step, n)
                    nc.vector.tensor_copy(vtab[:, :, 0:HD], vf[:]).then_inc(step, 1)
                    dve.wait_ge(step, n + 1)
                    nc.vector.tensor_tensor(vr[:], vf[:], vtab[:, :, 0:HD], ALU.subtract).then_inc(step, 1)
                    dve.wait_ge(step, n + 2)
                    nc.vector.tensor_copy(vtab[:, :, HD:2 * HD], vr[:]).then_inc(step, 1)
                    dve.wait_ge(step, n + 3)
                    nc.vector.tensor_tensor(vtab[:, :, 2 * HD:3 * HD], vr[:], vtab[:, :, HD:2 * HD],
                                            ALU.subtract).then_inc(step, 1)
                    dve.wait_ge(step, n + 4)

        q = [sb(f"q{u}", [P, S], BF16) for u in range(HEADS)]
        k = [[sb(f"k{l}{u}", [P, S], BF16) for u in range(HEADS)] for l in range(2)]
        v = [sb(f"v{i}", [P, 2, KT * VC], BF16) for i in range(2)]
        qband = sb("qband", [KS, 2, S + 2 * PAD], BF16)
        band = [sb(f"band{i}", [P, W * 2 * KT], F32) for i in range(2)]
        pwin = [sb(f"pwin{i}", [P, 2, KT, W], BF16) for i in range(2)]
        prob = [sb(f"prob{i}", [P, HALF], F32) for i in range(4)]
        low = [sb(f"low{i}", [P, HALF], BF16) for i in range(4)]
        kmax = [sb(f"kmax{i}", [P, HALF], F32) for i in range(2)]
        allmax = sb("allmax", [P, HALF], F32)
        ghi = sb("ghi", [1, HALF], BF16)
        glo = sb("glo", [1, HALF], BF16)
        oev = [sb(f"oev{i}", [VC - 1, HALF], F32) for i in range(2)]
        rel = sb("rel", [3 * HD, 2, S], F32)
        score = [ctx.enter_context(nc.psum_tensor(f"score{i}", [P, HALF], F32)) for i in range(2)]
        shared = ctx.enter_context(nc.psum_tensor("shared", [P, HALF], F32))
        oacc = ctx.enter_context(nc.psum_tensor("oacc", [P, HALF], F32))

        zeroed = sem("zeroed")
        ones_set = sem("ones_set")
        stack_in = [sem(f"stack_in{u}") for u in range(HEADS)]
        v_in = [sem(f"v_in{i}") for i in range(2)]
        qband_in = sem("qband_in")
        score_rdy, band_added, exp_done = sem("score_rdy"), sem("band_added"), sem("exp_done")
        low_dve, low_pool, win_hi, win_lo = sem("low_dve"), sem("low_pool"), sem("win_hi"), sem("win_lo")
        pv_done, o_read = sem("pv_done"), sem("o_read")
        sh_rdy, sh_dve, sh_act = sem("sh_rdy"), sem("sh_dve"), sem("sh_act")
        add_max = sem("add_max")
        all_max, ghi_rdy, glo_rdy = sem("all_max"), sem("ghi_rdy"), sem("glo_rdy")
        guard_in = [sem(f"guard_in{i}") for i in range(2)]
        o_out = [sem(f"o_out{i}") for i in range(2)]
        rel_out = sem("rel_out")

        plan = attention_plan()
        NS = len(plan)
        NW = sum(window(s // KT, s % KT) is not None for s in range(STEPS))

        NLP = sum(s % 5 in (1, 3) for s in range(NS))

        def pool_low(s):
            return s % 5 in (1, 3)

        def uses(items):
            return np.array([len(items), sum(i[0] in ("max", "side") for i in items),
                             sum(i[0] in ("band", "centre") for i in items)])
        ahead = [("band", i) for i in range(len(BAND_ITEMS))] + [("max", s // KT, s % KT) for s in range(STEPS)]
        before = [int(x) for x in uses(ahead)]
        each = [int(x) for x in uses([i for st in plan for i in st[3] + st[5]])]

        def load_stack(sp, u, head_row):
            for stack, src, parts in ((q[u], qs, Q_PARTS), (k[0][u], kh, K_PARTS), (k[1][u], kl, K_PARTS)):
                for r, p in enumerate(parts):
                    sp.dma_start(stack[r * HD:(r + 1) * HD, :], src[p, head_row, :]).then_inc(stack_in[u], 16)

        def load_qband(sp, rows):
            for hd in range(2):
                for r, p in enumerate(Q_PARTS):
                    sp.dma_start(qband[r * HD:(r + 1) * HD, hd, PAD:PAD + S], qs[p, rows[hd], :]).then_inc(qband_in, 16)
        STACK_INC, QBAND_INC = 18 * 16, 12 * 16

        with nc.Block() as block:
            @block.sync
            def _(sp):
                sp.wait_ge(zeroed, 2)
                load_qband(sp, [slice(0, HD), slice(HD, 2 * HD)])
                for u in range(HEADS):
                    load_stack(sp, u, slice(u * HD, (u + 1) * HD))
                    if u < 2:
                        sp.dma_start(v[u][:], vs[u].rearrange("l p c -> p l c")).then_inc(v_in[u], 16)

                def guard(half, seen, j, count):
                    sp.wait_ge(glo_rdy, seen)
                    nxt = count % HEADS
                    sp.dma_start(q[nxt][GUARD:GUARD + 1, half * HALF:(half + 1) * HALF], ghi[:]).then_inc(guard_in[half], 16)
                    sp.dma_start(q[nxt][GUARD + 1:GUARD + 2, half * HALF:(half + 1) * HALF], glo[:]).then_inc(guard_in[half], 16)
                sp.wait_ge(zeroed, HEADS + 4)
                guard(0, 1, None, 0)
                guard(1, 2, None, 0)
                sp.wait_ge(sh_rdy, len(BAND_ITEMS))
                load_qband(sp, [slice(2 * HD, 3 * HD), slice(3 * HD, 4 * HD)])
                with sp.Fori(0, NH // HEADS) as j:
                    for f, (u, half, kt, items, values, after) in enumerate(plan):
                        if kt == KT - 1:
                            guard(half, j * 2 * HEADS + 2 + 2 * u + half + 1, j, u + 1)
                        for g in values:
                            gu, ghalf, gkt = plan[g][:3]
                            if gkt == KT - 1:
                                n_half = 2 * gu + ghalf + 1
                                sp.wait_ge(o_read, j * 2 * HEADS + n_half)
                                for p in range(3):
                                    sp.dma_start(os_[p, bass.ds(j * HEADS * HD + gu * HD, HD), ghalf * HALF:(ghalf + 1) * HALF],
                                                 oev[ghalf][p * HD:(p + 1) * HD, :]).then_inc(o_out[ghalf], 16)
                                sp.dma_start(den[bass.ds(j * HEADS + gu, 1), ghalf * HALF:(ghalf + 1) * HALF],
                                             oev[ghalf][3 * HD:3 * HD + 1, :]).then_inc(o_out[ghalf], 16)
                                if ghalf == 1:
                                    sp.wait_ge(pv_done, j * NS + g + 1)
                                    load_stack(sp, gu, bass.ds(j * HEADS * HD + (gu + HEADS) * HD, HD))
                                    sp.dma_start(v[gu % 2][:], vs.rearrange("h l p c -> p h l c")[
                                        :, bass.ds(j * HEADS + gu + 2, 1)]).then_inc(v_in[gu % 2], 16)
                        if u % 2 == 0 and half == 1 and kt == KT - 1:
                            done = sum(len(st[3]) + len(st[5]) for st in plan[:f + 1])
                            sp.wait_ge(sh_rdy, j * each[0] + before[0] + done)
                            rows = j * HEADS * HD + (u + 4) * HD
                            load_qband(sp, [bass.ds(rows, HD), bass.ds(rows + HD, HD)])
                        if after:
                            done = sum(i[0] in ("max", "side") for st in plan[:f + 1] for i in st[3] + st[5])
                            sp.wait_ge(sh_dve, j * each[1] + before[1] + done)
                            for hd in range(2):
                                for p in range(3):
                                    sp.dma_start(os2[p, bass.ds(j * HEADS * HD + (u - 1 + hd) * HD, HD), :],
                                                 rel[p * HD:(p + 1) * HD, hd, :]).then_inc(rel_out, 16)
                for i in range(2):
                    sp.wait_ge(o_out[i], 64 * NH)
                    sp.wait_ge(v_in[i], 16 * (1 + NH // 2))
                    sp.wait_ge(guard_in[i], 32 * (NH + 1))
                for u in range(HEADS):
                    sp.wait_ge(stack_in[u], STACK_INC * (1 + NH // HEADS))
                sp.wait_ge(qband_in, QBAND_INC * (2 + NH // 2))
                sp.wait_ge(rel_out, 96 * NH // 2)

            def scores_of(out, u, half, kt, rows):
                for a, b, early in segments(half, kt):
                    mm = nc.tensor.matmul(out[:, a - half * HALF:b - half * HALF],
                                          k[early][u][0:rows, kt * P:(kt + 1) * P], q[u][0:rows, a:b],
                                          start=True, stop=True)
                return mm

            def band_products(item):
                w0, w1 = BAND_ITEMS[item]
                for w in range(w0, w1):
                    mm = nc.tensor.matmul(
                        shared[:, (w - w0) * 2 * KT:(w - w0 + 1) * 2 * KT].rearrange("p (h t) -> p h t", h=2),
                        ktab[0 if w < PAD else 1][:, W - 1 - w:W - 1 - w + P],
                        qband[:, :, w:w + (KT - 1) * P + 1:P], start=True, stop=True)
                return mm

            def value_band_products(w0, w1):
                for w in range(w0, w1):
                    for i in range(2):
                        mm = nc.tensor.matmul(
                            shared[0:3 * HD, (w - w0) * 2 * KT:(w - w0 + 1) * 2 * KT].rearrange("p (h t) -> p h t", h=2),
                            vtab[:, w, :], pwin[i][:, :, :, w], start=(i == 0), stop=(i == 1))
                return mm

            @block.tensor
            def _(pe):
                pe.wait_ge(zeroed, HEADS + 4)
                pe.wait_ge(ones_set, 4 * HEADS)
                pe.wait_ge(qband_in, QBAND_INC)
                n, nd, na = 0, 0, 0
                for item in ahead:
                    if item[0] == "band":
                        if n:
                            pe.wait_ge(sh_act, na)
                        band_products(item[1]).then_inc(sh_rdy, 1)
                        na += 1
                    else:
                        if nd == 0:
                            pe.wait_ge(sh_act, na)
                            pe.wait_ge(stack_in[0], STACK_INC)
                        else:
                            pe.wait_ge(sh_dve, nd)
                        scores_of(shared, 0, item[1], item[2], KS).then_inc(sh_rdy, 1)
                        nd += 1
                    n += 1
                with pe.Fori(0, NH // HEADS) as j:
                    def scores(f):
                        u, half, kt = plan[f][:3]
                        if kt == 0:
                            pe.wait_ge(guard_in[half], j * 32 * HEADS + 32 * (u + 1))
                        pe.wait_ge(exp_done, j * NS + max(f - 1, 0))
                        scores_of(score[f % 2], u, half, kt, P).then_inc(score_rdy, 1)

                    last = ("dve", 0)
                    cnt = {"dve": 0, "act": 0}
                    nw = 0
                    scores(0)
                    for f, (u, half, kt, items, values, after) in enumerate(plan):
                        if f + 1 < NS:
                            scores(f + 1)
                        nw += window(half, kt) is not None

                        def use(item):
                            nonlocal last
                            if last[0] == "dve":
                                pe.wait_ge(sh_dve, j * each[1] + before[1] + last[1])
                            else:
                                pe.wait_ge(sh_act, j * each[2] + before[2] + last[1])
                            if item[0] == "max":
                                nxt = (u + 1) % HEADS
                                if item[1:] == (0, 0):
                                    pe.wait_ge(stack_in[nxt], j * STACK_INC + (STACK_INC * 2 if nxt == 0 else STACK_INC))
                                mm = scores_of(shared, nxt, item[1], item[2], KS)
                            elif item[0] == "band":
                                if item[1] == 0:
                                    pe.wait_ge(qband_in, j * 2 * QBAND_INC + QBAND_INC * (2 + u // 2))
                                mm = band_products(item[1])
                            else:
                                if item == ("centre", 0):
                                    pe.wait_ge(win_hi, j * HEADS * NW + nw)
                                    pe.wait_ge(win_lo, j * HEADS * NW + nw)
                                mm = value_band_products(*(CENTRE_ITEMS if item[0] == "centre" else SIDE_ITEMS)[item[1]])
                            mm.then_inc(sh_rdy, 1)
                            who = "dve" if item[0] in ("max", "side") else "act"
                            cnt[who] += 1
                            last = (who, cnt[who])

                        for item in items:
                            use(item)
                        for g in values:
                            gu, ghalf, gkt = plan[g][:3]
                            if gkt == 0:
                                pe.wait_ge(o_read, j * 2 * HEADS + 2 * gu + ghalf)
                                pe.wait_ge(v_in[gu % 2], j * 32 + 16 * (gu // 2) + 16)
                            if pool_low(g):
                                pe.wait_ge(low_pool, j * NLP + sum(map(pool_low, range(g + 1))))
                            else:
                                pe.wait_ge(low_dve, j * (NS - NLP) + g + 1 - sum(map(pool_low, range(g + 1))))
                            segs = segments(ghalf, gkt)
                            for n, (a, b, early) in enumerate(segs):
                                a, b = a - ghalf * HALF, b - ghalf * HALF
                                vv = v[gu % 2][:, early, gkt * VC:gkt * VC + VC - 1]
                                first = gkt == 0
                                nc.tensor.matmul(oacc[0:VC - 1, a:b], vv, prob[g % 4][:].bitcast(BF16)[:, 2 * a + 1:2 * b:2],
                                                 start=first, stop=False, skip_group_check=True)
                                mm = nc.tensor.matmul(oacc[0:VC - 1, a:b], vv, low[g % 4][:, a:b],
                                                      start=False, stop=(gkt == KT - 1), skip_group_check=True)
                            mm.then_inc(pv_done, 1)
                        for item in after:
                            use(item)

            @block.scalar
            def _(act):
                for i in range(len(BAND_ITEMS)):
                    w0, w1 = BAND_ITEMS[i]
                    act.wait_ge(sh_rdy, i + 1)
                    nc.scalar.activation(band[0][:, w0 * 2 * KT:w1 * 2 * KT], shared[:, 0:(w1 - w0) * 2 * KT],
                                         ACT.Copy).then_inc(sh_act, 1)

                def guard_high(n, j=None):
                    act.wait_ge(all_max, n + 1 if j is None else j * 2 * HEADS + n + 1)
                    if j is not None:
                        act.wait_ge(guard_in[(n - 1) % 2], j * 32 * HEADS + 32 * ((n - 1) // 2 + 1))
                    elif n:
                        act.wait_ge(guard_in[0], 32)
                    nc.scalar.activation(ghi[:], allmax[0:1, :], ACT.Copy, scale=-1.0).then_inc(ghi_rdy, 1)
                guard_high(0)
                guard_high(1)
                with act.Fori(0, NH // HEADS) as j:
                    nw, nwin, nz, nc_, no = 0, 0, 0, 0, 0
                    pending_window = None

                    def copy_window(f):
                        nonlocal nw
                        u, half, kt = plan[f][:3]
                        q0, q1, w0 = window(half, kt)
                        if nw % (2 * NW) == 0:
                            zs = sum(len(st[3]) + len(st[5]) for st in plan[:2 * STEPS * (u // 2)])
                            act.wait_ge(sh_rdy, j * each[0] + before[0] + zs)
                        act.wait_ge(exp_done, j * NS + f + 1)
                        nc.scalar.activation(pwin[0][:, u % 2, kt, w0:w0 + q1 - q0],
                                             prob[f % 4][:].bitcast(BF16)[:, 2 * (q0 - half * HALF) + 1:2 * (q1 - half * HALF):2],
                                             ACT.Copy).then_inc(win_hi, 1)
                        nw += 1

                    def copy_band(item, z, u):
                        nonlocal nc_
                        w0, w1 = BAND_ITEMS[item]
                        act.wait_ge(sh_rdy, j * each[0] + before[0] + z + 1)
                        nc.scalar.activation(band[(u // 2 + 1) % 2][:, w0 * 2 * KT:w1 * 2 * KT],
                                             shared[:, 0:(w1 - w0) * 2 * KT], ACT.Copy).then_inc(sh_act, 1)

                    late, guards = [], []
                    for f, (u, half, kt, items, values, after) in enumerate(plan):
                        if window(half, kt) is not None:
                            nwin += 1
                            act.wait_ge(band_added, j * HEADS * NW + nwin)
                        else:
                            act.wait_ge(score_rdy, j * NS + f + 1)
                        act.wait_ge(pv_done, j * NS + max(f - 3, 0))
                        nc.scalar.activation(prob[f % 4][:], score[f % 2][:], ACT.Exp, scale=0.25).then_inc(exp_done, 1)
                        for item, z in late:
                            copy_band(item, z, u)
                        late = []
                        if pending_window is not None:
                            copy_window(pending_window)
                            pending_window = None
                        if window(half, kt) is not None:
                            pending_window = f
                        for item in items:
                            if item[0] == "band":
                                late.append((item[1], nz))
                            nz += 1
                        if kt == KT - 1:
                            guards.append((f + GUARD_LAG, 2 + 2 * u + half))
                        while guards and guards[0][0] <= f:
                            guard_high(guards.pop(0)[1], j)
                        if after and pending_window is not None:
                            copy_window(pending_window)
                            pending_window = None
                        for g in values:
                            gu, ghalf, gkt = plan[g][:3]
                            if gkt == KT - 1:
                                act.wait_ge(pv_done, j * NS + g + 1)
                                act.wait_ge(o_out[ghalf], j * 64 * HEADS + 64 * gu)
                                nc.scalar.activation(oev[ghalf][:], oacc[0:VC - 1, :], ACT.Copy).then_inc(o_read, 1)
                        for item in after:
                            if item[0] == "centre":
                                if item[1] == 0:
                                    act.wait_ge(rel_out, j * 192 + 96 * (u // 2))
                                i = item[1]
                                act.wait_ge(sh_rdy, j * each[0] + before[0] + nz + 1)
                                nc.scalar.activation(
                                    rel[:].rearrange("p h (t q) -> p h t q", t=KT)[:, :, :, i * WI:(i + 1) * WI],
                                    shared[0:3 * HD, :].rearrange("p (w h t) -> p h t w", h=2, t=KT),
                                    ACT.Copy).then_inc(sh_act, 1)
                            nz += 1
                    for _, n in guards:
                        guard_high(n, j)

            @block.gpsimd
            def _(pool):
                nc.gpsimd.memset(qband[:, :, 0:PAD], 0.0).then_inc(zeroed, 1)
                nc.gpsimd.memset(qband[:, :, PAD + S:S + 2 * PAD], 0.0).then_inc(zeroed, 1)
                for u in range(HEADS):
                    nc.gpsimd.memset(q[u][KS:P, :], 0.0).then_inc(zeroed, 1)
                for i in range(2):
                    pool.wait_ge(zeroed, HEADS + 2 + i)
                    nc.gpsimd.memset(pwin[i][:], 0.0).then_inc(zeroed, 1)
                pool.wait_ge(zeroed, HEADS + 4)

                def all_reduce(n, maxes, j=None, f=None):
                    if j is None:
                        pool.wait_ge(sh_dve, maxes)
                        if n:
                            pool.wait_ge(glo_rdy, n)
                    else:
                        maxes_in = pool.to_reg(j * each[1] + before[1] + maxes)
                        last_read = pool.to_reg(j * 2 * HEADS + n)
                        lows = pool.to_reg(j * NLP + sum(map(pool_low, range(f + 1))))
                        pool.wait_ge(zeroed, HEADS + 4)
                        pool.wait_ge(sh_dve, maxes_in)
                        pool.wait_ge(glo_rdy, last_read)
                        pool.wait_ge(low_pool, lows)
                    nc.gpsimd.partition_all_reduce(allmax[:], kmax[n % 2][:], P, RMAX).then_inc(all_max, 1)
                all_reduce(0, KT)
                all_reduce(1, 2 * KT)
                with pool.Fori(0, NH // HEADS) as j:
                    nz = 0

                    def low_part(f):
                        pool.wait_ge(all_max, j * 2 * HEADS + 2 + (f - 1) // KT if f else j * 2 * HEADS + 2)
                        pool.wait_ge(exp_done, j * NS + f + 1)
                        pool.wait_ge(pv_done, j * NS + max(f - 3, 0))
                        nc.gpsimd.tensor_tensor(low[f % 4][:], prob[f % 4][:],
                                                prob[f % 4][:].bitcast(BF16)[:, 1::2],
                                                ALU.subtract).then_inc(low_pool, 1)
                    for f, (u, half, kt, items, values, after) in enumerate(plan):
                        if pool_low(f):
                            low_part(f)
                        nz += 1
                        if kt == KT - 1:
                            all_reduce(2 + 2 * u + half, nz, j, f)
                        nz += sum(i[0] == "side" for i in after)

            @block.vector
            def _(dve):
                def band_of(pair, hd, kt, w0, w1):
                    return band[pair][:].rearrange("p (w h t) -> p w h t", h=2, t=KT)[:, w0:w1, hd, kt]

                def max_item(half, kt, pair, hd, z, m, am, j=None):
                    at = (lambda base, n: n) if j is None else (lambda base, n: j * base[0] + base[1] + n)
                    dve.wait_ge(sh_rdy, at((each[0], before[0]), z + 1))
                    win = window(half, kt)
                    if win is not None:
                        q0, q1, w0 = win
                        o = shared[:, q0 - half * HALF:q1 - half * HALF]
                        nc.vector.tensor_tensor(o, o, band_of(pair, hd, kt, w0, w0 + q1 - q0), ALU.add).then_inc(add_max, 1)
                        dve.wait_ge(add_max, at((HEADS * NW, NW), am + 1))
                    if kt == 0:
                        if j is not None:
                            dve.wait_ge(all_max, m[1])
                        nc.vector.tensor_copy(kmax[half][:], shared[:]).then_inc(sh_dve, 1)
                    else:
                        dve.wait_ge(sh_dve, at((each[1], before[1]), m[0]))
                        nc.vector.tensor_tensor(kmax[half][:], kmax[half][:], shared[:], ALU.max).then_inc(sh_dve, 1)

                def guard_low(n, j=None):
                    dve.wait_ge(ghi_rdy, n + 1 if j is None else j * 2 * HEADS + n + 1)
                    if j is not None:
                        dve.wait_ge(guard_in[(n - 1) % 2], j * 32 * HEADS + 32 * ((n - 1) // 2 + 1))
                    elif n:
                        dve.wait_ge(guard_in[0], 32)
                    nc.vector.scalar_tensor_tensor(out=glo[:], in0=allmax[0:1, :], scalar=-1.0, in1=ghi[:],
                                                   op0=ALU.mult, op1=ALU.subtract).then_inc(glo_rdy, 1)

                operands = [k[l][u] for l in range(2) for u in range(HEADS)]
                for o in operands:
                    nc.vector.memset(o[KS:P, :], 0.0).then_inc(ones_set, 1)
                for n, o in enumerate(operands):
                    dve.wait_ge(ones_set, n + 1)
                    nc.vector.memset(o[GUARD:GUARD + 2, :], 1.0).then_inc(ones_set, 1)
                dve.wait_ge(sh_act, len(BAND_ITEMS))
                am = 0
                for s in range(STEPS):
                    max_item(s // KT, s % KT, 0, 0, len(BAND_ITEMS) + s, (s, 0), am)
                    am += window(s // KT, s % KT) is not None
                    if s == KT + 8:
                        guard_low(0)
                guard_low(1)
                dve.wait_ge(zeroed, HEADS + 4)
                with dve.Fori(0, NH // HEADS) as j:
                    nz, nd, na, am, ba, nlow, nwl = 0, 0, 0, 0, 0, 0, 0
                    guards = []

                    def add_band(f):
                        nonlocal ba
                        u, half, kt = plan[f][:3]
                        win = window(half, kt)
                        if win is None:
                            return
                        q0, q1, w0 = win
                        dve.wait_ge(score_rdy, j * NS + f + 1)
                        o = score[f % 2][:, q0 - half * HALF:q1 - half * HALF]
                        nc.vector.tensor_tensor(o, o, band_of(u // 2, u % 2, kt, w0, w0 + q1 - q0),
                                                ALU.add).then_inc(band_added, 1)

                    def low_part(f):
                        nonlocal nwl
                        u, half, kt = plan[f][:3]
                        dve.wait_ge(exp_done, j * NS + f + 1)
                        dve.wait_ge(pv_done, j * NS + max(f - 3, 0))
                        if not pool_low(f):
                            nc.vector.tensor_tensor(low[f % 4][:], prob[f % 4][:],
                                                    prob[f % 4][:].bitcast(BF16)[:, 1::2],
                                                    ALU.subtract).then_inc(low_dve, 1)
                        win = window(half, kt)
                        if win is not None:
                            if nwl % (2 * NW) == 0:
                                zs = sum(len(st[3]) + len(st[5]) for st in plan[:2 * STEPS * (u // 2)])
                                dve.wait_ge(sh_rdy, j * each[0] + before[0] + zs)
                            a, b, w0 = win[0] - half * HALF, win[1] - half * HALF, win[2]
                            nc.vector.tensor_tensor(pwin[1][:, u % 2, kt, w0:w0 + b - a], prob[f % 4][:, a:b],
                                                    prob[f % 4][:].bitcast(BF16)[:, 2 * a + 1:2 * b:2],
                                                    ALU.subtract).then_inc(win_lo, 1)
                            nwl += 1

                    add_band(0)
                    for f, (u, half, kt, items, values, after) in enumerate(plan):
                        if f + 1 < NS:
                            add_band(f + 1)
                        if f and not plan[f - 1][5]:
                            low_part(f - 1)
                        for item in items:
                            if item[0] == "max":
                                nxt = u + 1
                                if item[1:] == (0, 0) and nxt == HEADS:
                                    pass
                                if item[1:] == (0, 0) and nxt % 2 == 0:
                                    dve.wait_ge(sh_act, j * each[2] + before[2] + na)
                                max_item(item[1], item[2], (nxt // 2) % 2, nxt % 2, nz,
                                         (nd, j * 2 * HEADS + 2 * u + item[1] + 1), am, j)
                                am += window(item[1], item[2]) is not None
                                nd += 1
                            else:
                                na += 1
                            nz += 1
                        if kt == KT - 1:
                            guards.append((f + GUARD_LAG, 2 + 2 * u + half))
                        if after:
                            low_part(f)
                        while guards and guards[0][0] <= f:
                            guard_low(guards.pop(0)[1], j)
                        for item in after:
                            if item[0] == "centre":
                                na += 1
                            else:
                                i = item[1]
                                dve.wait_ge(sh_rdy, j * each[0] + before[0] + nz + 1)
                                dve.wait_ge(sh_act, j * each[2] + before[2] + na)
                                view = rel[:].rearrange("p h (t q) -> p h t q", t=KT)
                                new = shared[0:3 * HD, 0:PAD * 2 * KT].rearrange("p (w h t) -> p h t w", h=2, t=KT)
                                if i == 0:
                                    old, new = view[:, :, 0:KT - 1, P - PAD:P], new[:, :, 1:KT, :]
                                else:
                                    old, new = view[:, :, 1:KT, 0:PAD], new[:, :, 0:KT - 1, :]
                                for hd in range(2):
                                    op = nc.vector.tensor_tensor(old[:, hd], old[:, hd], new[:, hd], ALU.add)
                                op.then_inc(sh_dve, 1)
                                nd += 1
                            nz += 1
                    for _, n in guards:
                        guard_low(n, j)


class Names:

    def __init__(self, nc, ctx, stage):
        self.nc, self.ctx, self.stage = nc, ctx, stage
        self.sem = semaphores(nc, ctx, stage)

    def sb(self, name, shape, dtype=F32):
        return self.ctx.enter_context(self.nc.sbuf_tensor(f"{self.stage}_{name}", shape, dtype))

    def ps(self, name, shape):
        return self.ctx.enter_context(self.nc.psum_tensor(f"{self.stage}_{name}", shape, F32))


def project_attention(nc, t, outs, x):
    os_, os2, den = outs
    with ExitStack() as ctx:
        m = Names(nc, ctx, "wo")
        w = m.sb("w", [P, EK2, E])
        bo = m.sb("bo", [P, EK2])
        xin = [m.sb(f"xin{i}", [P, EK2, CH]) for i in range(2)]
        parts = [m.sb(f"parts{i}", [P, EK2, 6, CH]) for i in range(2)]
        dn = [m.sb(f"den{i}", [P, EK2, CH]) for i in range(2)]
        total, recip, att = (m.sb(n, [P, EK2, CH]) for n in ("total", "recip", "att"))
        out = m.ps("out", [P, EK2, CH])
        w_in, in0, in1 = m.sem("w_in"), m.sem("in0"), m.sem("in1")
        chunk_in = [in0, in1]
        summed, recip_rdy, att_rdy, out_rdy, x_rdy = (m.sem(n) for n in ("summed", "recip", "att", "out", "x"))
        ND = 2 * (2 + 8) + 1
        with nc.Block() as block:
            @block.sync
            def _(sp):
                sp.dma_start(w[:], t["wo"].rearrange("(k p) n -> p k n", p=P)).then_inc(w_in, 16)
                sp.dma_start(bo[:], t["bo"]).then_inc(w_in, 16)
                with sp.Fori(0, B) as b:
                    for c in range(CPB):
                        sp.wait_ge(x_rdy, b * CPB + max(c - 1, 0))
                        cols = slice(c * CH, (c + 1) * CH)
                        s = chunk_in[c % 2]
                        sp.dma_start(xin[c % 2][:], t["xt"].rearrange("(k p) n -> p k n", p=P)[
                            :, :, bass.ds(b * S + c * CH, CH)]).then_inc(s, 16)
                        for e in range(EK2):
                            rows = bass.ds(b * E + e * P, P)
                            for i, src in enumerate((os_, os2)):
                                sp.dma_start(parts[c % 2][:, e, 3 * i:3 * i + 3, :],
                                             src.rearrange("a r n -> r a n")[rows, :, cols]).then_inc(s, 16)
                            for h in range(8):
                                sp.dma_start(dn[c % 2][h * HD:(h + 1) * HD, e, :],
                                             den[bass.ds(b * H + e * 8 + h, 1), cols].to_broadcast([HD, CH])).then_inc(s, 16)

            @block.vector
            def _(dve):
                dve.wait_ge(w_in, 32)
                with dve.Fori(0, B) as b:
                    for c in range(CPB):
                        n = b * CPB + c
                        dve.wait_ge(chunk_in[c % 2], b * (CPB // 2) * 16 * ND + 16 * ND * (c // 2 + 1))
                        nc.vector.tensor_reduce(total[:], parts[c % 2][:].rearrange("p e a n -> p e n a"), AX.X,
                                                ALU.add).then_inc(summed, 1)
                        nc.vector.reciprocal(recip[:], dn[c % 2][:]).then_inc(recip_rdy, 1)
                        dve.wait_ge(summed, n + 1)
                        dve.wait_ge(recip_rdy, n + 1)
                        dve.wait_ge(out_rdy, n)
                        nc.vector.tensor_tensor(att[:], total[:], recip[:], ALU.mult).then_inc(att_rdy, 1)
                        dve.wait_ge(out_rdy, n + 1)
                        for e in range(EK2):
                            op = nc.vector.scalar_tensor_tensor(
                                out=x[:, e, bass.ds(b * S + c * CH, CH)], in0=out[:, e, :], scalar=bo[:, e:e + 1],
                                in1=xin[c % 2][:, e, :], op0=ALU.add, op1=ALU.add)
                        op.then_inc(x_rdy, 1)

            @block.tensor
            def _(pe):
                pe.wait_ge(w_in, 32)
                with pe.Fori(0, NCH) as n:
                    pe.wait_ge(att_rdy, n + 1)
                    pe.wait_ge(x_rdy, n)
                    for e in range(EK2):
                        for k in range(EK2):
                            mm = nc.tensor.matmul(out[:, e, :], w[:, k, e * P:(e + 1) * P], att[:, k, :],
                                                  start=(k == 0), stop=(k == 1))
                    mm.then_inc(out_rdy, 1)


def layer_norm(nc, stage, x, out=None):
    with ExitStack() as ctx:
        m = Names(nc, ctx, stage)
        mean_of = m.sb("mean_of", [P, P])
        eps = m.sb("eps", [P, 1])
        dev = [m.sb(f"dev{i}", [P, EK2, CH]) for i in range(2)]
        sq = [m.sb(f"sq{i}", [P, EK2, CH]) for i in range(2)]
        sd = [m.sb(f"sd{i}", [P, CH]) for i in range(2)]
        rs = [m.sb(f"rs{i}", [P, CH]) for i in range(2)]
        mean = [m.ps(f"mean{i}", [P, CH]) for i in range(2)]
        var = [m.ps(f"var{i}", [P, CH]) for i in range(2)]
        ready, mean_rdy, dev_rdy, sq_rdy, var_rdy, sd_rdy, rs_rdy, x_rdy, x_out = (
            m.sem(n) for n in ("ready", "mean", "dev", "sq", "var", "sd", "rs", "x", "out"))
        with nc.Block() as block:
            def chunk(i, c):
                return x[:, :, bass.ds(i * 2 * CH + c * CH, CH)]

            @block.tensor
            def _(pe):
                pe.wait_ge(ready, 2)
                with pe.Fori(0, NCH // 2) as i:
                    for c in range(2):
                        pe.wait_ge(dev_rdy, i * 2)
                        for k in range(EK2):
                            mm = nc.tensor.matmul(mean[c][:], mean_of[:], x[:, k, bass.ds(i * 2 * CH + c * CH, CH)],
                                                  start=(k == 0), stop=(k == 1))
                        mm.then_inc(mean_rdy, 1)
                    for c in range(2):
                        pe.wait_ge(sq_rdy, i * 2 + c + 1)
                        pe.wait_ge(sd_rdy, i * 2)
                        for k in range(EK2):
                            mm = nc.tensor.matmul(var[c][:], mean_of[:], sq[c][:, k, :], start=(k == 0), stop=(k == 1))
                        mm.then_inc(var_rdy, 1)

            @block.vector
            def _(dve):
                nc.vector.memset(mean_of[:], 1.0 / E).then_inc(ready, 1)
                nc.vector.memset(eps[:], EPS).then_inc(ready, 1)
                with dve.Fori(0, NCH // 2) as i:
                    for c in range(2):
                        dve.wait_ge(mean_rdy, i * 2 + c + 1)
                        dve.wait_ge(x_rdy, i * 2)
                        dve.wait_ge(sq_rdy, i * 2)
                        nc.vector.tensor_tensor(dev[c][:], chunk(i, c), mean[c][:].unsqueeze(1).to_broadcast([P, EK2, CH]),
                                                ALU.subtract).then_inc(dev_rdy, 1)
                    for c in range(2):
                        dve.wait_ge(sd_rdy, i * 2 + c + 1)
                        nc.vector.reciprocal(rs[c][:], sd[c][:]).then_inc(rs_rdy, 1)
                        dve.wait_ge(rs_rdy, i * 2 + c + 1)
                        nc.vector.tensor_tensor(chunk(i, c), dev[c][:], rs[c][:].unsqueeze(1).to_broadcast([P, EK2, CH]),
                                                ALU.mult).then_inc(x_rdy, 1)

            @block.scalar
            def _(act):
                act.wait_ge(ready, 2)
                with act.Fori(0, NCH // 2) as i:
                    for c in range(2):
                        act.wait_ge(dev_rdy, i * 2 + c + 1)
                        act.wait_ge(var_rdy, i * 2)
                        nc.scalar.activation(sq[c][:], dev[c][:], ACT.Square).then_inc(sq_rdy, 1)
                    for c in range(2):
                        act.wait_ge(var_rdy, i * 2 + c + 1)
                        act.wait_ge(rs_rdy, i * 2)
                        nc.scalar.activation(sd[c][:], var[c][:], ACT.Sqrt, bias=eps[:]).then_inc(sd_rdy, 1)

            if out is not None:
                @block.sync
                def _(sp):
                    with sp.Fori(0, NCH) as n:
                        sp.wait_ge(x_rdy, n + 1)
                        sp.dma_start(out.rearrange("(k p) n -> p k n", p=P)[:, :, bass.ds(n * CH, CH)],
                                     x[:, :, bass.ds(n * CH, CH)]).then_inc(x_out, 16)
                    sp.wait_ge(x_out, 16 * NCH)


NEXP = 8
TILES = T // P


def route(nc, stage, t, x, weight, normalise):
    with ExitStack() as ctx:
        m = Names(nc, ctx, stage)
        rw = m.sb("rw", [P, EK2, NEXP])
        rb = m.sb("rb", [P, NEXP])
        iota = m.sb("iota", [P, NEXP])
        xs = [m.sb(f"xs{i}", [P, EK2, CH]) for i in range(2)]
        lg = [m.ps(f"lg{i}", [P, 4, NEXP]) for i in range(2)]
        names = ("logit", "shift", "ex", "prob", "mask1", "mask", "kept")
        logit, shift, ex, prob, mask1, mask, kept = (m.sb(n, [P, 4, NEXP]) for n in names)
        mx, tot, inv, tot2, inv2 = (m.sb(n, [P, 4]) for n in ("mx", "tot", "inv", "tot2", "inv2"))
        top = m.sb("top", [P, 4, 8])
        where = m.sb("where", [P, 4, 8], mybir.dt.uint32)
        wheref = m.sb("wheref", [P, 4, 8])
        w_in, xs_rdy, lg_rdy, ex_rdy, d = (m.sem(n) for n in ("w_in", "xs", "lg", "ex", "d"))
        with nc.Block() as block:
            @block.sync
            def _(sp):
                sp.dma_start(rw[:], t[f"{stage}_w"].rearrange("(k p) n -> p k n", p=P)).then_inc(w_in, 16)
                sp.dma_start(rb[:], t[f"{stage}_b"]).then_inc(w_in, 16)
                sp.dma_start(iota[:], t["iota"]).then_inc(w_in, 16)

            ND = 5 + 2 * 4 + 5 + (4 if normalise else 1)

            @block.tensor
            def _(pe):
                pe.wait_ge(w_in, 48)
                with pe.Fori(0, NCH // 2) as i:
                    for c in range(2):
                        pe.wait_ge(xs_rdy, i * 2 + c + 1)
                        pe.wait_ge(d, i * 2 * ND)
                        for a in range(4):
                            for k in range(EK2):
                                mm = nc.tensor.matmul(lg[c][:, a, :], xs[c][:, k, a * P:(a + 1) * P], rw[:, k, :],
                                                      start=(k == 0), stop=(k == 1))
                        mm.then_inc(lg_rdy, 1)

            @block.scalar
            def _(act):
                with act.Fori(0, NCH // 2) as i:
                    for c in range(2):
                        act.wait_ge(lg_rdy, i * 2)
                        nc.scalar.activation(xs[c][:], x[:, :, bass.ds(i * 2 * CH + c * CH, CH)], ACT.Copy).then_inc(xs_rdy, 1)
                    for c in range(2):
                        act.wait_ge(d, i * 2 * ND + c * ND + 3)
                        nc.scalar.activation(ex[:], shift[:], ACT.Exp).then_inc(ex_rdy, 1)

            @block.vector
            def _(dve):
                dve.wait_ge(w_in, 48)
                wide = [P, 4, NEXP]
                with dve.Fori(0, NCH // 2) as i:
                    for c in range(2):
                        n = c * ND

                        def then(op, last=True, constants=False):
                            nonlocal n
                            op.then_inc(d, 1)
                            n += 1
                            if last:
                                before = dve.to_reg(i * 2 * ND + n)
                                if constants:
                                    dve.wait_ge(w_in, 48)
                                dve.wait_ge(d, before)
                        dve.wait_ge(lg_rdy, i * 2 + c + 1)
                        then(nc.vector.tensor_tensor(logit[:], lg[c][:], rb[:].unsqueeze(1).to_broadcast(wide), ALU.add))
                        then(nc.vector.tensor_reduce(mx[:], logit[:], AX.X, ALU.max))
                        then(nc.vector.tensor_tensor(shift[:], logit[:], mx[:].unsqueeze(2).to_broadcast(wide), ALU.subtract))
                        dve.wait_ge(ex_rdy, i * 2 + c + 1)
                        then(nc.vector.tensor_reduce(tot[:], ex[:], AX.X, ALU.add))
                        then(nc.vector.reciprocal(inv[:], tot[:]))
                        then(nc.vector.tensor_tensor(prob[:], ex[:], inv[:].unsqueeze(2).to_broadcast(wide), ALU.mult), constants=True)
                        for a in range(4):
                            then(nc.vector.max(top[:, a, :], prob[:, a, :]), a == 3, a == 3)
                        for a in range(4):
                            then(nc.vector.max_index(where[:, a, :], top[:, a, :], prob[:, a, :]), a == 3)
                        then(nc.vector.tensor_copy(wheref[:], where[:]))
                        it = iota[:].unsqueeze(1).to_broadcast(wide)
                        then(nc.vector.tensor_tensor(mask1[:], it, wheref[:, :, 0:1].to_broadcast(wide), ALU.is_equal))
                        then(nc.vector.tensor_tensor(mask[:], it, wheref[:, :, 1:2].to_broadcast(wide), ALU.is_equal))
                        then(nc.vector.tensor_tensor(mask[:], mask1[:], mask[:], ALU.add))
                        dst = weight[:, bass.ds(i * 8 + c * 4, 4), 0:NEXP]
                        if not normalise:
                            then(nc.vector.tensor_tensor(dst, prob[:], mask[:], ALU.mult))
                        else:
                            then(nc.vector.tensor_tensor(kept[:], prob[:], mask[:], ALU.mult))
                            then(nc.vector.tensor_reduce(tot2[:], kept[:], AX.X, ALU.add))
                            then(nc.vector.reciprocal(inv2[:], tot2[:]))
                            then(nc.vector.tensor_tensor(dst, kept[:], inv2[:].unsqueeze(2).to_broadcast(wide), ALU.mult))
                        assert n == (c + 1) * ND, (n, ND)


def load_split(nc, stage, jobs):
    with ExitStack() as ctx:
        m = Names(nc, ctx, stage)
        size = max(int(np.prod(hi.shape[1:])) for _, hi, _ in jobs)
        raw = [m.sb(f"raw{i}", [P, size]) for i in range(2)]
        ins = [m.sem(f"in{i}") for i in range(2)]
        hi_rdy, lo_rdy = m.sem("hi"), m.sem("lo")

        def view(n):
            hi = jobs[n][1]
            return raw[n % 2][:, 0:int(np.prod(hi.shape[1:]))].rearrange("p (k n) -> p k n", k=hi.shape[1])
        with nc.Block() as block:
            @block.sync
            def _(sp):
                for n, (src, _, _) in enumerate(jobs):
                    if n >= 2:
                        sp.wait_ge(lo_rdy, n - 1)
                    sp.dma_start(view(n), src).then_inc(ins[n % 2], 16)

            @block.scalar
            def _(act):
                for n, (_, hi, _) in enumerate(jobs):
                    act.wait_ge(ins[n % 2], 16 * (n // 2 + 1))
                    nc.scalar.activation(hi[:], view(n), ACT.Copy).then_inc(hi_rdy, 1)

            @block.vector
            def _(dve):
                for n, (_, hi, lo) in enumerate(jobs):
                    dve.wait_ge(hi_rdy, n + 1)
                    nc.vector.tensor_tensor(lo[:], view(n), hi[:].bitcast(F32), ALU.subtract).then_inc(lo_rdy, 1)


def product3(nc, out, left, right, start, stop):
    (lh, ll), (rh, rl) = left, right
    nc.tensor.matmul(out, ll, rh, start=start, stop=False)
    nc.tensor.matmul(out, lh, rl, start=False, stop=False)
    return nc.tensor.matmul(out, lh, rh, start=False, stop=stop)


RANK, FF = 64, 1024
ER = NEXP * RANK // P
FT = FF // P


def low_rank_ffn(nc, t, x, weight):
    with ExitStack() as ctx:
        m = Names(nc, ctx, "ffn0")
        pair = lambda n, s: (m.sb(n + "_hi", s, F32R), m.sb(n + "_lo", s, F32R))
        w1, w2, w3 = pair("w1", [P, EK2, NEXP * RANK]), pair("w2", [P, ER, FF]), pair("w3", [P, FT, E])
        load_split(nc, "ffn0w", [(t["w1"].rearrange("(k p) n -> p k n", p=P), *w1),
                                 (t["w2"].rearrange("(k p) n -> p k n", p=P), *w2),
                                 (t["w3"].rearrange("(k p) n -> p k n", p=P), *w3)])
        b3 = m.sb("b3", [P, EK2])
        ident = m.sb("ident", [P, P])
        rep = m.sb("rep", [P, 4, NEXP, RANK])
        wb = m.sb("wb", [P, ER, CH])
        xs = pair("xs", [P, EK2, CH])
        tt = m.sb("tt", [P, ER, CH])
        ts = pair("ts", [P, ER, CH])
        hf = [m.sb(f"hf{i}", [P, CH]) for i in range(2)]
        hs = pair("hs", [P, FT, CH])
        low = [m.ps(f"low{i}", [P, CH]) for i in range(2)]
        wacc = [m.ps(f"wacc{i}", [P, CH]) for i in range(2)]
        mid = [m.ps(f"mid{i}", [P, CH]) for i in range(2)]
        rep_rdy, wb_mm, wb_rdy = m.sem("rep"), m.sem("wb_mm"), m.sem("wb")
        out = m.ps("out", [P, EK2, CH])
        b_in, xh, xl, low_mm, tt_rdy, th, tl = (
            m.sem(n) for n in ("b_in", "xh", "xl", "low_mm", "tt", "th", "tl"))
        mid_mm, hf_rdy, hh, hl, out_mm, x_rdy = (m.sem(n) for n in ("mid_mm", "hf", "hh", "hl", "out_mm", "x"))
        with nc.Block() as block:
            @block.sync
            def _(sp):
                sp.dma_start(b3[:], t["b3"]).then_inc(b_in, 16)
                sp.dma_start(ident[:], t["ident"]).then_inc(b_in, 16)

            @block.tensor
            def _(pe):
                pe.wait_ge(b_in, 32)
                with pe.Fori(0, NCH) as n:
                    pe.wait_ge(rep_rdy, n + 1)
                    for r in range(ER):
                        pe.wait_ge(wb_rdy, n * ER + max(r - 1, 0))
                        for a in range(4):
                            mm = nc.tensor.matmul(wacc[r % 2][:, a * P:(a + 1) * P],
                                                  rep[:, a, 2 * r:2 * r + 2, :].rearrange("p e r -> p (e r)"),
                                                  ident[:], start=True, stop=True)
                        mm.then_inc(wb_mm, 1)
                    pe.wait_ge(xl, n + 1)
                    for r in range(ER):
                        pe.wait_ge(tt_rdy, n * ER + max(r - 1, 0))
                        for k in range(EK2):
                            mm = product3(nc, low[r % 2][:], [w[:, k, r * P:(r + 1) * P] for w in w1],
                                          [a[:, k, :] for a in xs], k == 0, k == 1)
                        mm.then_inc(low_mm, 1)
                    for f in range(FT):
                        pe.wait_ge(tl, n * ER + ER)
                        pe.wait_ge(hf_rdy, n * FT + max(f - 1, 0))
                        for r in range(ER):
                            mm = product3(nc, mid[f % 2][:], [w[:, r, f * P:(f + 1) * P] for w in w2],
                                          [a[:, r, :] for a in ts], r == 0, r == ER - 1)
                        mm.then_inc(mid_mm, 1)
                    pe.wait_ge(x_rdy, n)
                    for f in range(FT):
                        pe.wait_ge(hl, n * FT + f + 1)
                        for e in range(EK2):
                            mm = product3(nc, out[:, e, :], [w[:, f, e * P:(e + 1) * P] for w in w3],
                                          [a[:, f, :] for a in hs], f == 0, f == FT - 1)
                    mm.then_inc(out_mm, 1)

            @block.scalar
            def _(act):
                with act.Fori(0, NCH) as n:
                    act.wait_ge(low_mm, n * ER)
                    nc.scalar.activation(xs[0][:], x[:, :, bass.ds(n * CH, CH)], ACT.Copy).then_inc(xh, 1)
                    act.wait_ge(tt_rdy, n * ER)
                    for r in range(ER):
                        act.wait_ge(wb_mm, n * ER + r + 1)
                        nc.scalar.activation(wb[:, r, :], wacc[r % 2][:], ACT.Copy).then_inc(wb_rdy, 1)
                    for r in range(ER):
                        act.wait_ge(tt_rdy, n * ER + r + 1)
                        act.wait_ge(mid_mm, n * FT)
                        nc.scalar.activation(ts[0][:, r, :], tt[:, r, :], ACT.Copy).then_inc(th, 1)
                    for f in range(FT):
                        act.wait_ge(mid_mm, n * FT + f + 1)
                        act.wait_ge(hl, n * FT + max(f - 1, 0))
                        nc.scalar.activation(hf[f % 2][:], mid[f % 2][:], ACT.Gelu).then_inc(hf_rdy, 1)

            @block.vector
            def _(dve):
                dve.wait_ge(b_in, 32)
                with dve.Fori(0, NCH) as n:
                    dve.wait_ge(wb_mm, n * ER)
                    nc.vector.tensor_copy(rep[:], weight[:, bass.ds(n * 4, 4), :].unsqueeze(3).to_broadcast(
                        [P, 4, NEXP, RANK])).then_inc(rep_rdy, 1)
                    dve.wait_ge(xh, n + 1)
                    nc.vector.tensor_tensor(xs[1][:], x[:, :, bass.ds(n * CH, CH)], xs[0][:].bitcast(F32),
                                            ALU.subtract).then_inc(xl, 1)
                    for r in range(ER):
                        dve.wait_ge(wb_rdy, n * ER + r + 1)
                        dve.wait_ge(low_mm, n * ER + r + 1)
                        dve.wait_ge(tl, n * ER)
                        nc.vector.tensor_tensor(tt[:, r, :], low[r % 2][:], wb[:, r, :],
                                                ALU.mult).then_inc(tt_rdy, 1)
                    for r in range(ER):
                        dve.wait_ge(th, n * ER + r + 1)
                        nc.vector.tensor_tensor(ts[1][:, r, :], tt[:, r, :], ts[0][:, r, :].bitcast(F32),
                                                ALU.subtract).then_inc(tl, 1)
                    for f in range(FT):
                        dve.wait_ge(hf_rdy, n * FT + f + 1)
                        dve.wait_ge(out_mm, n)
                        nc.vector.tensor_copy(hs[0][:, f, :], hf[f % 2][:]).then_inc(hh, 1)
                        dve.wait_ge(hh, n * FT + f + 1)
                        nc.vector.tensor_tensor(hs[1][:, f, :], hf[f % 2][:], hs[0][:, f, :].bitcast(F32),
                                                ALU.subtract).then_inc(hl, 1)
                    dve.wait_ge(out_mm, n + 1)
                    for e in range(EK2):
                        here = x[:, e, bass.ds(n * CH, CH)]
                        op = nc.vector.scalar_tensor_tensor(out=here, in0=out[:, e, :], scalar=b3[:, e:e + 1],
                                                            in1=here, op0=ALU.add, op1=ALU.add)
                    op.then_inc(x_rdy, 1)


INNER, DH = 1024, 64
PAIRS = INNER // P
VA = P + 2


def linear_keys(nc, t, x, kv, ks):
    with ExitStack() as ctx:
        m = Names(nc, ctx, "lk")
        w = (m.sb("w_hi", [P, EK2, 2 * INNER], F32R), m.sb("w_lo", [P, EK2, 2 * INNER], F32R))
        load_split(nc, "lkw", [(t["wkv"].rearrange("(k p) n -> p k n", p=P), *w)])
        xs = [(m.sb(f"xh{i}", [P, EK2, CH], F32R), m.sb(f"xl{i}", [P, EK2, CH], F32R)) for i in range(2)]
        ek = m.sb("ek", [P, INNER])
        em = m.sb("em", [P, INNER])
        kf = [m.sb(f"kf{i}", [P, INNER]) for i in range(2)]
        vn = [m.sb(f"vn{i}", [P, PAIRS, VA]) for i in range(2)]
        kacc = m.ps("kacc", [P, INNER])
        vacc = m.ps("vacc", [P, INNER])
        kvacc = [m.ps(f"kvacc{i}", [P, 3, VA]) for i in range(3)]
        ready, xh, xl, k_mm, v_mm, ek_rdy, em_rdy, kf_rdy, vn_rdy, kv_mm, kv_read = (
            m.sem(n) for n in ("ready", "xh", "xl", "k_mm", "v_mm", "ek", "em", "kf", "vn", "kv_mm", "kv_read"))
        NT = S // P
        with nc.Block() as block:
            @block.tensor
            def _(pe):
                pe.wait_ge(ready, 4)
                with pe.Fori(0, B) as b:
                    def sums(tile):
                        n = b * NT + tile
                        pe.wait_ge(kf_rdy, n + 1)
                        pe.wait_ge(vn_rdy, n + 1)
                        if tile == 0:
                            pe.wait_ge(kv_read, b * 4)
                        for p in range(PAIRS):
                            mm = nc.tensor.matmul(kvacc[p // 3][:, p % 3, :], kf[tile % 2][:, p * P:(p + 1) * P],
                                                  vn[tile % 2][:, p, :], start=(tile == 0 and p % 3 == 0),
                                                  stop=(tile == NT - 1), skip_group_check=True)
                        mm.then_inc(kv_mm, 1)
                    for tile in range(NT):
                        n = b * NT + tile
                        c, a = tile // 4, tile % 4
                        if a == 0:
                            pe.wait_ge(xl, b * CPB + c + 1)
                        for acc, done, mm_rdy, base in ((kacc, kf_rdy, k_mm, 0), (vacc, vn_rdy, v_mm, INNER)):
                            pe.wait_ge(done, n)
                            for h in range(2):
                                for k in range(EK2):
                                    cols = slice(base + h * CH, base + (h + 1) * CH)
                                    mm = product3(nc, acc[:, h * CH:(h + 1) * CH],
                                                  [s[:, k, a * P:(a + 1) * P] for s in xs[c % 2]],
                                                  [s[:, k, cols] for s in w], k == 0, k == 1)
                            mm.then_inc(mm_rdy, 1)
                        if tile:
                            sums(tile - 1)
                    sums(NT - 1)

            @block.scalar
            def _(act):
                act.wait_ge(ready, 4)
                with act.Fori(0, B) as b:
                    for tile in range(NT):
                        n = b * NT + tile
                        if tile % 4 == 0:
                            act.wait_ge(v_mm, b * NT + max(tile - 4, 0))
                            nc.scalar.activation(xs[tile // 4 % 2][0][:], x[:, :, bass.ds(b * S + tile * P, CH)],
                                                 ACT.Copy).then_inc(xh, 1)
                        act.wait_ge(k_mm, n + 1)
                        act.wait_ge(em_rdy, n)
                        nc.scalar.activation(ek[:], kacc[:], ACT.Exp).then_inc(ek_rdy, 1)
                        act.wait_ge(v_mm, n + 1)
                        act.wait_ge(kv_mm, b * NT + max(tile - 1, 0))
                        nc.scalar.activation(vn[tile % 2][:, :, 0:P], vacc[:].rearrange("p (a n) -> p a n", a=PAIRS),
                                             ACT.Copy).then_inc(vn_rdy, 1)

            @block.vector
            def _(dve):
                for i in range(2):
                    nc.vector.memset(vn[i][:, :, P:VA], 1.0).then_inc(ready, 1)
                nc.vector.memset(kv[:], 0.0).then_inc(ready, 1)
                nc.vector.memset(ks[:], 0.0).then_inc(ready, 1)
                dve.wait_ge(ready, 4)
                with dve.Fori(0, B) as b:
                    for tile in range(NT):
                        n = b * NT + tile
                        if tile % 4 == 0:
                            dve.wait_ge(xh, b * CPB + tile // 4 + 1)
                            nc.vector.tensor_tensor(xs[tile // 4 % 2][1][:], x[:, :, bass.ds(b * S + tile * P, CH)],
                                                    xs[tile // 4 % 2][0][:].bitcast(F32), ALU.subtract).then_inc(xl, 1)
                        dve.wait_ge(ek_rdy, n + 1)
                        dve.wait_ge(kf_rdy, n)
                        nc.vector.tensor_scalar(em[:], ek[:], 1.0, None, ALU.min).then_inc(em_rdy, 1)
                        dve.wait_ge(em_rdy, n + 1)
                        dve.wait_ge(kv_mm, b * NT + max(tile - 1, 0))
                        nc.vector.scalar_tensor_tensor(out=kf[tile % 2][:], in0=kacc[:], scalar=0.0, in1=em[:],
                                                       op0=ALU.max, op1=ALU.add).then_inc(kf_rdy, 1)
                    dve.wait_ge(kv_mm, b * NT + NT)
                    for h in range(2):
                        rows = slice(h * DH, (h + 1) * DH)
                        for g in range(3):
                            np_ = min(3, PAIRS - 3 * g)
                            op = nc.vector.tensor_copy(kv[rows, bass.ds(b * PAIRS + 3 * g, np_), rows],
                                                       kvacc[g][rows, 0:np_, rows])
                            op2 = nc.vector.tensor_copy(ks[rows, bass.ds(b * PAIRS + 3 * g, np_), rows],
                                                        kvacc[g][rows, 0:np_, P:P + 1].to_broadcast([DH, np_, DH]))
                        op.then_inc(kv_read, 1)
                        op2.then_inc(kv_read, 1)


def linear_attention(nc, t, x, kv, ks):
    with ExitStack() as ctx:
        m = Names(nc, ctx, "la")
        pair = lambda n, s: (m.sb(n + "_hi", s, F32R), m.sb(n + "_lo", s, F32R))
        wq, wo = pair("wq", [P, EK2, INNER]), pair("wo", [P, PAIRS, E])
        load_split(nc, "law", [(t["wq1"].rearrange("(k p) n -> p k n", p=P), *wq),
                               (t["wout"].rearrange("(k p) n -> p k n", p=P), *wo)])
        bo = m.sb("bo", [P, EK2])
        xs = pair("xs", [P, EK2, CH])
        eq, em, qf, dn, rd, of = ([m.sb(f"{n}{i}", [P, CH]) for i in range(2)] for n in ("eq", "em", "qf", "dn", "rd", "of"))
        os_ = pair("os", [P, PAIRS, CH])
        qacc = [m.ps(f"qacc{i}", [P, CH]) for i in range(2)]
        num, den = ([m.ps(f"{n}{i}", [P, CH]) for i in range(2)] for n in ("num", "den"))
        out = m.ps("out", [P, EK2, CH])
        b_in, xh, xl, q_mm, eq_rdy, em_rdy, qf_rdy, nd_mm, dn_rdy, rd_rdy, of_rdy, oh, ol, out_mm, x_rdy = (
            m.sem(n) for n in ("b_in", "xh", "xl", "q_mm", "eq", "em", "qf", "nd_mm", "dn", "rd", "of", "oh", "ol", "out_mm", "x"))
        with nc.Block() as block:
            @block.sync
            def _(sp):
                sp.dma_start(bo[:], t["bout"]).then_inc(b_in, 16)

            @block.tensor
            def _(pe):
                for b in range(B):
                    with pe.Fori(b * CPB, (b + 1) * CPB) as n:
                        pe.wait_ge(xl, n + 1)

                        def queries(p):
                            pe.wait_ge(qf_rdy, n * PAIRS + max(p - 1, 0))
                            for k in range(EK2):
                                mm = product3(nc, qacc[p % 2][:], [w[:, k, p * P:(p + 1) * P] for w in wq],
                                              [a[:, k, :] for a in xs], k == 0, k == 1)
                            mm.then_inc(q_mm, 1)

                        queries(0)
                        for p in range(PAIRS):
                            if p + 1 < PAIRS:
                                queries(p + 1)
                            pe.wait_ge(qf_rdy, n * PAIRS + p + 1)
                            pe.wait_ge(of_rdy, n * PAIRS + max(p - 1, 0))
                            nc.tensor.matmul(den[p % 2][:], ks[:, b * PAIRS + p, :], qf[p % 2][:], start=True, stop=True)
                            nc.tensor.matmul(num[p % 2][:], kv[:, b * PAIRS + p, :], qf[p % 2][:],
                                             start=True, stop=True).then_inc(nd_mm, 1)
                        pe.wait_ge(x_rdy, n)
                        for p in range(PAIRS):
                            pe.wait_ge(ol, n * PAIRS + p + 1)
                            for e in range(EK2):
                                mm = product3(nc, out[:, e, :], [w[:, p, e * P:(e + 1) * P] for w in wo],
                                              [a[:, p, :] for a in os_], p == 0, p == PAIRS - 1)
                        mm.then_inc(out_mm, 1)

            @block.scalar
            def _(act):
                with act.Fori(0, NCH) as n:
                    act.wait_ge(q_mm, n * PAIRS)
                    nc.scalar.activation(xs[0][:], x[:, :, bass.ds(n * CH, CH)], ACT.Copy).then_inc(xh, 1)
                    for p in range(PAIRS):
                        act.wait_ge(q_mm, n * PAIRS + p + 1)
                        act.wait_ge(em_rdy, n * PAIRS + max(p - 1, 0))
                        nc.scalar.activation(eq[p % 2][:], qacc[p % 2][:], ACT.Exp).then_inc(eq_rdy, 1)
                        if p:
                            act.wait_ge(of_rdy, n * PAIRS + p)
                            act.wait_ge(out_mm, n)
                            nc.scalar.activation(os_[0][:, p - 1, :], of[(p - 1) % 2][:], ACT.Copy).then_inc(oh, 1)
                    act.wait_ge(of_rdy, n * PAIRS + PAIRS)
                    nc.scalar.activation(os_[0][:, PAIRS - 1, :], of[(PAIRS - 1) % 2][:], ACT.Copy).then_inc(oh, 1)

            @block.vector
            def _(dve):
                dve.wait_ge(b_in, 16)
                with dve.Fori(0, NCH) as n:
                    dve.wait_ge(xh, n + 1)
                    nc.vector.tensor_tensor(xs[1][:], x[:, :, bass.ds(n * CH, CH)], xs[0][:].bitcast(F32),
                                            ALU.subtract).then_inc(xl, 1)

                    def low_of(p):
                        dve.wait_ge(oh, n * PAIRS + p + 1)
                        nc.vector.tensor_tensor(os_[1][:, p, :], of[p % 2][:], os_[0][:, p, :].bitcast(F32),
                                                ALU.subtract).then_inc(ol, 1)

                    def features(p):
                        dve.wait_ge(eq_rdy, n * PAIRS + p + 1)
                        dve.wait_ge(qf_rdy, n * PAIRS + max(p - 1, 0))
                        nc.vector.tensor_scalar(em[p % 2][:], eq[p % 2][:], 1.0, None, ALU.min).then_inc(em_rdy, 1)
                        dve.wait_ge(em_rdy, n * PAIRS + p + 1)
                        dve.wait_ge(nd_mm, n * PAIRS + max(p - 1, 0))
                        nc.vector.scalar_tensor_tensor(out=qf[p % 2][:], in0=qacc[p % 2][:], scalar=0.0, in1=em[p % 2][:],
                                                       op0=ALU.max, op1=ALU.add).then_inc(qf_rdy, 1)
                    features(0)
                    for p in range(PAIRS):
                        if p + 1 < PAIRS:
                            features(p + 1)
                        dve.wait_ge(nd_mm, n * PAIRS + p + 1)
                        dve.wait_ge(rd_rdy, n * PAIRS + max(p - 1, 0))
                        nc.vector.tensor_scalar(dn[p % 2][:], den[p % 2][:], 1e-6, None, ALU.add).then_inc(dn_rdy, 1)
                        dve.wait_ge(dn_rdy, n * PAIRS + p + 1)
                        dve.wait_ge(of_rdy, n * PAIRS + max(p - 1, 0))
                        nc.vector.reciprocal(rd[p % 2][:], dn[p % 2][:]).then_inc(rd_rdy, 1)
                        dve.wait_ge(rd_rdy, n * PAIRS + p + 1)
                        dve.wait_ge(ol, n * PAIRS + max(p - 1, 0))
                        nc.vector.tensor_tensor(of[p % 2][:], num[p % 2][:], rd[p % 2][:], ALU.mult).then_inc(of_rdy, 1)
                        if p:
                            low_of(p - 1)
                    low_of(PAIRS - 1)
                    dve.wait_ge(out_mm, n + 1)
                    for e in range(EK2):
                        here = x[:, e, bass.ds(n * CH, CH)]
                        op = nc.vector.scalar_tensor_tensor(out=here, in0=out[:, e, :], scalar=bo[:, e:e + 1],
                                                            in1=here, op0=ALU.add, op1=ALU.add)
                    op.then_inc(x_rdy, 1)


HF = 512
HT = HF // P


def routed_ffn(nc, t, x, weight):
    with ExitStack() as ctx:
        m = Names(nc, ctx, "ffn1")
        xh, xl = m.sb("xh", [P, EK2, T], F32R), m.sb("xl", [P, EK2, T], F32R)
        ident = m.sb("ident", [P, P])
        raw = m.sb("raw", [P, 3, HT * E])
        wh = [m.sb(f"wh{i}", [P, 3, HT * E], F32R) for i in range(2)]
        wl = [m.sb(f"wl{i}", [P, 3, HT * E], F32R) for i in range(2)]
        rep = m.sb("rep", [P, 4, P])
        wb = [m.sb(f"wb{i}", [P, CH]) for i in range(2)]
        sg = [m.sb(f"sg{i}", [P, CH]) for i in range(2)]
        su = m.sb("su", [P, CH])
        hw = [m.sb(f"hw{i}", [P, CH]) for i in range(2)]
        hh = [m.sb(f"hh{i}", [P, HT, CH], F32R) for i in range(2)]
        hl = [m.sb(f"hl{i}", [P, HT, CH], F32R) for i in range(2)]
        gate = [m.ps(f"gate{i}", [P, CH]) for i in range(2)]
        up = [m.ps(f"up{i}", [P, CH]) for i in range(2)]
        wacc = m.ps("wacc", [P, CH])
        out = m.ps("out", [P, EK2, CH])
        id_in, xh_rdy, xl_rdy, raw_in, wh_rdy, wl_rdy, rep_rdy, wb_mm, wb_rdy = (
            m.sem(n) for n in ("id_in", "xh", "xl", "raw_in", "wh", "wl", "rep", "wb_mm", "wb"))
        gu_mm, sg_rdy, su_rdy, hw_rdy, hh_rdy, hl_rdy, out_mm, x_rdy = (
            m.sem(n) for n in ("gu_mm", "sg", "su", "hw", "hh", "hl", "out_mm", "x"))
        one_rdy = m.sem("one")
        NE = NEXP + 1

        def operand(i, which, k, a, b):
            n = HF if which < 2 else E
            return [w[i][:, which, k * n + a:k * n + b] for w in (wh, wl)]

        def every_expert(eng, body):
            body(0, 0)
            with eng.Fori(0, NEXP // 2) as pair:
                body(pair * 2 + 1, 1)
                body(pair * 2 + 2, 0)

        def next_high(eng, expert, split):
            eng.wait_ge(wl_rdy, 1)
            split(1, 1)
            expert(0, 0)
            with eng.Fori(0, NEXP // 2 - 1) as pair:
                eng.wait_ge(out_mm, pair * 2 * NCH + NCH)
                eng.wait_ge(wl_rdy, pair * 2 + 2)
                split(pair * 2 + 2, 0)
                expert(pair * 2 + 1, 1)
                eng.wait_ge(out_mm, pair * 2 * NCH + 2 * NCH)
                eng.wait_ge(wl_rdy, pair * 2 + 3)
                split(pair * 2 + 3, 1)
                expert(pair * 2 + 2, 0)
            eng.wait_ge(out_mm, (NEXP - 1) * NCH)
            eng.wait_ge(wl_rdy, NEXP)
            split(NEXP, 0)
            expert(NEXP - 1, 1)
            expert(NEXP, 0)

        with nc.Block() as block:
            @block.sync
            def _(sp):
                sp.dma_start(ident[:], t["ident"]).then_inc(id_in, 16)
                with sp.Fori(0, NE) as g:
                    sp.wait_ge(wl_rdy, g)
                    sp.dma_start(raw[:].rearrange("p a n -> p (a n)"), t["experts"].rearrange("e p n -> p e n")[
                        :, bass.ds(g, 1)].rearrange("p e n -> p (e n)")).then_inc(raw_in, 16)

            @block.tensor
            def _(pe):
                pe.wait_ge(id_in, 16)
                pe.wait_ge(xl_rdy, NCH)

                def expert(g, i):
                    with pe.Fori(0, NCH // 2) as mm_:
                        base = g * NCH + mm_ * 2
                        pe.wait_ge(wl_rdy, g + 1)
                        for c in range(2):
                            pe.wait_ge(rep_rdy, base + c + 1)
                            pe.wait_ge(wb_rdy, base + c)
                            for a in range(4):
                                mm = nc.tensor.matmul(wacc[:, a * P:(a + 1) * P], rep[:, a, :], ident[:],
                                                      start=True, stop=True)
                            mm.then_inc(wb_mm, 1)
                            for h in range(HT):
                                pe.wait_ge(su_rdy, base * HT + max(c * HT + h - 1, 0))
                                for which, acc in ((0, gate), (1, up)):
                                    for k in range(EK2):
                                        mm = product3(nc, acc[h % 2][:], operand(i, which, k, h * P, (h + 1) * P),
                                                      [s[:, k, bass.ds(mm_ * 2 * CH + c * CH, CH)] for s in (xh, xl)],
                                                      k == 0, k == 1)
                                mm.then_inc(gu_mm, 1)
                        for c in range(2):
                            pe.wait_ge(x_rdy, base + c)
                            for h in range(HT):
                                pe.wait_ge(hl_rdy, base * HT + c * HT + h + 1)
                                for e in range(EK2):
                                    mm = product3(nc, out[:, e, :], operand(i, 2, h, e * P, (e + 1) * P),
                                                  [hh[c][:, h, :], hl[c][:, h, :]], h == 0, h == HT - 1)
                            mm.then_inc(out_mm, 1)
                every_expert(pe, expert)

            @block.scalar
            def _(act):
                with act.Fori(0, NCH) as n:
                    nc.scalar.activation(xh[:, :, bass.ds(n * CH, CH)], x[:, :, bass.ds(n * CH, CH)],
                                         ACT.Copy).then_inc(xh_rdy, 1)

                def split_high(g, i):
                    act.wait_ge(raw_in, g * 16 + 16)
                    nc.scalar.activation(wh[i][:], raw[:], ACT.Copy).then_inc(wh_rdy, 1)
                split_high(0, 0)

                def high(base, f):
                    act.wait_ge(hw_rdy, base * HT + f + 1)
                    act.wait_ge(out_mm, base)
                    nc.scalar.activation(hh[f // HT][:, f % HT, :], hw[f % 2][:], ACT.Copy).then_inc(hh_rdy, 1)

                def expert(g, i):
                    with act.Fori(0, NCH // 2) as mm_:
                        base = g * NCH + mm_ * 2
                        for c in range(2):
                            act.wait_ge(wb_mm, base + c + 1)
                            act.wait_ge(hw_rdy, base * HT)
                            nc.scalar.activation(wb[c][:], wacc[:], ACT.Copy).then_inc(wb_rdy, 1)
                            for h in range(HT):
                                f = c * HT + h
                                act.wait_ge(gu_mm, base * HT + f + 1)
                                act.wait_ge(su_rdy, base * HT + max(f - 1, 0))
                                nc.scalar.activation(sg[h % 2][:], gate[h % 2][:], ACT.Silu).then_inc(sg_rdy, 1)
                                if f:
                                    high(base, f - 1)
                        high(base, 2 * HT - 1)

                next_high(act, expert, split_high)

            @block.vector
            def _(dve):
                nc.vector.memset(weight[:, :, 0:1], 1.0).then_inc(one_rdy, 1)
                dve.wait_ge(one_rdy, 1)
                with dve.Fori(0, NCH) as n:
                    dve.wait_ge(xh_rdy, n + 1)
                    nc.vector.tensor_tensor(xl[:, :, bass.ds(n * CH, CH)], x[:, :, bass.ds(n * CH, CH)],
                                            xh[:, :, bass.ds(n * CH, CH)].bitcast(F32), ALU.subtract).then_inc(xl_rdy, 1)

                def split_low(g, i):
                    dve.wait_ge(wh_rdy, g + 1)
                    nc.vector.tensor_tensor(wl[i][:], raw[:], wh[i][:].bitcast(F32), ALU.subtract).then_inc(wl_rdy, 1)
                split_low(0, 0)

                def low(base, f):
                    dve.wait_ge(hh_rdy, base * HT + f + 1)
                    nc.vector.tensor_tensor(hl[f // HT][:, f % HT, :], hw[f % 2][:], hh[f // HT][:, f % HT, :].bitcast(F32),
                                            ALU.subtract).then_inc(hl_rdy, 1)

                def expert(g, i):
                    with dve.Fori(0, NCH // 2) as mm_:
                        base = g * NCH + mm_ * 2
                        for c in range(2):
                            dve.wait_ge(wb_mm, base + c)
                            nc.vector.tensor_copy(
                                rep[:], weight[:, bass.ds(mm_ * 8 + c * 4, 4), bass.ds(g, 1)].to_broadcast(
                                    [P, 4, P])).then_inc(rep_rdy, 1)
                            for h in range(HT):
                                f = c * HT + h
                                dve.wait_ge(sg_rdy, base * HT + f + 1)
                                dve.wait_ge(hw_rdy, base * HT + f)
                                nc.vector.tensor_tensor(su[:], sg[h % 2][:], up[h % 2][:], ALU.mult).then_inc(su_rdy, 1)
                                dve.wait_ge(su_rdy, base * HT + f + 1)
                                dve.wait_ge(wb_rdy, base + c + 1)
                                dve.wait_ge(hl_rdy, base * HT + max(f - 1, 0))
                                nc.vector.tensor_tensor(hw[h % 2][:], su[:], wb[c][:], ALU.mult).then_inc(hw_rdy, 1)
                                if f:
                                    low(base, f - 1)
                        low(base, 2 * HT - 1)
                        for c in range(2):
                            dve.wait_ge(out_mm, base + c + 1)
                            here = x[:, :, bass.ds(mm_ * 2 * CH + c * CH, CH)]
                            dve.wait_ge(x_rdy, base + c)
                            nc.vector.tensor_tensor(here, here, out[:], ALU.add).then_inc(x_rdy, 1)

                next_high(dve, expert, split_low)


def transformer(nc, t, out):
    dram = lambda n, s, d: nc.dram_tensor(n, s, d, kind="Internal").ap()
    scratch = (dram("q_parts", [3, NHP * HD, S], BF16), dram("k_late", [3, NHP * HD, S], BF16),
               dram("k_early", [3, NHP * HD, S], BF16), dram("v_parts", [NHP, 2, P, KT * VC], BF16))
    sums = (dram("value_sums", [3, NH * HD, S], F32), dram("band_sums", [3, NH * HD, S], F32),
            dram("denominators", [NH, S], F32))
    project_qkv(nc, t, scratch)
    attention(nc, t, scratch, sums)
    with nc.sbuf_tensor("x", [P, EK2, T], F32) as x, nc.sbuf_tensor("weight", [P, TILES, NEXP + 1], F32) as weight:
        project_attention(nc, t, sums, x)
        layer_norm(nc, "ln0", x)
        route(nc, "route0", t, x, weight[:, :, 1:NEXP + 1], False)
        low_rank_ffn(nc, t, x, weight[:, :, 1:NEXP + 1])
        layer_norm(nc, "ln1", x)
        with nc.sbuf_tensor("kv", [P, B * PAIRS, P], F32) as kv, nc.sbuf_tensor("ks", [P, B * PAIRS, P], F32) as ks:
            linear_keys(nc, t, x, kv, ks)
            linear_attention(nc, t, x, kv, ks)
        layer_norm(nc, "ln2", x)
        route(nc, "route1", t, x, weight[:, :, 1:NEXP + 1], True)
        routed_ffn(nc, t, x, weight)
        layer_norm(nc, "ln3", x, out)


def layouts(i):
    c = np.ascontiguousarray
    heads = lambda v: np.tile(v, H)
    halves = lambda v: c(v.reshape(EK2, P).T)
    rk, rv = i["L0_attn_rel_k"], i["L0_attn_rel_v"]
    far = 2 * REL
    place = lambda d: np.clip(d, -REL, REL) + REL
    masks = np.zeros((KS, 3), np.float32)
    for r, p in enumerate(K_PARTS):
        masks[r * HD:(r + 1) * HD, p] = 1
    m, w = np.meshgrid(np.arange(P), np.arange(W), indexing="ij")

    def expert(g, u, d):
        rows = lambda a: a.reshape(-1, P, a.shape[1]).transpose(1, 0, 2).reshape(P, -1)
        return np.concatenate([rows(c(g.T)), rows(c(u.T)), rows(c(d.T))], 1)
    experts = [expert(i["L1_ffn_sg"], i["L1_ffn_su"], i["L1_ffn_sd"])] + [
        expert(i["L1_ffn_eg"][e], i["L1_ffn_eu"][e], i["L1_ffn_ed"][e]) for e in range(NEXP)]
    wqkv = i["L1_attn_Wqkv"]
    return {
        "xt": c(i["L0_attn_hidden_states"].reshape(T, E).T),
        "wqkv": c(np.stack([i[f"L0_attn_W{n}"].T for n in "qkv"])),
        "cols": c(np.stack([i["L0_attn_bq"], i["L0_attn_bk"], heads(rk[far]), heads(rk[0])], 1)),
        "rows": c(np.broadcast_to(np.stack([i["L0_attn_bv"], heads(rv[far]), heads(rv[0])]), (P, 3, E))),
        "rk": c(np.tile(rk[place(np.arange(TAB) - (W - 1 - PAD))].T, (NPT, 1))),
        "rkb": c(np.tile(np.stack([rk[far], rk[0]], 1), (NPT, 1))),
        "msk": masks,
        "rv": c(rv[place(m - w + PAD)]),
        "rvb": c(np.broadcast_to(np.stack([rv[far], rv[0]]), (P, 2, HD))),
        "wo": c(i["L0_attn_Wo"].T), "bo": halves(i["L0_attn_bo"]),
        "route0_w": c(i["L0_ffn_router_w"]), "route0_b": c(np.broadcast_to(i["L0_ffn_router_b"], (P, NEXP))),
        "route1_w": c(i["L1_ffn_router_w"].T), "route1_b": np.zeros((P, NEXP), np.float32),
        "iota": c(np.broadcast_to(np.arange(NEXP, dtype=np.float32), (P, NEXP))),
        "ident": np.eye(P, dtype=np.float32),
        "w1": c(i["L0_ffn_w1"].transpose(1, 0, 2).reshape(E, NEXP * RANK)),
        "w2": c(i["L0_ffn_w2"].reshape(NEXP * RANK, FF)),
        "w3": c(i["L0_ffn_lin2_w"]), "b3": halves(i["L0_ffn_lin2_b"]),
        "wkv": c(wqkv[:, INNER:]), "wq1": c(wqkv[:, :INNER]),
        "wout": c(i["L1_attn_Wout"]), "bout": halves(i["L1_attn_bout"]),
        "experts": c(np.stack(experts)),
    }


def kernel(**inputs):
    import concourse.bacc as bacc
    from concourse.bass_utils import run_bass_kernel_spmd

    nc = bacc.Bacc("TRN2", target_bir_lowering=False, num_devices=1)
    arrays = {f"in_{n}": a for n, a in layouts({n: np.asarray(a) for n, a in inputs.items()}).items()}
    t = {n[3:]: nc.dram_tensor(n, a.shape, mybir.dt.from_np(a.dtype), kind="ExternalInput").ap()
         for n, a in arrays.items()}
    out = nc.dram_tensor("out_t", [E, T], F32, kind="ExternalOutput").ap()
    transformer(nc, t, out)
    got = run_bass_kernel_spmd(nc, [arrays], core_ids=[0])
    return np.ascontiguousarray(got.results[0]["out_t"].T).reshape(B, S, E)
```

```python
from contextlib import ExitStack

import numpy as np

import concourse.bass as bass
from concourse import mybir

F32 = mybir.dt.float32
F32R = mybir.dt.float32r
BF16 = mybir.dt.bfloat16
ALU = mybir.AluOpType
ACT = mybir.ActivationFunctionType
AX = mybir.AxisListType
RMAX = bass.bass_isa.ReduceOp.max

P = 128
B, S, E = 2, 2048, 256
T = B * S
H, HD = 16, 16
REL = 20
NREL = 2 * REL + 1
EK2 = E // P
CH = 512
NCH = T // CH
CPB = S // CH
KT = S // P
PAD = REL - 1
W = P + 2 * PAD
HALF = 1024
NH = B * H
NHP = NH + 4
VC = 32
EPS = 1e-5
ONE = 1


class Semaphores:

    def __init__(self, nc, ctx, stage):
        self.nc, self.stage, self.mine = nc, stage, []
        ctx.callback(self.end)

    def __call__(self, name):
        self.mine.append(self.nc.alloc_semaphore(name=f"{self.stage}_{name}"))
        return self.mine[-1]

    def start(self):
        for one in self.mine:
            self.nc.sync.sem_inc(one, ONE)
        self.nc.all_engine_barrier()

    def end(self):
        self.nc.clear_and_free_semaphores(self.mine)
        self.nc.all_engine_barrier()


def project_qkv(nc, t, scratch):
    qs, kh, kl, vs = scratch
    with ExitStack() as ctx:
        sb = lambda n, s, d: ctx.enter_context(nc.sbuf_tensor("qkv_" + n, s, d))
        ps = lambda n, s: ctx.enter_context(nc.psum_tensor("qkv_" + n, s, F32))
        sem = Semaphores(nc, ctx, "qkv")
        wts = sb("wts", [P, 3, EK2, E], F32)
        cols = sb("cols", [P, EK2, 4], F32)
        kbias = sb("kbias", [P, EK2, 2], F32)
        rows = sb("rows", [P, 3, E], F32)
        vrow = sb("vrow", [P, 2, E], F32)
        xc = [sb(f"xc{i}", [P, EK2, CH], F32) for i in range(2)]
        full = [sb(f"full{i}", [P, CH], F32) for i in range(2)]
        rest = [sb(f"rest{i}", [P, CH], F32) for i in range(2)]
        part = [sb(f"part{i}", [P, 3, CH], BF16) for i in range(4)]
        vst = sb("vst", [P, 2, H, KT, VC], F32)
        acc = [ps(f"acc{i}", [P, CH]) for i in range(4)]
        vacc = ps("vacc", [P, 4 * E])
        w_in, x_in0, x_in1 = sem("w_in"), sem("x_in0"), sem("x_in1")
        x_in = [x_in0, x_in1]
        prep, qk_mm, v_mm = sem("prep"), sem("qk_mm"), sem("v_mm")
        f_rdy, p1_rdy, r_rdy, p2_rdy, p3_rdy = (sem(n) for n in ("f_rdy", "p1_rdy", "r_rdy", "p2_rdy", "p3_rdy"))
        v_rdy = sem("v_rdy")
        part_out = [sem(f"part_out{i}") for i in range(4)]
        v_out, pad_out = sem("v_out"), sem("pad_out")
        units = [(0, ("q", 0), qs, 0), (1, ("q", 1), qs, 1), (2, (0, 0), kh, 0), (2, (0, 1), kl, 0),
                 (3, (1, 0), kh, 1), (3, (1, 1), kl, 1)]
        NU = len(units)
        NUB = NU * CPB

        def bias_of(key):
            return cols[:, key[1], 0:1] if key[0] == "q" else kbias[:, key[0], key[1]:key[1] + 1]

        def s_slot(c, s):
            return (c * NU + s) % 4

        sem.start()
        with nc.Block() as block:
            @block.sync
            def _(sp):
                sp.dma_start(wts[:], t["wqkv"].rearrange("w (k p) n -> p w k n", p=P)).then_inc(w_in, 16)
                sp.dma_start(cols[:], t["cols"].rearrange("(k p) n -> p k n", p=P)).then_inc(w_in, 16)
                sp.dma_start(rows[:], t["rows"]).then_inc(w_in, 16)
                with sp.Fori(0, B) as b:
                    for c in range(CPB):
                        if c >= 2:
                            sp.wait_ge(v_mm, b * CPB + c - 1 + ONE)
                        else:
                            sp.wait_ge(v_mm, b * CPB + ONE)
                        sp.dma_start(xc[c % 2][:], t["xt"].rearrange("(k p) n -> p k n", p=P)[
                            :, :, bass.ds(b * S + c * CH, CH)]).then_inc(x_in[c % 2], 16)
                        for s, (_, _, dst, e) in enumerate(units):
                            sp.wait_ge(p3_rdy, b * NUB + c * NU + s + 1 + ONE)
                            sp.dma_start(dst.rearrange("a r n -> r a n")[
                                bass.ds(b * E + e * P, P), :, c * CH:(c + 1) * CH],
                                part[s_slot(c, s)][:]).then_inc(part_out[s_slot(c, s)], 16)
                    sp.wait_ge(v_rdy, b * CPB + CPB + ONE)
                    for l in range(2):
                        sp.dma_start(vs.rearrange("h l p c -> p h l c")[:, bass.ds(b * H, H), l],
                                     vst[:, l].rearrange("p h t c -> p h (t c)")).then_inc(v_out, 16)
                for i in range(4):
                    sp.wait_ge(part_out[i], 16 * B * NUB // 4 + ONE)
                sp.wait_ge(v_out, 32 * B + ONE)
                for dst in (qs, kh, kl):
                    sp.dma_start(dst[:, NH * HD:NHP * HD], dst[:, 0:4 * HD]).then_inc(pad_out, 16)
                sp.dma_start(vs[NH:NHP], vs[0:4]).then_inc(pad_out, 16)
                sp.wait_ge(pad_out, 64 + ONE)

            @block.tensor
            def _(pe):
                pe.wait_ge(w_in, 48 + ONE)
                with pe.Fori(0, B) as b:
                    for c in range(CPB):
                        x = xc[c % 2]
                        pe.wait_ge(x_in[c % 2], b * 32 + 16 * (c // 2) + 16 + ONE)
                        pe.wait_ge(p1_rdy, b * NUB + c * NU + ONE)
                        for a, (w, e) in enumerate(((0, 0), (0, 1), (1, 0), (1, 1))):
                            for k in range(EK2):
                                mm = nc.tensor.matmul(acc[a][:], wts[:, w, k, e * P:(e + 1) * P], x[:, k, :],
                                                      start=(k == 0), stop=(k == 1))
                            mm.then_inc(qk_mm, 1)
                        pe.wait_ge(v_rdy, b * CPB + c + ONE)
                        for i in range(4):
                            for k in range(EK2):
                                mm = nc.tensor.matmul(vacc[:, i * E:(i + 1) * E], x[:, k, i * P:(i + 1) * P],
                                                      wts[:, 2, k, :], start=(k == 0), stop=(k == 1))
                        mm.then_inc(v_mm, 1)

            @block.scalar
            def _(act):
                act.wait_ge(prep, 6 + ONE)
                with act.Fori(0, B) as b:
                    for c in range(CPB):
                        for s, (a, key, _, _) in enumerate(units):
                            n = c * NU + s
                            act.wait_ge(qk_mm, b * 4 * CPB + 4 * c + a + 1 + ONE)
                            act.wait_ge(r_rdy, b * NUB + max(n - 1, 0) + ONE)
                            nc.scalar.activation(full[n % 2][:], acc[a][:], ACT.Identity,
                                                 bias=bias_of(key)).then_inc(f_rdy, 1)
                            act.wait_ge(part_out[n % 4], b * (16 * NUB // 4) + 16 * (n // 4) + ONE)
                            nc.scalar.activation(part[n % 4][:, 0, :], acc[a][:], ACT.Identity,
                                                 bias=bias_of(key)).then_inc(p1_rdy, 1)
                            act.wait_ge(r_rdy, b * NUB + n + 1 + ONE)
                            nc.scalar.activation(part[n % 4][:, 1, :], rest[n % 2][:], ACT.Copy).then_inc(p2_rdy, 1)

            @block.vector
            def _(dve):
                nc.vector.memset(vst[:, :, :, :, HD:VC], 1.0).then_inc(prep, 1)
                dve.wait_ge(w_in, 48 + ONE)
                for e in range(EK2):
                    for l in range(2):
                        nc.vector.tensor_tensor(kbias[:, e, l:l + 1], cols[:, e, 1:2], cols[:, e, 2 + l:3 + l],
                                                ALU.add).then_inc(prep, 1)
                for l in range(2):
                    op = nc.vector.tensor_tensor(vrow[:, l, :], rows[:, 0, :], rows[:, 1 + l, :], ALU.add)
                    if l == 1:
                        op.then_inc(prep, 1)
                dve.wait_ge(prep, 6 + ONE)
                with dve.Fori(0, B) as b:
                    for c in range(CPB):
                        for s in range(NU):
                            n = c * NU + s
                            dve.wait_ge(f_rdy, b * NUB + n + 1 + ONE)
                            dve.wait_ge(p1_rdy, b * NUB + n + 1 + ONE)
                            dve.wait_ge(p3_rdy, b * NUB + max(n - 1, 0) + ONE)
                            nc.vector.tensor_tensor(rest[n % 2][:], full[n % 2][:], part[n % 4][:, 0, :],
                                                    ALU.subtract).then_inc(r_rdy, 1)
                            dve.wait_ge(p2_rdy, b * NUB + n + 1 + ONE)
                            dve.wait_ge(r_rdy, b * NUB + n + 1 + ONE)
                            nc.vector.tensor_tensor(part[n % 4][:, 2, :], rest[n % 2][:], part[n % 4][:, 1, :],
                                                    ALU.subtract).then_inc(p3_rdy, 1)
                        dve.wait_ge(v_mm, b * CPB + c + 1 + ONE)
                        if c == 0:
                            dve.wait_ge(v_out, b * 32 + ONE)
                        for l in range(2):
                            op = nc.vector.tensor_tensor(
                                vst[:, l, :, 4 * c:4 * c + 4, 0:HD].rearrange("p h t d -> p t h d"),
                                vacc[:].rearrange("p (t h d) -> p t h d", t=4, h=H),
                                vrow[:, l, :].rearrange("p (h d) -> p h d", h=H).unsqueeze(1).to_broadcast([P, 4, H, HD]),
                                ALU.add)
                        op.then_inc(v_rdy, 1)


NPT = 6
KS = NPT * HD
Q_PARTS, K_PARTS = (0, 0, 0, 1, 1, 2), (0, 1, 2, 0, 1, 0)
TAB = P + W - 1
HEADS = 4
STEPS = 2 * KT
WI = CH // (2 * KT)
GUARD_LAG = 8
STORE_LAG = 2
NPROB = 3
QG = HALF // 4
ZEROS = 2 + HEADS + 2
GUARD = KS


def window(a, b, kt):
    q0, q1 = max(P * kt - PAD, a), min(P * kt - PAD + W, b)
    return (q0, q1, q0 - (P * kt - PAD)) if q1 > q0 else None


def half_window(half, kt):
    return window(half * HALF, (half + 1) * HALF, kt)


def segments(a, b, step, kt):
    out = []
    for q0 in range(a, b, step):
        cut = min(max(P * kt, q0), q0 + step)
        out += [(c, d, early) for c, d, early in ((q0, cut, 0), (cut, q0 + step, 1)) if d > c]
    return out


BAND_ITEMS = [("band", w, min(w + WI, W)) for w in range(0, W, WI)]
VALUE_ITEMS = [("centre", w, w + WI) for w in range(PAD, PAD + P, WI)] + [
    ("side", a, min(a + WI, b)) for w0, b in ((0, PAD), (PAD + P, W)) for a in range(w0, b, WI)]
NCENTRE = P // WI


def attention_plan():
    steps = []
    for u in range(HEADS):
        todo = VALUE_ITEMS if u % 2 else BAND_ITEMS
        for s in range(STEPS):
            item = todo[s // 2] if s % 2 and s // 2 < len(todo) else None
            steps.append((u, s // KT, s % KT, item))
    return steps


def attention(nc, t, scratch, outs):
    qs, kh, kl, vs = scratch
    values, band_values, den = outs
    with ExitStack() as ctx:
        sb = lambda n, s, d: ctx.enter_context(nc.sbuf_tensor("att_" + n, s, d))
        sem = Semaphores(nc, ctx, "att")
        ktab = [sb(f"ktab{l}", [KS, TAB], BF16) for l in range(2)]
        vtab = sb("vtab", [P, W, HD], F32)
        with ExitStack() as tctx:
            tb = lambda n, s, d: tctx.enter_context(nc.sbuf_tensor("tab_" + n, s, d))
            tsem = Semaphores(nc, tctx, "tab")
            rk, rkb, msk = tb("rk", [KS, TAB], F32), tb("rkb", [KS, 2], F32), tb("msk", [KS, 3], F32)
            kf, kr = tb("kf", [KS, TAB], F32), tb("kr", [KS, TAB], F32)
            kp = [tb(f"kp{i}", [KS, TAB], BF16) for i in range(3)]
            rv, rvb = tb("rv", [P, W, HD], F32), tb("rvb", [P, 2, HD], F32)
            tin, step = tsem("in"), tsem("step")
            tsem.start()
            with nc.Block() as block:
                @block.sync
                def _(sp):
                    for dst, name in ((rk, "rk"), (rkb, "rkb"), (msk, "msk"), (rv, "rv"), (rvb, "rvb")):
                        sp.dma_start(dst[:], t[name]).then_inc(tin, 16)

                @block.vector
                def _(dve):
                    dve.wait_ge(tin, 80 + ONE)
                    n = 0
                    for l in range(2):
                        dve.wait_ge(step, n + ONE)
                        nc.vector.tensor_scalar(kf[:], rk[:], rkb[:, l:l + 1], None, ALU.subtract).then_inc(step, 1)
                        dve.wait_ge(step, n + 1 + ONE)
                        nc.vector.tensor_copy(kp[0][:], kf[:]).then_inc(step, 1)
                        dve.wait_ge(step, n + 2 + ONE)
                        nc.vector.tensor_tensor(kr[:], kf[:], kp[0][:], ALU.subtract).then_inc(step, 1)
                        dve.wait_ge(step, n + 3 + ONE)
                        nc.vector.tensor_copy(kp[1][:], kr[:]).then_inc(step, 1)
                        dve.wait_ge(step, n + 4 + ONE)
                        nc.vector.tensor_tensor(kp[2][:], kr[:], kp[1][:], ALU.subtract).then_inc(step, 1)
                        dve.wait_ge(step, n + 5 + ONE)
                        nc.vector.tensor_scalar(kf[:], kp[0][:], msk[:, 0:1], None, ALU.mult).then_inc(step, 1)
                        dve.wait_ge(step, n + 6 + ONE)
                        nc.vector.scalar_tensor_tensor(out=kr[:], in0=kp[1][:], scalar=msk[:, 1:2], in1=kf[:],
                                                       op0=ALU.mult, op1=ALU.add).then_inc(step, 1)
                        dve.wait_ge(step, n + 7 + ONE)
                        nc.vector.scalar_tensor_tensor(out=ktab[l][:], in0=kp[2][:], scalar=msk[:, 2:3], in1=kr[:],
                                                       op0=ALU.mult, op1=ALU.add).then_inc(step, 1)
                        n += 8
                    for l, (a, b) in enumerate(((0, PAD), (PAD, W))):
                        nc.vector.tensor_tensor(vtab[:, a:b, :], rv[:, a:b, :],
                                                rvb[:, l:l + 1, :].to_broadcast([P, b - a, HD]),
                                                ALU.subtract).then_inc(step, 1)
                    dve.wait_ge(step, n + 2 + ONE)

        q = [sb(f"q{u}", [P, S], BF16) for u in range(HEADS)]
        k = [[sb(f"k{l}{u}", [P, S], BF16) for u in range(HEADS)] for l in range(2)]
        v = [sb(f"v{i}", [P, 2, KT * VC], F32) for i in range(2)]
        qband = sb("qband", [KS, 2, S + 2 * PAD], BF16)
        band = [sb(f"band{i}", [P, W * 2 * KT], F32) for i in range(2)]
        pwin = [sb(f"pwin{i}", [P, 2, KT, W], F32) for i in range(2)]
        prob = [sb(f"prob{i}", [P, HALF], F32) for i in range(NPROB)]
        kmax = [sb(f"kmax{i}", [P, HALF], F32) for i in range(2)]
        allmax = sb("allmax", [P, HALF], F32)
        ghi = sb("ghi", [1, HALF], BF16)
        glo = sb("glo", [1, HALF], BF16)
        oev = [sb(f"oev{i}", [P, QG], F32) for i in range(2)]
        rel = sb("rel", [HD, 2, S], F32)
        score = [ctx.enter_context(nc.psum_tensor(f"score{i}", [P, HALF], F32)) for i in range(2)]
        again = [ctx.enter_context(nc.psum_tensor(f"again{i}", [P, CH], F32)) for i in range(2)]
        item_acc = ctx.enter_context(nc.psum_tensor("item_acc", [P, CH], F32))
        oacc = ctx.enter_context(nc.psum_tensor("oacc", [P, CH], F32))

        zeroed, ones_set = sem("zeroed"), sem("ones_set")
        stack_in = [sem(f"stack_in{u}") for u in range(HEADS)]
        v_in = [sem(f"v_in{i}") for i in range(2)]
        qband_in = sem("qband_in")
        score_rdy, band_added, exp_done = sem("score_rdy"), sem("band_added"), sem("exp_done")
        window_rdy, pv_done, o_read = sem("window_rdy"), sem("pv_done"), sem("o_read")
        again_rdy, again_added, again_read = sem("again_rdy"), sem("again_added"), sem("again_read")
        item_rdy, item_act, item_dve = sem("item_rdy"), sem("item_act"), sem("item_dve")
        all_max, ghi_rdy, glo_rdy = sem("all_max"), sem("ghi_rdy"), sem("glo_rdy")
        guard_in = [sem(f"guard_in{i}") for i in range(2)]
        o_out = [sem(f"o_out{i}") for i in range(2)]
        rel_out = sem("rel_out")

        plan = attention_plan()
        NS = len(plan)
        NW = sum(half_window(s // KT, s % KT) is not None for s in range(STEPS))
        chunks = [(half, kt, c) for half in range(2) for kt in range(KT) for c in range(2)]
        NC = len(chunks)

        def chunk_window(half, kt, c):
            q0 = half * HALF + c * CH
            return window(q0, q0 + CH, kt)
        NA = sum(chunk_window(*c) is not None for c in chunks)
        NB, NV = len(BAND_ITEMS), len(VALUE_ITEMS)
        NSIDE = NV - NCENTRE
        ITEMS, ITEMS_ACT, ITEMS_DVE = 2 * (NB + NV), 2 * (NB + NCENTRE), 2 * NSIDE

        def items_before(f):
            kinds = [st[3][0] for st in plan[:f] if st[3]]
            side = kinds.count("side")
            return len(kinds), len(kinds) - side, side

        def windows_before(f):
            return sum(half_window(st[1], st[2]) is not None for st in plan[:f])

        def load_stack(sp, u, head_row):
            for stack, src, parts in ((q[u], qs, Q_PARTS), (k[0][u], kh, K_PARTS), (k[1][u], kl, K_PARTS)):
                for r, p in enumerate(parts):
                    sp.dma_start(stack[r * HD:(r + 1) * HD, :], src[p, head_row, :]).then_inc(stack_in[u], 16)

        def load_qband(sp, rows):
            for hd in range(2):
                for r, p in enumerate(Q_PARTS):
                    sp.dma_start(qband[r * HD:(r + 1) * HD, hd, PAD:PAD + S], qs[p, rows[hd], :]).then_inc(qband_in, 16)
        STACK_INC, QBAND_INC = 18 * 16, 12 * 16

        sem.start()
        with nc.Block() as block:
            @block.sync
            def _(sp):
                sp.wait_ge(zeroed, 2 + ONE)
                load_qband(sp, [slice(0, HD), slice(HD, 2 * HD)])
                for u in range(HEADS):
                    load_stack(sp, u, slice(u * HD, (u + 1) * HD))
                    if u < 2:
                        sp.dma_start(v[u][:], vs[u].rearrange("l p c -> p l c")).then_inc(v_in[u], 16)

                def guard(half, seen, nxt):
                    sp.wait_ge(glo_rdy, seen + ONE)
                    cols = slice(half * HALF, (half + 1) * HALF)
                    sp.dma_start(q[nxt][GUARD:GUARD + 1, cols], ghi[:]).then_inc(guard_in[half], 16)
                    sp.dma_start(q[nxt][GUARD + 1:GUARD + 2, cols], glo[:]).then_inc(guard_in[half], 16)
                sp.wait_ge(zeroed, ZEROS + ONE)
                guard(0, 1, 0)
                guard(1, 2, 0)
                sp.wait_ge(item_rdy, NB + ONE)
                load_qband(sp, [slice(2 * HD, 3 * HD), slice(3 * HD, 4 * HD)])

                def store_values(n, head, half):
                    sp.wait_ge(o_read, n + ONE)
                    for g in range(HALF // QG):
                        sp.dma_start(values[bass.ds(head * HD, HD), half * HALF + g * QG:half * HALF + (g + 1) * QG],
                                     oev[half][g * VC:g * VC + HD, :]).then_inc(o_out[half], 16)
                        sp.dma_start(den[bass.ds(head, 1), half * HALF + g * QG:half * HALF + (g + 1) * QG],
                                     oev[half][g * VC + HD:g * VC + HD + 1, :]).then_inc(o_out[half], 16)

                def store_band_values(n, pair):
                    sp.wait_ge(item_dve, n + ONE)
                    sp.dma_start(band_values.rearrange("(h d) s -> d h s", d=HD)[:, bass.ds(pair * 2, 2), :],
                                 rel[:]).then_inc(rel_out, 16)

                with sp.Fori(0, NH // HEADS) as j:
                    for f, (u, half, kt, item) in enumerate(plan):
                        if kt == GUARD_LAG and (u or half):
                            n = 2 * u + half
                            guard(1 - half, j * 2 * HEADS + 2 + n, (n + 1) // 2 % HEADS)
                        if kt == STORE_LAG and (u or half):
                            n = 2 * u + half
                            store_values(j * 2 * HEADS + n, j * HEADS + (n - 1) // 2, 1 - half)
                            if half == 0:
                                sp.wait_ge(pv_done, j * NS + u * STEPS + ONE)
                                load_stack(sp, u - 1, bass.ds(j * HEADS * HD + (u - 1 + HEADS) * HD, HD))
                                sp.dma_start(v[(u - 1) % 2][:], vs.rearrange("h l p c -> p h l c")[
                                    :, bass.ds(j * HEADS + u + 1, 1)]).then_inc(v_in[(u - 1) % 2], 16)
                        if item == BAND_ITEMS[-1]:
                            sp.wait_ge(item_rdy, j * ITEMS + NB + items_before(f + 1)[0] + ONE)
                            rows = j * HEADS * HD + (u + 4) * HD
                            load_qband(sp, [bass.ds(rows, HD), bass.ds(rows + HD, HD)])
                        if item == VALUE_ITEMS[-1]:
                            store_band_values(j * ITEMS_DVE + items_before(f + 1)[2], j * 2 + u // 2)
                    guard(1, j * 2 * HEADS + 2 + 2 * HEADS, 0)
                    store_values(j * 2 * HEADS + 2 * HEADS, j * HEADS + HEADS - 1, 1)
                    sp.wait_ge(pv_done, j * NS + NS + ONE)
                    load_stack(sp, HEADS - 1, bass.ds(j * HEADS * HD + (2 * HEADS - 1) * HD, HD))
                    sp.dma_start(v[(HEADS - 1) % 2][:], vs.rearrange("h l p c -> p h l c")[
                        :, bass.ds(j * HEADS + HEADS + 1, 1)]).then_inc(v_in[(HEADS - 1) % 2], 16)
                store_band_values(NH // HEADS * ITEMS_DVE + NSIDE, NH // 2)
                for i in range(2):
                    sp.wait_ge(o_out[i], 16 * 2 * (HALF // QG) * NH + ONE)
                    sp.wait_ge(v_in[i], 16 * (1 + NH // 2) + ONE)
                    sp.wait_ge(guard_in[i], 32 * (NH + 1) + ONE)
                for u in range(HEADS):
                    sp.wait_ge(stack_in[u], STACK_INC * (1 + NH // HEADS) + ONE)
                sp.wait_ge(qband_in, QBAND_INC * (2 + NH // 2) + ONE)
                sp.wait_ge(rel_out, 16 * (1 + NH // 2) + ONE)

            def scores_of(out, a, b, u, kt, rows):
                for c, d, early in segments(a, b, CH, kt):
                    mm = nc.tensor.matmul(out[:, c - a:d - a], k[early][u][0:rows, kt * P:(kt + 1) * P],
                                          q[u][0:rows, c:d], start=True, stop=True)
                return mm

            def band_products(w0, w1):
                for w in range(w0, w1):
                    mm = nc.tensor.matmul(
                        item_acc[:, (w - w0) * 2 * KT:(w - w0 + 1) * 2 * KT].rearrange("p (h t) -> p h t", h=2),
                        ktab[0 if w < PAD else 1][:, W - 1 - w:W - 1 - w + P],
                        qband[:, :, w:w + (KT - 1) * P + 1:P], start=True, stop=True)
                return mm

            def value_band_products(w0, w1, pair):
                for w in range(w0, w1):
                    mm = nc.tensor.matmul(
                        item_acc[0:HD, (w - w0) * 2 * KT:(w - w0 + 1) * 2 * KT].rearrange("p (h t) -> p h t", h=2),
                        vtab[:, w, :], pwin[pair][:, :, :, w], start=True, stop=True)
                return mm

            @block.tensor
            def _(pe):
                pe.wait_ge(zeroed, ZEROS + ONE)
                pe.wait_ge(ones_set, 4 * HEADS + ONE)
                pe.wait_ge(qband_in, QBAND_INC + ONE)
                for n, (_, w0, w1) in enumerate(BAND_ITEMS):
                    if n:
                        pe.wait_ge(item_act, n + ONE)
                    band_products(w0, w1).then_inc(item_rdy, 1)
                pe.wait_ge(stack_in[0], STACK_INC + ONE)
                for n, (half, kt, c) in enumerate(chunks):
                    if n >= 2:
                        pe.wait_ge(again_read, n - 1 + ONE)
                    a = half * HALF + c * CH
                    scores_of(again[c], a, a + CH, 0, kt, KS).then_inc(again_rdy, 1)

                def scores(f, j=None):
                    u, half, kt = plan[f % NS][:3]
                    if kt == 0:
                        n = 32 * (f // STEPS + 1)
                        pe.wait_ge(guard_in[half], (n if j is None else j * 32 * HEADS + n) + ONE)
                    if j is not None:
                        pe.wait_ge(exp_done, j * NS + max(f - 1, 0) + ONE)
                    scores_of(score[f % 2], half * HALF, (half + 1) * HALF, u, kt, P).then_inc(score_rdy, 1)
                scores(0)
                with pe.Fori(0, NH // HEADS) as j:
                    last = ("dve", 0)

                    def maximum_chunk(f, c):
                        u, half, kt = plan[f][:3]
                        nxt = (u + 1) % HEADS
                        if half == 0 and kt == 0 and c == 0:
                            pe.wait_ge(stack_in[nxt], (j * STACK_INC + (STACK_INC * 2 if nxt == 0 else STACK_INC)) + ONE)
                        pe.wait_ge(again_read, j * 2 * NS + NC + 2 * f + c - 1 + ONE)
                        a = half * HALF + c * CH
                        scores_of(again[c], a, a + CH, nxt, kt, KS).then_inc(again_rdy, 1)

                    def value_products(f):
                        u, half, kt = plan[f][:3]
                        if kt == 0:
                            pe.wait_ge(o_read, j * 2 * HEADS + 2 * u + half + ONE)
                            pe.wait_ge(v_in[u % 2], j * 32 + 16 * (u // 2) + 16 + ONE)
                        pe.wait_ge(exp_done, j * NS + f + 1 + ONE)
                        for a, b, early in segments(half * HALF, (half + 1) * HALF, QG, kt):
                            a, b = a - half * HALF, b - half * HALF
                            g = a // QG
                            mm = nc.tensor.matmul(oacc[g * VC:(g + 1) * VC, a - g * QG:b - g * QG],
                                                  v[u % 2][:, early, kt * VC:(kt + 1) * VC], prob[f % NPROB][:, a:b],
                                                  start=(kt == 0), stop=(kt == KT - 1), skip_group_check=True)
                        mm.then_inc(pv_done, 1)

                    def item_products(f):
                        u, _, _, item = plan[f]
                        kind, w0, w1 = item
                        n, na, nd = items_before(f)
                        if n and plan[f - 2][3] and plan[f - 2][3][0] == "side":
                            pe.wait_ge(item_dve, j * ITEMS_DVE + nd + ONE)
                        elif n == 0:
                            pe.wait_ge(item_act, j * ITEMS_ACT + NB + ONE)
                            pe.wait_ge(item_dve, j * ITEMS_DVE + ONE)
                        else:
                            pe.wait_ge(item_act, j * ITEMS_ACT + NB + na + ONE)
                            pe.wait_ge(item_dve, j * ITEMS_DVE + nd + ONE)
                        if kind == "band":
                            if w0 == 0:
                                pe.wait_ge(qband_in, j * 2 * QBAND_INC + QBAND_INC * (2 + u // 2) + ONE)
                            mm = band_products(w0, w1)
                        else:
                            if item == VALUE_ITEMS[0]:
                                pe.wait_ge(window_rdy, j * HEADS * NW + (u // 2) * 2 * NW + ONE)
                            mm = value_band_products(w0, w1, (u // 2 + 1) % 2)
                        mm.then_inc(item_rdy, 1)

                    for f, st in enumerate(plan):
                        scores(f + 1, j)
                        maximum_chunk(f, 0)
                        if f:
                            value_products(f - 1)
                        maximum_chunk(f, 1)
                        if st[3]:
                            item_products(f)
                    value_products(NS - 1)
                passes = NH // HEADS
                pe.wait_ge(window_rdy, passes * HEADS * NW + ONE)
                pe.wait_ge(item_dve, passes * ITEMS_DVE + ONE)
                for n, (kind, w0, w1) in enumerate(VALUE_ITEMS):
                    if n <= NCENTRE:
                        pe.wait_ge(item_act, passes * ITEMS_ACT + NB + n + ONE)
                    else:
                        pe.wait_ge(item_dve, passes * ITEMS_DVE + n - NCENTRE + ONE)
                    value_band_products(w0, w1, 1).then_inc(item_rdy, 1)

            @block.scalar
            def _(act):
                for n, (_, w0, w1) in enumerate(BAND_ITEMS):
                    act.wait_ge(item_rdy, n + 1 + ONE)
                    nc.scalar.activation(band[0][:, w0 * 2 * KT:w1 * 2 * KT], item_acc[:, 0:(w1 - w0) * 2 * KT],
                                         ACT.Copy).then_inc(item_act, 1)

                def guard_high(n, j=None):
                    act.wait_ge(all_max, (n + 1 if j is None else j * 2 * HEADS + n + 1) + ONE)
                    if j is not None:
                        act.wait_ge(guard_in[(n - 1) % 2], j * 32 * HEADS + 32 * ((n - 1) // 2 + 1) + ONE)
                    elif n:
                        act.wait_ge(guard_in[0], 32 + ONE)
                    nc.scalar.activation(ghi[:], allmax[0:1, :], ACT.Copy, scale=-1.0).then_inc(ghi_rdy, 1)
                guard_high(0)
                guard_high(1)

                def copy_centre(w0, w1, products):
                    act.wait_ge(item_rdy, products + ONE)
                    nc.scalar.activation(
                        rel[:].rearrange("p h (t q) -> p h t q", t=KT)[:, :, :, w0 - PAD:w1 - PAD],
                        item_acc[0:HD, :].rearrange("p (w h t) -> p h t w", h=2, t=KT), ACT.Copy).then_inc(item_act, 1)

                with act.Fori(0, NH // HEADS) as j:
                    nwin = 0

                    def copy_window(f):
                        u, half, kt, _ = plan[f]
                        win = half_window(half, kt)
                        if win is None:
                            return
                        q0, q1, w0 = win
                        if u % 2 == 0 and half == 0 and kt == 0:
                            act.wait_ge(item_rdy, j * ITEMS + NB + items_before(f)[0] + ONE)
                        act.wait_ge(exp_done, j * NS + f + 1 + ONE)
                        nc.scalar.activation(pwin[u // 2][:, u % 2, kt, w0:w0 + q1 - q0],
                                             prob[f % NPROB][:, q0 - half * HALF:q1 - half * HALF],
                                             ACT.Copy).then_inc(window_rdy, 1)

                    def copy_item(f):
                        u, _, _, item = plan[f]
                        if item is None or item[0] == "side":
                            return
                        kind, w0, w1 = item
                        n = items_before(f)[0]
                        if kind == "band":
                            act.wait_ge(item_rdy, j * ITEMS + NB + n + 1 + ONE)
                            nc.scalar.activation(band[(u // 2 + 1) % 2][:, w0 * 2 * KT:w1 * 2 * KT],
                                                 item_acc[:, 0:(w1 - w0) * 2 * KT], ACT.Copy).then_inc(item_act, 1)
                        else:
                            if item == VALUE_ITEMS[0]:
                                act.wait_ge(rel_out, j * 32 + 16 * (u // 2) + ONE)
                            copy_centre(w0, w1, j * ITEMS + NB + n + 1)

                    def evacuate(n):
                        act.wait_ge(pv_done, j * NS + (n + 1) * KT + ONE)
                        act.wait_ge(o_out[n % 2], (j * HEADS + n // 2) * (16 * 2 * (HALF // QG)) + ONE)
                        nc.scalar.activation(oev[n % 2][:], oacc[:, 0:QG], ACT.Copy).then_inc(o_read, 1)

                    for f, (u, half, kt, item) in enumerate(plan):
                        if half_window(half, kt) is not None:
                            nwin += 1
                            act.wait_ge(band_added, j * HEADS * NW + nwin + ONE)
                        else:
                            act.wait_ge(score_rdy, j * NS + f + 1 + ONE)
                        act.wait_ge(pv_done, j * NS + max(f - NPROB + 1, 0) + ONE)
                        act.wait_ge(window_rdy, j * HEADS * NW + windows_before(max(f - NPROB + 1, 0)) + ONE)
                        nc.scalar.activation(prob[f % NPROB][:], score[f % 2][:], ACT.Exp, scale=0.25).then_inc(exp_done, 1)
                        n = 2 * u + half
                        if n and kt == 0:
                            evacuate(n - 1)
                        if f:
                            copy_window(f - 1)
                            copy_item(f - 1)
                        if n and kt == GUARD_LAG:
                            guard_high(1 + n, j)
                    copy_window(NS - 1)
                    guard_high(2 * HEADS + 1, j)
                    evacuate(2 * HEADS - 1)
                passes = NH // HEADS
                act.wait_ge(rel_out, 32 * passes + ONE)
                for n, (_, w0, w1) in enumerate(VALUE_ITEMS[:NCENTRE]):
                    copy_centre(w0, w1, passes * ITEMS + NB + n + 1)

            @block.gpsimd
            def _(pool):
                nc.gpsimd.memset(qband[:, :, 0:PAD], 0.0).then_inc(zeroed, 1)
                nc.gpsimd.memset(qband[:, :, PAD + S:S + 2 * PAD], 0.0).then_inc(zeroed, 1)
                for u in range(HEADS):
                    nc.gpsimd.memset(q[u][KS:P, :], 0.0).then_inc(zeroed, 1)
                for i in range(2):
                    pool.wait_ge(zeroed, HEADS + 2 + i + ONE)
                    nc.gpsimd.memset(pwin[i][:], 0.0).then_inc(zeroed, 1)

                def all_reduce(n, j=None):
                    if j is None:
                        pool.wait_ge(zeroed, ZEROS + ONE)
                        pool.wait_ge(again_read, (n + 1) * NC // 2 + ONE)
                        if n:
                            pool.wait_ge(glo_rdy, n + ONE)
                    else:
                        maxes_in = pool.to_reg(j * 2 * NS + (n + 1) * (NC // 2) + ONE)
                        last_read = pool.to_reg(j * 2 * HEADS + n + ONE)
                        pool.wait_ge(zeroed, ZEROS + ONE)
                        pool.wait_ge(again_read, maxes_in)
                        pool.wait_ge(glo_rdy, last_read)
                    nc.gpsimd.partition_all_reduce(allmax[:], kmax[n % 2][:], P, RMAX).then_inc(all_max, 1)
                all_reduce(0)
                all_reduce(1)
                with pool.Fori(0, NH // HEADS) as j:
                    for n in range(2 * HEADS):
                        all_reduce(2 + n, j)

            @block.vector
            def _(dve):
                def band_of(pair, hd, kt, w0, w1):
                    return band[pair][:].rearrange("p (w h t) -> p w h t", h=2, t=KT)[:, w0:w1, hd, kt]

                def add_chunk_band(chunk, pair, hd, products):
                    half, kt, c = chunk
                    dve.wait_ge(again_rdy, products + ONE)
                    win = chunk_window(half, kt, c)
                    if win is not None:
                        q0, q1, w0 = win
                        a = half * HALF + c * CH
                        o = again[c][:, q0 - a:q1 - a]
                        nc.vector.tensor_tensor(o, o, band_of(pair, hd, kt, w0, w0 + q1 - q0),
                                                ALU.add).then_inc(again_added, 1)

                def chunk_maximum(chunk, added, before, reduced=None):
                    half, kt, c = chunk
                    if added is not None:
                        dve.wait_ge(again_added, added + ONE)
                    here = kmax[half][:, c * CH:(c + 1) * CH]
                    if kt == 0:
                        if reduced is not None:
                            dve.wait_ge(all_max, reduced + ONE)
                        nc.vector.tensor_copy(here, again[c][:]).then_inc(again_read, 1)
                    else:
                        dve.wait_ge(again_read, before)
                        nc.vector.tensor_tensor(here, here, again[c][:], ALU.max).then_inc(again_read, 1)

                def added_by(i):
                    if chunk_window(*chunks[i]) is None:
                        return None
                    return sum(chunk_window(*c) is not None for c in chunks[:i + 1])

                def guard_low(n, j=None):
                    dve.wait_ge(ghi_rdy, (n + 1 if j is None else j * 2 * HEADS + n + 1) + ONE)
                    if j is not None:
                        dve.wait_ge(guard_in[(n - 1) % 2], j * 32 * HEADS + 32 * ((n - 1) // 2 + 1) + ONE)
                    elif n:
                        dve.wait_ge(guard_in[0], 32 + ONE)
                    nc.vector.scalar_tensor_tensor(out=glo[:], in0=allmax[0:1, :], scalar=-1.0, in1=ghi[:],
                                                   op0=ALU.mult, op1=ALU.subtract).then_inc(glo_rdy, 1)

                def add_side(w0, w1, products, copied, mine):
                    dve.wait_ge(item_rdy, products + ONE)
                    dve.wait_ge(item_act, copied + ONE)
                    dve.wait_ge(item_dve, mine + ONE)
                    view = rel[:].rearrange("p h (t q) -> p h t q", t=KT)
                    new = item_acc[0:HD, 0:(w1 - w0) * 2 * KT].rearrange("p (w h t) -> p h t w", h=2, t=KT)
                    if w0 < PAD:
                        old, new = view[:, :, 0:KT - 1, P - PAD + w0:P - PAD + w1], new[:, :, 1:KT, :]
                    else:
                        old, new = view[:, :, 1:KT, w0 - PAD - P:w1 - PAD - P], new[:, :, 0:KT - 1, :]
                    for hd in range(2):
                        op = nc.vector.tensor_tensor(old[:, hd], old[:, hd], new[:, hd], ALU.add)
                    op.then_inc(item_dve, 1)

                operands = [k[l][u] for l in range(2) for u in range(HEADS)]
                for o in operands:
                    nc.vector.memset(o[KS:P, :], 0.0).then_inc(ones_set, 1)
                for n, o in enumerate(operands):
                    dve.wait_ge(ones_set, n + 1 + ONE)
                    nc.vector.memset(o[GUARD:GUARD + 2, :], 1.0).then_inc(ones_set, 1)
                dve.wait_ge(item_act, NB + ONE)
                for i, chunk in enumerate(chunks):
                    add_chunk_band(chunk, 0, 0, i + 1)
                    chunk_maximum(chunk, added_by(i), i - 1)
                    if i == NC // 2 + 24:
                        guard_low(0)
                guard_low(1)

                def add_band(f, j=None):
                    u, half, kt, _ = plan[f % NS]
                    win = half_window(half, kt)
                    if win is None:
                        return
                    q0, q1, w0 = win
                    dve.wait_ge(score_rdy, (f + 1 if j is None else j * NS + f + 1) + ONE)
                    o = score[f % 2][:, q0 - half * HALF:q1 - half * HALF]
                    nc.vector.tensor_tensor(o, o, band_of(u // 2, u % 2, kt, w0, w0 + q1 - q0),
                                            ALU.add).then_inc(band_added, 1)
                add_band(0)
                with dve.Fori(0, NH // HEADS) as j:
                    for f, (u, half, kt, item) in enumerate(plan):
                        nxt = u + 1
                        for c in range(2):
                            i = 2 * (f % STEPS) + c
                            if i == 0 and nxt % 2 == 0:
                                dve.wait_ge(item_act, j * ITEMS_ACT + NB + items_before(f)[1] + ONE)
                            done = j * 2 * NS + NC + 2 * f + c
                            add_chunk_band(chunks[i], nxt // 2 % 2, nxt % 2, done + 1)
                            if c == 0:
                                add_band(f + 1, j)
                            added = added_by(i)
                            chunk_maximum(chunks[i], None if added is None else j * HEADS * NA + nxt * NA + added,
                                          done - 1, j * 2 * HEADS + 2 * u + half + 1)
                        if f and plan[f - 1][3] and plan[f - 1][3][0] == "side":
                            _, w0, w1 = plan[f - 1][3]
                            n, na, nd = items_before(f - 1)
                            add_side(w0, w1, j * ITEMS + NB + n + 1, j * ITEMS_ACT + NB + na, j * ITEMS_DVE + nd)
                        n = 2 * u + half
                        if n and kt == GUARD_LAG:
                            guard_low(1 + n, j)
                    guard_low(2 * HEADS + 1, j)
                passes = NH // HEADS
                for n, (_, w0, w1) in enumerate(VALUE_ITEMS[NCENTRE:]):
                    add_side(w0, w1, passes * ITEMS + NB + NCENTRE + n + 1, passes * ITEMS_ACT + NB + NCENTRE,
                             passes * ITEMS_DVE + n)


class Names:

    def __init__(self, nc, ctx, stage):
        self.nc, self.ctx, self.stage = nc, ctx, stage
        self.sem = Semaphores(nc, ctx, stage)

    def sb(self, name, shape, dtype=F32):
        return self.ctx.enter_context(self.nc.sbuf_tensor(f"{self.stage}_{name}", shape, dtype))

    def ps(self, name, shape):
        return self.ctx.enter_context(self.nc.psum_tensor(f"{self.stage}_{name}", shape, F32))


def project_attention(nc, t, outs, x):
    values, band_values, den = outs
    with ExitStack() as ctx:
        m = Names(nc, ctx, "wo")
        w = m.sb("w", [P, EK2, E])
        bo = m.sb("bo", [P, EK2])
        xin = [m.sb(f"xin{i}", [P, EK2, CH]) for i in range(2)]
        parts = [m.sb(f"parts{i}", [P, EK2, 2, CH]) for i in range(2)]
        dn = [m.sb(f"den{i}", [P, EK2, CH]) for i in range(2)]
        total, recip, att = (m.sb(n, [P, EK2, CH]) for n in ("total", "recip", "att"))
        out = m.ps("out", [P, EK2, CH])
        w_in, in0, in1 = m.sem("w_in"), m.sem("in0"), m.sem("in1")
        chunk_in = [in0, in1]
        summed, recip_rdy, att_rdy, out_rdy, x_rdy = (m.sem(n) for n in ("summed", "recip", "att", "out", "x"))
        ND = 2 * (2 + 8) + 1
        m.sem.start()
        with nc.Block() as block:
            @block.sync
            def _(sp):
                sp.dma_start(w[:], t["wo"].rearrange("(k p) n -> p k n", p=P)).then_inc(w_in, 16)
                sp.dma_start(bo[:], t["bo"]).then_inc(w_in, 16)
                with sp.Fori(0, B) as b:
                    for c in range(CPB):
                        sp.wait_ge(x_rdy, b * CPB + max(c - 1, 0) + ONE)
                        cols = slice(c * CH, (c + 1) * CH)
                        s = chunk_in[c % 2]
                        sp.dma_start(xin[c % 2][:], t["xt"].rearrange("(k p) n -> p k n", p=P)[
                            :, :, bass.ds(b * S + c * CH, CH)]).then_inc(s, 16)
                        for e in range(EK2):
                            rows = bass.ds(b * E + e * P, P)
                            sp.dma_start(parts[c % 2][:, e, 0, :], values[rows, cols]).then_inc(s, 16)
                            sp.dma_start(parts[c % 2][:, e, 1, :],
                                         band_values[bass.ds(b * E + e * P + 2 * HD, P), cols]).then_inc(s, 16)
                            for h in range(8):
                                sp.dma_start(dn[c % 2][h * HD:(h + 1) * HD, e, :],
                                             den[bass.ds(b * H + e * 8 + h, 1), cols].to_broadcast([HD, CH])).then_inc(s, 16)

            @block.vector
            def _(dve):
                dve.wait_ge(w_in, 32 + ONE)
                with dve.Fori(0, B) as b:
                    for c in range(CPB):
                        n = b * CPB + c
                        dve.wait_ge(chunk_in[c % 2], b * (CPB // 2) * 16 * ND + 16 * ND * (c // 2 + 1) + ONE)
                        nc.vector.tensor_tensor(total[:], parts[c % 2][:, :, 0, :], parts[c % 2][:, :, 1, :],
                                                ALU.add).then_inc(summed, 1)
                        nc.vector.reciprocal(recip[:], dn[c % 2][:]).then_inc(recip_rdy, 1)
                        dve.wait_ge(summed, n + 1 + ONE)
                        dve.wait_ge(recip_rdy, n + 1 + ONE)
                        dve.wait_ge(out_rdy, n + ONE)
                        nc.vector.tensor_tensor(att[:], total[:], recip[:], ALU.mult).then_inc(att_rdy, 1)
                        dve.wait_ge(out_rdy, n + 1 + ONE)
                        for e in range(EK2):
                            op = nc.vector.scalar_tensor_tensor(
                                out=x[:, e, bass.ds(b * S + c * CH, CH)], in0=out[:, e, :], scalar=bo[:, e:e + 1],
                                in1=xin[c % 2][:, e, :], op0=ALU.add, op1=ALU.add)
                        op.then_inc(x_rdy, 1)

            @block.tensor
            def _(pe):
                pe.wait_ge(w_in, 32 + ONE)
                with pe.Fori(0, NCH) as n:
                    pe.wait_ge(att_rdy, n + 1 + ONE)
                    pe.wait_ge(x_rdy, n + ONE)
                    for e in range(EK2):
                        for k in range(EK2):
                            mm = nc.tensor.matmul(out[:, e, :], w[:, k, e * P:(e + 1) * P], att[:, k, :],
                                                  start=(k == 0), stop=(k == 1))
                    mm.then_inc(out_rdy, 1)


def layer_norm(nc, stage, x, out=None):
    with ExitStack() as ctx:
        m = Names(nc, ctx, stage)
        mean_of = m.sb("mean_of", [P, P])
        eps = m.sb("eps", [P, 1])
        dev = [m.sb(f"dev{i}", [P, EK2, CH]) for i in range(2)]
        sq = [m.sb(f"sq{i}", [P, EK2, CH]) for i in range(2)]
        sd = [m.sb(f"sd{i}", [P, CH]) for i in range(2)]
        rs = [m.sb(f"rs{i}", [P, CH]) for i in range(2)]
        mean = [m.ps(f"mean{i}", [P, CH]) for i in range(2)]
        var = [m.ps(f"var{i}", [P, CH]) for i in range(2)]
        ready, mean_rdy, dev_rdy, sq_rdy, var_rdy, sd_rdy, rs_rdy, x_rdy, x_out = (
            m.sem(n) for n in ("ready", "mean", "dev", "sq", "var", "sd", "rs", "x", "out"))
        m.sem.start()
        with nc.Block() as block:
            def chunk(i, c):
                return x[:, :, bass.ds(i * 2 * CH + c * CH, CH)]

            @block.tensor
            def _(pe):
                pe.wait_ge(ready, 2 + ONE)
                with pe.Fori(0, NCH // 2) as i:
                    for c in range(2):
                        pe.wait_ge(dev_rdy, i * 2 + ONE)
                        for k in range(EK2):
                            mm = nc.tensor.matmul(mean[c][:], mean_of[:], x[:, k, bass.ds(i * 2 * CH + c * CH, CH)],
                                                  start=(k == 0), stop=(k == 1))
                        mm.then_inc(mean_rdy, 1)
                    for c in range(2):
                        pe.wait_ge(sq_rdy, i * 2 + c + 1 + ONE)
                        pe.wait_ge(sd_rdy, i * 2 + ONE)
                        for k in range(EK2):
                            mm = nc.tensor.matmul(var[c][:], mean_of[:], sq[c][:, k, :], start=(k == 0), stop=(k == 1))
                        mm.then_inc(var_rdy, 1)

            @block.vector
            def _(dve):
                nc.vector.memset(mean_of[:], 1.0 / E).then_inc(ready, 1)
                nc.vector.memset(eps[:], EPS).then_inc(ready, 1)
                with dve.Fori(0, NCH // 2) as i:
                    for c in range(2):
                        dve.wait_ge(mean_rdy, i * 2 + c + 1 + ONE)
                        dve.wait_ge(x_rdy, i * 2 + ONE)
                        dve.wait_ge(sq_rdy, i * 2 + ONE)
                        nc.vector.tensor_tensor(dev[c][:], chunk(i, c), mean[c][:].unsqueeze(1).to_broadcast([P, EK2, CH]),
                                                ALU.subtract).then_inc(dev_rdy, 1)
                    for c in range(2):
                        dve.wait_ge(sd_rdy, i * 2 + c + 1 + ONE)
                        nc.vector.reciprocal(rs[c][:], sd[c][:]).then_inc(rs_rdy, 1)
                        dve.wait_ge(rs_rdy, i * 2 + c + 1 + ONE)
                        nc.vector.tensor_tensor(chunk(i, c), dev[c][:], rs[c][:].unsqueeze(1).to_broadcast([P, EK2, CH]),
                                                ALU.mult).then_inc(x_rdy, 1)

            @block.scalar
            def _(act):
                act.wait_ge(ready, 2 + ONE)
                with act.Fori(0, NCH // 2) as i:
                    for c in range(2):
                        act.wait_ge(dev_rdy, i * 2 + c + 1 + ONE)
                        act.wait_ge(var_rdy, i * 2 + ONE)
                        nc.scalar.activation(sq[c][:], dev[c][:], ACT.Square).then_inc(sq_rdy, 1)
                    for c in range(2):
                        act.wait_ge(var_rdy, i * 2 + c + 1 + ONE)
                        act.wait_ge(rs_rdy, i * 2 + ONE)
                        nc.scalar.activation(sd[c][:], var[c][:], ACT.Sqrt, bias=eps[:]).then_inc(sd_rdy, 1)

            if out is not None:
                @block.sync
                def _(sp):
                    with sp.Fori(0, NCH) as n:
                        sp.wait_ge(x_rdy, n + 1 + ONE)
                        sp.dma_start(out.rearrange("(k p) n -> p k n", p=P)[:, :, bass.ds(n * CH, CH)],
                                     x[:, :, bass.ds(n * CH, CH)]).then_inc(x_out, 16)
                    sp.wait_ge(x_out, 16 * NCH + ONE)


NEXP = 8
TILES = T // P


def route(nc, stage, t, x, weight, normalise):
    with ExitStack() as ctx:
        m = Names(nc, ctx, stage)
        rw = m.sb("rw", [P, EK2, NEXP])
        rb = m.sb("rb", [P, NEXP])
        iota = m.sb("iota", [P, NEXP])
        xs = [m.sb(f"xs{i}", [P, EK2, CH]) for i in range(2)]
        lg = [m.ps(f"lg{i}", [P, 4, NEXP]) for i in range(2)]
        names = ("logit", "shift", "ex", "prob", "mask1", "mask", "kept")
        logit, shift, ex, prob, mask1, mask, kept = (m.sb(n, [P, 4, NEXP]) for n in names)
        mx, tot, inv, tot2, inv2 = (m.sb(n, [P, 4]) for n in ("mx", "tot", "inv", "tot2", "inv2"))
        top = m.sb("top", [P, 4, 8])
        where = m.sb("where", [P, 4, 8], mybir.dt.uint32)
        wheref = m.sb("wheref", [P, 4, 8])
        w_in, xs_rdy, lg_rdy, ex_rdy, d = (m.sem(n) for n in ("w_in", "xs", "lg", "ex", "d"))
        m.sem.start()
        with nc.Block() as block:
            @block.sync
            def _(sp):
                sp.dma_start(rw[:], t[f"{stage}_w"].rearrange("(k p) n -> p k n", p=P)).then_inc(w_in, 16)
                sp.dma_start(rb[:], t[f"{stage}_b"]).then_inc(w_in, 16)
                sp.dma_start(iota[:], t["iota"]).then_inc(w_in, 16)

            ND = 5 + 2 * 4 + 5 + (4 if normalise else 1)

            @block.tensor
            def _(pe):
                pe.wait_ge(w_in, 48 + ONE)
                with pe.Fori(0, NCH // 2) as i:
                    for c in range(2):
                        pe.wait_ge(xs_rdy, i * 2 + c + 1 + ONE)
                        pe.wait_ge(d, i * 2 * ND + ONE)
                        for a in range(4):
                            for k in range(EK2):
                                mm = nc.tensor.matmul(lg[c][:, a, :], xs[c][:, k, a * P:(a + 1) * P], rw[:, k, :],
                                                      start=(k == 0), stop=(k == 1))
                        mm.then_inc(lg_rdy, 1)

            @block.scalar
            def _(act):
                with act.Fori(0, NCH // 2) as i:
                    for c in range(2):
                        act.wait_ge(lg_rdy, i * 2 + ONE)
                        nc.scalar.activation(xs[c][:], x[:, :, bass.ds(i * 2 * CH + c * CH, CH)], ACT.Copy).then_inc(xs_rdy, 1)
                    for c in range(2):
                        act.wait_ge(d, i * 2 * ND + c * ND + 3 + ONE)
                        nc.scalar.activation(ex[:], shift[:], ACT.Exp).then_inc(ex_rdy, 1)

            @block.vector
            def _(dve):
                dve.wait_ge(w_in, 48 + ONE)
                wide = [P, 4, NEXP]
                with dve.Fori(0, NCH // 2) as i:
                    for c in range(2):
                        n = c * ND

                        def then(op, last=True, constants=False):
                            nonlocal n
                            op.then_inc(d, 1)
                            n += 1
                            if last:
                                before = dve.to_reg(i * 2 * ND + n + ONE)
                                if constants:
                                    dve.wait_ge(w_in, 48 + ONE)
                                dve.wait_ge(d, before)
                        dve.wait_ge(lg_rdy, i * 2 + c + 1 + ONE)
                        then(nc.vector.tensor_tensor(logit[:], lg[c][:], rb[:].unsqueeze(1).to_broadcast(wide), ALU.add))
                        then(nc.vector.tensor_reduce(mx[:], logit[:], AX.X, ALU.max))
                        then(nc.vector.tensor_tensor(shift[:], logit[:], mx[:].unsqueeze(2).to_broadcast(wide), ALU.subtract))
                        dve.wait_ge(ex_rdy, i * 2 + c + 1 + ONE)
                        then(nc.vector.tensor_reduce(tot[:], ex[:], AX.X, ALU.add))
                        then(nc.vector.reciprocal(inv[:], tot[:]))
                        then(nc.vector.tensor_tensor(prob[:], ex[:], inv[:].unsqueeze(2).to_broadcast(wide), ALU.mult), constants=True)
                        for a in range(4):
                            then(nc.vector.max(top[:, a, :], prob[:, a, :]), a == 3, a == 3)
                        for a in range(4):
                            then(nc.vector.max_index(where[:, a, :], top[:, a, :], prob[:, a, :]), a == 3)
                        then(nc.vector.tensor_copy(wheref[:], where[:]))
                        it = iota[:].unsqueeze(1).to_broadcast(wide)
                        then(nc.vector.tensor_tensor(mask1[:], it, wheref[:, :, 0:1].to_broadcast(wide), ALU.is_equal))
                        then(nc.vector.tensor_tensor(mask[:], it, wheref[:, :, 1:2].to_broadcast(wide), ALU.is_equal))
                        then(nc.vector.tensor_tensor(mask[:], mask1[:], mask[:], ALU.add))
                        dst = weight[:, bass.ds(i * 8 + c * 4, 4), 0:NEXP]
                        if not normalise:
                            then(nc.vector.tensor_tensor(dst, prob[:], mask[:], ALU.mult))
                        else:
                            then(nc.vector.tensor_tensor(kept[:], prob[:], mask[:], ALU.mult))
                            then(nc.vector.tensor_reduce(tot2[:], kept[:], AX.X, ALU.add))
                            then(nc.vector.reciprocal(inv2[:], tot2[:]))
                            then(nc.vector.tensor_tensor(dst, kept[:], inv2[:].unsqueeze(2).to_broadcast(wide), ALU.mult))
                        assert n == (c + 1) * ND, (n, ND)


def load_split(nc, stage, jobs):
    with ExitStack() as ctx:
        m = Names(nc, ctx, stage)
        size = max(int(np.prod(hi.shape[1:])) for _, hi, _ in jobs)
        raw = [m.sb(f"raw{i}", [P, size]) for i in range(2)]
        ins = [m.sem(f"in{i}") for i in range(2)]
        hi_rdy, lo_rdy = m.sem("hi"), m.sem("lo")

        def view(n):
            hi = jobs[n][1]
            return raw[n % 2][:, 0:int(np.prod(hi.shape[1:]))].rearrange("p (k n) -> p k n", k=hi.shape[1])
        m.sem.start()
        with nc.Block() as block:
            @block.sync
            def _(sp):
                for n, (src, _, _) in enumerate(jobs):
                    if n >= 2:
                        sp.wait_ge(lo_rdy, n - 1 + ONE)
                    sp.dma_start(view(n), src).then_inc(ins[n % 2], 16)

            @block.scalar
            def _(act):
                for n, (_, hi, _) in enumerate(jobs):
                    act.wait_ge(ins[n % 2], 16 * (n // 2 + 1) + ONE)
                    nc.scalar.activation(hi[:], view(n), ACT.Copy).then_inc(hi_rdy, 1)

            @block.vector
            def _(dve):
                for n, (_, hi, lo) in enumerate(jobs):
                    dve.wait_ge(hi_rdy, n + 1 + ONE)
                    nc.vector.tensor_tensor(lo[:], view(n), hi[:].bitcast(F32), ALU.subtract).then_inc(lo_rdy, 1)


def product3(nc, out, left, right, start, stop):
    (lh, ll), (rh, rl) = left, right
    nc.tensor.matmul(out, ll, rh, start=start, stop=False)
    nc.tensor.matmul(out, lh, rl, start=False, stop=False)
    return nc.tensor.matmul(out, lh, rh, start=False, stop=stop)


RANK, FF = 64, 1024
ER = NEXP * RANK // P
FT = FF // P


def low_rank_ffn(nc, t, x, weight):
    with ExitStack() as ctx:
        m = Names(nc, ctx, "ffn0")
        pair = lambda n, s: (m.sb(n + "_hi", s, F32R), m.sb(n + "_lo", s, F32R))
        w1, w2, w3 = pair("w1", [P, EK2, NEXP * RANK]), pair("w2", [P, ER, FF]), pair("w3", [P, FT, E])
        load_split(nc, "ffn0w", [(t["w1"].rearrange("(k p) n -> p k n", p=P), *w1),
                                 (t["w2"].rearrange("(k p) n -> p k n", p=P), *w2),
                                 (t["w3"].rearrange("(k p) n -> p k n", p=P), *w3)])
        b3 = m.sb("b3", [P, EK2])
        ident = m.sb("ident", [P, P])
        rep = m.sb("rep", [P, 4, NEXP, RANK])
        wb = m.sb("wb", [P, ER, CH])
        xs = pair("xs", [P, EK2, CH])
        tt = m.sb("tt", [P, ER, CH])
        ts = pair("ts", [P, ER, CH])
        hf = [m.sb(f"hf{i}", [P, CH]) for i in range(2)]
        hs = pair("hs", [P, FT, CH])
        low = [m.ps(f"low{i}", [P, CH]) for i in range(2)]
        wacc = [m.ps(f"wacc{i}", [P, CH]) for i in range(2)]
        mid = [m.ps(f"mid{i}", [P, CH]) for i in range(2)]
        rep_rdy, wb_mm, wb_rdy = m.sem("rep"), m.sem("wb_mm"), m.sem("wb")
        out = m.ps("out", [P, EK2, CH])
        b_in, xh, xl, low_mm, tt_rdy, th, tl = (
            m.sem(n) for n in ("b_in", "xh", "xl", "low_mm", "tt", "th", "tl"))
        mid_mm, hf_rdy, hh, hl, out_mm, x_rdy = (m.sem(n) for n in ("mid_mm", "hf", "hh", "hl", "out_mm", "x"))
        m.sem.start()
        with nc.Block() as block:
            @block.sync
            def _(sp):
                sp.dma_start(b3[:], t["b3"]).then_inc(b_in, 16)
                sp.dma_start(ident[:], t["ident"]).then_inc(b_in, 16)

            @block.tensor
            def _(pe):
                pe.wait_ge(b_in, 32 + ONE)
                with pe.Fori(0, NCH) as n:
                    pe.wait_ge(rep_rdy, n + 1 + ONE)
                    for r in range(ER):
                        pe.wait_ge(wb_rdy, n * ER + max(r - 1, 0) + ONE)
                        for a in range(4):
                            mm = nc.tensor.matmul(wacc[r % 2][:, a * P:(a + 1) * P],
                                                  rep[:, a, 2 * r:2 * r + 2, :].rearrange("p e r -> p (e r)"),
                                                  ident[:], start=True, stop=True)
                        mm.then_inc(wb_mm, 1)
                    pe.wait_ge(xl, n + 1 + ONE)
                    for r in range(ER):
                        pe.wait_ge(tt_rdy, n * ER + max(r - 1, 0) + ONE)
                        for k in range(EK2):
                            mm = product3(nc, low[r % 2][:], [w[:, k, r * P:(r + 1) * P] for w in w1],
                                          [a[:, k, :] for a in xs], k == 0, k == 1)
                        mm.then_inc(low_mm, 1)
                    for f in range(FT):
                        pe.wait_ge(tl, n * ER + ER + ONE)
                        pe.wait_ge(hf_rdy, n * FT + max(f - 1, 0) + ONE)
                        for r in range(ER):
                            mm = product3(nc, mid[f % 2][:], [w[:, r, f * P:(f + 1) * P] for w in w2],
                                          [a[:, r, :] for a in ts], r == 0, r == ER - 1)
                        mm.then_inc(mid_mm, 1)
                    pe.wait_ge(x_rdy, n + ONE)
                    for f in range(FT):
                        pe.wait_ge(hl, n * FT + f + 1 + ONE)
                        for e in range(EK2):
                            mm = product3(nc, out[:, e, :], [w[:, f, e * P:(e + 1) * P] for w in w3],
                                          [a[:, f, :] for a in hs], f == 0, f == FT - 1)
                    mm.then_inc(out_mm, 1)

            @block.scalar
            def _(act):
                with act.Fori(0, NCH) as n:
                    act.wait_ge(low_mm, n * ER + ONE)
                    nc.scalar.activation(xs[0][:], x[:, :, bass.ds(n * CH, CH)], ACT.Copy).then_inc(xh, 1)
                    act.wait_ge(tt_rdy, n * ER + ONE)
                    for r in range(ER):
                        act.wait_ge(wb_mm, n * ER + r + 1 + ONE)
                        nc.scalar.activation(wb[:, r, :], wacc[r % 2][:], ACT.Copy).then_inc(wb_rdy, 1)
                    for r in range(ER):
                        act.wait_ge(tt_rdy, n * ER + r + 1 + ONE)
                        act.wait_ge(mid_mm, n * FT + ONE)
                        nc.scalar.activation(ts[0][:, r, :], tt[:, r, :], ACT.Copy).then_inc(th, 1)
                    for f in range(FT):
                        act.wait_ge(mid_mm, n * FT + f + 1 + ONE)
                        act.wait_ge(hl, n * FT + max(f - 1, 0) + ONE)
                        nc.scalar.activation(hf[f % 2][:], mid[f % 2][:], ACT.Gelu).then_inc(hf_rdy, 1)

            @block.vector
            def _(dve):
                dve.wait_ge(b_in, 32 + ONE)
                with dve.Fori(0, NCH) as n:
                    dve.wait_ge(wb_mm, n * ER + ONE)
                    nc.vector.tensor_copy(rep[:], weight[:, bass.ds(n * 4, 4), :].unsqueeze(3).to_broadcast(
                        [P, 4, NEXP, RANK])).then_inc(rep_rdy, 1)
                    dve.wait_ge(xh, n + 1 + ONE)
                    nc.vector.tensor_tensor(xs[1][:], x[:, :, bass.ds(n * CH, CH)], xs[0][:].bitcast(F32),
                                            ALU.subtract).then_inc(xl, 1)
                    for r in range(ER):
                        dve.wait_ge(wb_rdy, n * ER + r + 1 + ONE)
                        dve.wait_ge(low_mm, n * ER + r + 1 + ONE)
                        dve.wait_ge(tl, n * ER + ONE)
                        nc.vector.tensor_tensor(tt[:, r, :], low[r % 2][:], wb[:, r, :],
                                                ALU.mult).then_inc(tt_rdy, 1)
                    for r in range(ER):
                        dve.wait_ge(th, n * ER + r + 1 + ONE)
                        nc.vector.tensor_tensor(ts[1][:, r, :], tt[:, r, :], ts[0][:, r, :].bitcast(F32),
                                                ALU.subtract).then_inc(tl, 1)
                    for f in range(FT):
                        dve.wait_ge(hf_rdy, n * FT + f + 1 + ONE)
                        dve.wait_ge(out_mm, n + ONE)
                        nc.vector.tensor_copy(hs[0][:, f, :], hf[f % 2][:]).then_inc(hh, 1)
                        dve.wait_ge(hh, n * FT + f + 1 + ONE)
                        nc.vector.tensor_tensor(hs[1][:, f, :], hf[f % 2][:], hs[0][:, f, :].bitcast(F32),
                                                ALU.subtract).then_inc(hl, 1)
                    dve.wait_ge(out_mm, n + 1 + ONE)
                    for e in range(EK2):
                        here = x[:, e, bass.ds(n * CH, CH)]
                        op = nc.vector.scalar_tensor_tensor(out=here, in0=out[:, e, :], scalar=b3[:, e:e + 1],
                                                            in1=here, op0=ALU.add, op1=ALU.add)
                    op.then_inc(x_rdy, 1)


INNER, DH = 1024, 64
PAIRS = INNER // P
VA = P + 2


def linear_keys(nc, t, x, kv, ks):
    with ExitStack() as ctx:
        m = Names(nc, ctx, "lk")
        w = (m.sb("w_hi", [P, EK2, 2 * INNER], F32R), m.sb("w_lo", [P, EK2, 2 * INNER], F32R))
        load_split(nc, "lkw", [(t["wkv"].rearrange("(k p) n -> p k n", p=P), *w)])
        xs = [(m.sb(f"xh{i}", [P, EK2, CH], F32R), m.sb(f"xl{i}", [P, EK2, CH], F32R)) for i in range(2)]
        ek = m.sb("ek", [P, INNER])
        em = m.sb("em", [P, INNER])
        kf = [m.sb(f"kf{i}", [P, INNER]) for i in range(2)]
        vn = [m.sb(f"vn{i}", [P, PAIRS, VA]) for i in range(2)]
        kacc = m.ps("kacc", [P, INNER])
        vacc = m.ps("vacc", [P, INNER])
        kvacc = [m.ps(f"kvacc{i}", [P, 3, VA]) for i in range(3)]
        ready, xh, xl, k_mm, v_mm, ek_rdy, em_rdy, kf_rdy, vn_rdy, kv_mm, kv_read = (
            m.sem(n) for n in ("ready", "xh", "xl", "k_mm", "v_mm", "ek", "em", "kf", "vn", "kv_mm", "kv_read"))
        NT = S // P
        m.sem.start()
        with nc.Block() as block:
            @block.tensor
            def _(pe):
                pe.wait_ge(ready, 4 + ONE)
                with pe.Fori(0, B) as b:
                    def sums(tile):
                        n = b * NT + tile
                        pe.wait_ge(kf_rdy, n + 1 + ONE)
                        pe.wait_ge(vn_rdy, n + 1 + ONE)
                        if tile == 0:
                            pe.wait_ge(kv_read, b * 4 + ONE)
                        for p in range(PAIRS):
                            mm = nc.tensor.matmul(kvacc[p // 3][:, p % 3, :], kf[tile % 2][:, p * P:(p + 1) * P],
                                                  vn[tile % 2][:, p, :], start=(tile == 0 and p % 3 == 0),
                                                  stop=(tile == NT - 1), skip_group_check=True)
                        mm.then_inc(kv_mm, 1)
                    for tile in range(NT):
                        n = b * NT + tile
                        c, a = tile // 4, tile % 4
                        if a == 0:
                            pe.wait_ge(xl, b * CPB + c + 1 + ONE)
                        for acc, done, mm_rdy, base in ((kacc, kf_rdy, k_mm, 0), (vacc, vn_rdy, v_mm, INNER)):
                            pe.wait_ge(done, n + ONE)
                            for h in range(2):
                                for k in range(EK2):
                                    cols = slice(base + h * CH, base + (h + 1) * CH)
                                    mm = product3(nc, acc[:, h * CH:(h + 1) * CH],
                                                  [s[:, k, a * P:(a + 1) * P] for s in xs[c % 2]],
                                                  [s[:, k, cols] for s in w], k == 0, k == 1)
                            mm.then_inc(mm_rdy, 1)
                        if tile:
                            sums(tile - 1)
                    sums(NT - 1)

            @block.scalar
            def _(act):
                act.wait_ge(ready, 4 + ONE)
                with act.Fori(0, B) as b:
                    for tile in range(NT):
                        n = b * NT + tile
                        if tile % 4 == 0:
                            act.wait_ge(v_mm, b * NT + max(tile - 4, 0) + ONE)
                            nc.scalar.activation(xs[tile // 4 % 2][0][:], x[:, :, bass.ds(b * S + tile * P, CH)],
                                                 ACT.Copy).then_inc(xh, 1)
                        act.wait_ge(k_mm, n + 1 + ONE)
                        act.wait_ge(em_rdy, n + ONE)
                        nc.scalar.activation(ek[:], kacc[:], ACT.Exp).then_inc(ek_rdy, 1)
                        act.wait_ge(v_mm, n + 1 + ONE)
                        act.wait_ge(kv_mm, b * NT + max(tile - 1, 0) + ONE)
                        nc.scalar.activation(vn[tile % 2][:, :, 0:P], vacc[:].rearrange("p (a n) -> p a n", a=PAIRS),
                                             ACT.Copy).then_inc(vn_rdy, 1)

            @block.vector
            def _(dve):
                for i in range(2):
                    nc.vector.memset(vn[i][:, :, P:VA], 1.0).then_inc(ready, 1)
                nc.vector.memset(kv[:], 0.0).then_inc(ready, 1)
                nc.vector.memset(ks[:], 0.0).then_inc(ready, 1)
                dve.wait_ge(ready, 4 + ONE)
                with dve.Fori(0, B) as b:
                    for tile in range(NT):
                        n = b * NT + tile
                        if tile % 4 == 0:
                            dve.wait_ge(xh, b * CPB + tile // 4 + 1 + ONE)
                            nc.vector.tensor_tensor(xs[tile // 4 % 2][1][:], x[:, :, bass.ds(b * S + tile * P, CH)],
                                                    xs[tile // 4 % 2][0][:].bitcast(F32), ALU.subtract).then_inc(xl, 1)
                        dve.wait_ge(ek_rdy, n + 1 + ONE)
                        dve.wait_ge(kf_rdy, n + ONE)
                        nc.vector.tensor_scalar(em[:], ek[:], 1.0, None, ALU.min).then_inc(em_rdy, 1)
                        dve.wait_ge(em_rdy, n + 1 + ONE)
                        dve.wait_ge(kv_mm, b * NT + max(tile - 1, 0) + ONE)
                        nc.vector.scalar_tensor_tensor(out=kf[tile % 2][:], in0=kacc[:], scalar=0.0, in1=em[:],
                                                       op0=ALU.max, op1=ALU.add).then_inc(kf_rdy, 1)
                    dve.wait_ge(kv_mm, b * NT + NT + ONE)
                    for h in range(2):
                        rows = slice(h * DH, (h + 1) * DH)
                        for g in range(3):
                            np_ = min(3, PAIRS - 3 * g)
                            op = nc.vector.tensor_copy(kv[rows, bass.ds(b * PAIRS + 3 * g, np_), rows],
                                                       kvacc[g][rows, 0:np_, rows])
                            op2 = nc.vector.tensor_copy(ks[rows, bass.ds(b * PAIRS + 3 * g, np_), rows],
                                                        kvacc[g][rows, 0:np_, P:P + 1].to_broadcast([DH, np_, DH]))
                        op.then_inc(kv_read, 1)
                        op2.then_inc(kv_read, 1)


def linear_attention(nc, t, x, kv, ks):
    with ExitStack() as ctx:
        m = Names(nc, ctx, "la")
        pair = lambda n, s: (m.sb(n + "_hi", s, F32R), m.sb(n + "_lo", s, F32R))
        wq, wo = pair("wq", [P, EK2, INNER]), pair("wo", [P, PAIRS, E])
        load_split(nc, "law", [(t["wq1"].rearrange("(k p) n -> p k n", p=P), *wq),
                               (t["wout"].rearrange("(k p) n -> p k n", p=P), *wo)])
        bo = m.sb("bo", [P, EK2])
        xs = pair("xs", [P, EK2, CH])
        eq, em, qf, dn, rd, of = ([m.sb(f"{n}{i}", [P, CH]) for i in range(2)] for n in ("eq", "em", "qf", "dn", "rd", "of"))
        os_ = pair("os", [P, PAIRS, CH])
        qacc = [m.ps(f"qacc{i}", [P, CH]) for i in range(2)]
        num, den = ([m.ps(f"{n}{i}", [P, CH]) for i in range(2)] for n in ("num", "den"))
        out = m.ps("out", [P, EK2, CH])
        b_in, xh, xl, q_mm, eq_rdy, em_rdy, qf_rdy, nd_mm, dn_rdy, rd_rdy, of_rdy, oh, ol, out_mm, x_rdy = (
            m.sem(n) for n in ("b_in", "xh", "xl", "q_mm", "eq", "em", "qf", "nd_mm", "dn", "rd", "of", "oh", "ol", "out_mm", "x"))
        m.sem.start()
        with nc.Block() as block:
            @block.sync
            def _(sp):
                sp.dma_start(bo[:], t["bout"]).then_inc(b_in, 16)

            @block.tensor
            def _(pe):
                for b in range(B):
                    with pe.Fori(b * CPB, (b + 1) * CPB) as n:
                        pe.wait_ge(xl, n + 1 + ONE)

                        def queries(p):
                            pe.wait_ge(qf_rdy, n * PAIRS + max(p - 1, 0) + ONE)
                            for k in range(EK2):
                                mm = product3(nc, qacc[p % 2][:], [w[:, k, p * P:(p + 1) * P] for w in wq],
                                              [a[:, k, :] for a in xs], k == 0, k == 1)
                            mm.then_inc(q_mm, 1)

                        queries(0)
                        for p in range(PAIRS):
                            if p + 1 < PAIRS:
                                queries(p + 1)
                            pe.wait_ge(qf_rdy, n * PAIRS + p + 1 + ONE)
                            pe.wait_ge(of_rdy, n * PAIRS + max(p - 1, 0) + ONE)
                            nc.tensor.matmul(den[p % 2][:], ks[:, b * PAIRS + p, :], qf[p % 2][:], start=True, stop=True)
                            nc.tensor.matmul(num[p % 2][:], kv[:, b * PAIRS + p, :], qf[p % 2][:],
                                             start=True, stop=True).then_inc(nd_mm, 1)
                        pe.wait_ge(x_rdy, n + ONE)
                        for p in range(PAIRS):
                            pe.wait_ge(ol, n * PAIRS + p + 1 + ONE)
                            for e in range(EK2):
                                mm = product3(nc, out[:, e, :], [w[:, p, e * P:(e + 1) * P] for w in wo],
                                              [a[:, p, :] for a in os_], p == 0, p == PAIRS - 1)
                        mm.then_inc(out_mm, 1)

            @block.scalar
            def _(act):
                with act.Fori(0, NCH) as n:
                    act.wait_ge(q_mm, n * PAIRS + ONE)
                    nc.scalar.activation(xs[0][:], x[:, :, bass.ds(n * CH, CH)], ACT.Copy).then_inc(xh, 1)
                    for p in range(PAIRS):
                        act.wait_ge(q_mm, n * PAIRS + p + 1 + ONE)
                        act.wait_ge(em_rdy, n * PAIRS + max(p - 1, 0) + ONE)
                        nc.scalar.activation(eq[p % 2][:], qacc[p % 2][:], ACT.Exp).then_inc(eq_rdy, 1)
                        if p:
                            act.wait_ge(of_rdy, n * PAIRS + p + ONE)
                            act.wait_ge(out_mm, n + ONE)
                            nc.scalar.activation(os_[0][:, p - 1, :], of[(p - 1) % 2][:], ACT.Copy).then_inc(oh, 1)
                    act.wait_ge(of_rdy, n * PAIRS + PAIRS + ONE)
                    nc.scalar.activation(os_[0][:, PAIRS - 1, :], of[(PAIRS - 1) % 2][:], ACT.Copy).then_inc(oh, 1)

            @block.vector
            def _(dve):
                dve.wait_ge(b_in, 16 + ONE)
                with dve.Fori(0, NCH) as n:
                    dve.wait_ge(xh, n + 1 + ONE)
                    nc.vector.tensor_tensor(xs[1][:], x[:, :, bass.ds(n * CH, CH)], xs[0][:].bitcast(F32),
                                            ALU.subtract).then_inc(xl, 1)

                    def low_of(p):
                        dve.wait_ge(oh, n * PAIRS + p + 1 + ONE)
                        nc.vector.tensor_tensor(os_[1][:, p, :], of[p % 2][:], os_[0][:, p, :].bitcast(F32),
                                                ALU.subtract).then_inc(ol, 1)

                    def features(p):
                        dve.wait_ge(eq_rdy, n * PAIRS + p + 1 + ONE)
                        dve.wait_ge(qf_rdy, n * PAIRS + max(p - 1, 0) + ONE)
                        nc.vector.tensor_scalar(em[p % 2][:], eq[p % 2][:], 1.0, None, ALU.min).then_inc(em_rdy, 1)
                        dve.wait_ge(em_rdy, n * PAIRS + p + 1 + ONE)
                        dve.wait_ge(nd_mm, n * PAIRS + max(p - 1, 0) + ONE)
                        nc.vector.scalar_tensor_tensor(out=qf[p % 2][:], in0=qacc[p % 2][:], scalar=0.0, in1=em[p % 2][:],
                                                       op0=ALU.max, op1=ALU.add).then_inc(qf_rdy, 1)
                    features(0)
                    for p in range(PAIRS):
                        if p + 1 < PAIRS:
                            features(p + 1)
                        dve.wait_ge(nd_mm, n * PAIRS + p + 1 + ONE)
                        dve.wait_ge(rd_rdy, n * PAIRS + max(p - 1, 0) + ONE)
                        nc.vector.tensor_scalar(dn[p % 2][:], den[p % 2][:], 1e-6, None, ALU.add).then_inc(dn_rdy, 1)
                        dve.wait_ge(dn_rdy, n * PAIRS + p + 1 + ONE)
                        dve.wait_ge(of_rdy, n * PAIRS + max(p - 1, 0) + ONE)
                        nc.vector.reciprocal(rd[p % 2][:], dn[p % 2][:]).then_inc(rd_rdy, 1)
                        dve.wait_ge(rd_rdy, n * PAIRS + p + 1 + ONE)
                        dve.wait_ge(ol, n * PAIRS + max(p - 1, 0) + ONE)
                        nc.vector.tensor_tensor(of[p % 2][:], num[p % 2][:], rd[p % 2][:], ALU.mult).then_inc(of_rdy, 1)
                        if p:
                            low_of(p - 1)
                    low_of(PAIRS - 1)
                    dve.wait_ge(out_mm, n + 1 + ONE)
                    for e in range(EK2):
                        here = x[:, e, bass.ds(n * CH, CH)]
                        op = nc.vector.scalar_tensor_tensor(out=here, in0=out[:, e, :], scalar=bo[:, e:e + 1],
                                                            in1=here, op0=ALU.add, op1=ALU.add)
                    op.then_inc(x_rdy, 1)


HF = 512
HT = HF // P


def router_weights(nc, stage, t, weight, rows):
    with ExitStack() as ctx:
        m = Names(nc, ctx, stage)
        ident = m.sb("ident", [P, P])
        turned = m.sb("turned", [P, 2, P])
        acc = m.ps("acc", [P, 2, P])
        ident_in, acc_rdy, turned_rdy, out_done = (m.sem(n) for n in ("ident", "acc", "turned", "out"))
        m.sem.start()
        with nc.Block() as block:
            @block.sync
            def _(sp):
                sp.dma_start(ident[:], t["ident"]).then_inc(ident_in, 16)
                sp.wait_ge(turned_rdy, 1 + ONE)
                sp.dma_start(rows.rearrange("(a t) e n -> (t e) a n", a=2), turned[:]).then_inc(out_done, 16)
                sp.wait_ge(out_done, 16 + ONE)

            @block.tensor
            def _(pe):
                pe.wait_ge(ident_in, 16 + ONE)
                for a in range(2):
                    mm = nc.tensor.matmul(acc[:, a, :], weight[:, a * TILES // 2:(a + 1) * TILES // 2, :].rearrange(
                        "p t e -> p (t e)"), ident[:], start=True, stop=True)
                mm.then_inc(acc_rdy, 1)

            @block.scalar
            def _(act):
                act.wait_ge(acc_rdy, 1 + ONE)
                nc.scalar.activation(turned[:], acc[:], ACT.Copy).then_inc(turned_rdy, 1)


def routed_ffn(nc, t, x, rows):
    with ExitStack() as ctx:
        m = Names(nc, ctx, "ffn1")
        xh, xl = m.sb("xh", [P, EK2, T], F32R), m.sb("xl", [P, EK2, T], F32R)
        raw = m.sb("raw", [P, 3, HT * E])
        wh = [m.sb(f"wh{i}", [P, 3, HT * E], F32R) for i in range(2)]
        wl = [m.sb(f"wl{i}", [P, 3, HT * E], F32R) for i in range(2)]
        wb = [m.sb(f"wb{i}", [P, CH]) for i in range(2)]
        sg = [m.sb(f"sg{i}", [P, CH]) for i in range(2)]
        su = m.sb("su", [P, CH])
        hw = [m.sb(f"hw{i}", [P, CH]) for i in range(2)]
        hh = [m.sb(f"hh{i}", [P, HT, CH], F32R) for i in range(2)]
        hl = [m.sb(f"hl{i}", [P, HT, CH], F32R) for i in range(2)]
        gate = [m.ps(f"gate{i}", [P, CH]) for i in range(2)]
        up = [m.ps(f"up{i}", [P, CH]) for i in range(2)]
        out = m.ps("out", [P, EK2, CH])
        xh_rdy, xl_rdy, raw_in, wh_rdy, wl_rdy, one_rdy = (m.sem(n) for n in ("xh", "xl", "raw_in", "wh", "wl", "one"))
        wb_in = [m.sem(f"wb_in{i}") for i in range(2)]
        gu_mm, sg_rdy, su_rdy, hw_rdy, hh_rdy, hl_rdy, out_mm, x_rdy = (
            m.sem(n) for n in ("gu_mm", "sg", "su", "hw", "hh", "hl", "out_mm", "x"))
        NE = NEXP + 1
        assert NCH % 2 == 0 and NEXP % 2 == 0

        def operand(i, which, k, a, b):
            n = HF if which < 2 else E
            return [w[i][:, which, k * n + a:k * n + b] for w in (wh, wl)]

        def every_expert(eng, expert):
            expert(0, 0)
            with eng.Fori(0, NEXP // 2 - 1) as pair:
                expert(pair * 2 + 1, 1)
                expert(pair * 2 + 2, 0)
            expert(NE - 2, 1)
            expert(NE - 1, 0, True)

        def every_chunk(eng, g, body):
            for c in range(2):
                body(g * NCH + c, c, c, c)
            with eng.Fori(1, NCH // 2) as pair:
                for i in range(2):
                    body(g * NCH + pair * 2 + i, pair * 2 + i, i, None)

        m.sem.start()
        with nc.Block() as block:
            @block.sync
            def _(sp):
                def load_weights(g):
                    sp.wait_ge(wl_rdy, g + ONE)
                    sp.dma_start(raw[:].rearrange("p a n -> p (a n)"), t["experts"].rearrange("e p n -> p e n")[
                        :, bass.ds(g, 1)].rearrange("p e n -> p (e n)")).then_inc(raw_in, 16)

                def expert(g, i, final=False):
                    if type(g) is int and g == 0:
                        load_weights(0)
                        load_weights(1)
                        return
                    if not final:
                        load_weights(g + 1)
                    with sp.Fori(0, NCH // 2) as pair:
                        for b in range(2):
                            sp.wait_ge(hw_rdy, (g * NCH + pair * 2 + b - 1) * HT + ONE)
                            sp.dma_start(wb[b][:].rearrange("p (t n) -> p t n", n=P), rows.rearrange("t e n -> e t n")[
                                bass.ds(g - 1, 1), bass.ds(pair * 8 + b * 4, 4)].to_broadcast([P, 4, P])).then_inc(wb_in[b], 16)
                every_expert(sp, expert)

            @block.tensor
            def _(pe):
                pe.wait_ge(xl_rdy, NCH + ONE)

                def down(n, b, i):
                    pe.wait_ge(x_rdy, n + ONE)
                    for h in range(HT):
                        pe.wait_ge(hl_rdy, n * HT + h + 1 + ONE)
                        for e in range(EK2):
                            mm = product3(nc, out[:, e, :], operand(i, 2, h, e * P, (e + 1) * P),
                                          [hh[b][:, h, :], hl[b][:, h, :]], h == 0, h == HT - 1)
                    mm.then_inc(out_mm, 1)

                def expert(g, i, final=False):
                    pe.wait_ge(wl_rdy, g + 1 + ONE)

                    def chunk(n, c, b, first):
                        for h in range(HT):
                            pe.wait_ge(su_rdy, n * HT + max(h - 1, 0) + ONE)
                            for which, acc in ((0, gate), (1, up)):
                                for k in range(EK2):
                                    mm = product3(nc, acc[h % 2][:], operand(i, which, k, h * P, (h + 1) * P),
                                                  [s[:, k, bass.ds(c * CH, CH)] for s in (xh, xl)], k == 0, k == 1)
                            mm.then_inc(gu_mm, 1)
                        if first != 0:
                            down(n - 1, 1 - b, i)
                        elif not (type(g) is int and g == 0):
                            down(n - 1, 1 - b, 1 - i)
                    every_chunk(pe, g, chunk)
                    if final:
                        down(NE * NCH - 1, 1, i)
                every_expert(pe, expert)

            @block.scalar
            def _(act):
                with act.Fori(0, NCH) as n:
                    nc.scalar.activation(xh[:, :, bass.ds(n * CH, CH)], x[:, :, bass.ds(n * CH, CH)],
                                         ACT.Copy).then_inc(xh_rdy, 1)

                def split_high(g, i):
                    act.wait_ge(raw_in, g * 16 + 16 + ONE)
                    nc.scalar.activation(wh[i][:], raw[:], ACT.Copy).then_inc(wh_rdy, 1)
                split_high(0, 0)

                def expert(g, i, final=False):
                    def chunk(n, c, b, first):
                        def high(h):
                            act.wait_ge(hw_rdy, n * HT + h + 1 + ONE)
                            if not (type(n) is int and n == 0):
                                act.wait_ge(out_mm, n - 1 + ONE)
                            nc.scalar.activation(hh[b][:, h, :], hw[h % 2][:], ACT.Copy).then_inc(hh_rdy, 1)
                        for h in range(HT):
                            act.wait_ge(gu_mm, n * HT + h + 1 + ONE)
                            act.wait_ge(su_rdy, n * HT + max(h - 1, 0) + ONE)
                            nc.scalar.activation(sg[h % 2][:], gate[h % 2][:], ACT.Silu).then_inc(sg_rdy, 1)
                            if h:
                                high(h - 1)
                        high(HT - 1)
                        if first == 1 and not final:
                            act.wait_ge(out_mm, g * NCH + ONE)
                            split_high(g + 1, 1 - i)
                    every_chunk(act, g, chunk)
                every_expert(act, expert)

            @block.vector
            def _(dve):
                for i in range(2):
                    nc.vector.memset(wb[i][:], 1.0).then_inc(one_rdy, 1)
                dve.wait_ge(one_rdy, 2 + ONE)
                with dve.Fori(0, NCH) as n:
                    dve.wait_ge(xh_rdy, n + 1 + ONE)
                    nc.vector.tensor_tensor(xl[:, :, bass.ds(n * CH, CH)], x[:, :, bass.ds(n * CH, CH)],
                                            xh[:, :, bass.ds(n * CH, CH)].bitcast(F32), ALU.subtract).then_inc(xl_rdy, 1)

                def split_low(g, i):
                    dve.wait_ge(wh_rdy, g + 1 + ONE)
                    nc.vector.tensor_tensor(wl[i][:], raw[:], wh[i][:].bitcast(F32), ALU.subtract).then_inc(wl_rdy, 1)
                split_low(0, 0)

                def add(n, c):
                    dve.wait_ge(out_mm, n + 1 + ONE)
                    dve.wait_ge(x_rdy, n + ONE)
                    here = x[:, :, bass.ds(c * CH, CH)]
                    nc.vector.tensor_tensor(here, here, out[:], ALU.add).then_inc(x_rdy, 1)

                def expert(g, i, final=False):
                    shared = type(g) is int and g == 0

                    def chunk(n, c, b, first):
                        def low(h):
                            dve.wait_ge(hh_rdy, n * HT + h + 1 + ONE)
                            nc.vector.tensor_tensor(hl[b][:, h, :], hw[h % 2][:], hh[b][:, h, :].bitcast(F32),
                                                    ALU.subtract).then_inc(hl_rdy, 1)
                        if not shared:
                            loads = (n - NCH - b) * 8 + 16
                            dve.wait_ge(wb_in[b], loads + ONE)
                        for h in range(HT):
                            dve.wait_ge(sg_rdy, n * HT + h + 1 + ONE)
                            dve.wait_ge(hw_rdy, n * HT + h + ONE)
                            nc.vector.tensor_tensor(su[:], sg[h % 2][:], up[h % 2][:], ALU.mult).then_inc(su_rdy, 1)
                            dve.wait_ge(su_rdy, n * HT + h + 1 + ONE)
                            dve.wait_ge(hl_rdy, n * HT + max(h - 1, 0) + ONE)
                            nc.vector.tensor_tensor(hw[h % 2][:], su[:], wb[b][:], ALU.mult).then_inc(hw_rdy, 1)
                            if h:
                                low(h - 1)
                            if h == 0 and not (shared and first is not None):
                                add(n - 2, c - 2 if first is None else NCH - 2 + c)
                        low(HT - 1)
                        if first == 1 and not final:
                            split_low(g + 1, 1 - i)
                    every_chunk(dve, g, chunk)
                    if final:
                        for c in (NCH - 2, NCH - 1):
                            add(NEXP * NCH + c, c)
                every_expert(dve, expert)


def transformer(nc, t, out):
    dram = lambda n, s, d: nc.dram_tensor(n, s, d, kind="Internal").ap()
    scratch = (dram("q_parts", [3, NHP * HD, S], BF16), dram("k_late", [3, NHP * HD, S], BF16),
               dram("k_early", [3, NHP * HD, S], BF16), dram("v_heads", [NHP, 2, P, KT * VC], F32))
    sums = (dram("value_sums", [NH * HD, S], F32), dram("band_sums", [(NH + 2) * HD, S], F32),
            dram("denominators", [NH, S], F32))
    project_qkv(nc, t, scratch)
    attention(nc, t, scratch, sums)
    rows = dram("router_rows", [TILES, NEXP, P], F32)
    with nc.sbuf_tensor("x", [P, EK2, T], F32) as x, nc.sbuf_tensor("weight", [P, TILES, NEXP], F32) as weight:
        project_attention(nc, t, sums, x)
        layer_norm(nc, "ln0", x)
        route(nc, "route0", t, x, weight, False)
        low_rank_ffn(nc, t, x, weight)
        layer_norm(nc, "ln1", x)
        with nc.sbuf_tensor("kv", [P, B * PAIRS, P], F32) as kv, nc.sbuf_tensor("ks", [P, B * PAIRS, P], F32) as ks:
            linear_keys(nc, t, x, kv, ks)
            linear_attention(nc, t, x, kv, ks)
        layer_norm(nc, "ln2", x)
        route(nc, "route1", t, x, weight, True)
        router_weights(nc, "rows1", t, weight, rows)
        routed_ffn(nc, t, x, rows)
        layer_norm(nc, "ln3", x, out)


def layouts(i):
    c = np.ascontiguousarray
    heads = lambda v: np.tile(v, H)
    halves = lambda v: c(v.reshape(EK2, P).T)
    rk, rv = i["L0_attn_rel_k"], i["L0_attn_rel_v"]
    far = 2 * REL
    place = lambda d: np.clip(d, -REL, REL) + REL
    masks = np.zeros((KS, 3), np.float32)
    for r, p in enumerate(K_PARTS):
        masks[r * HD:(r + 1) * HD, p] = 1
    m, w = np.meshgrid(np.arange(P), np.arange(W), indexing="ij")

    def expert(g, u, d):
        rows = lambda a: a.reshape(-1, P, a.shape[1]).transpose(1, 0, 2).reshape(P, -1)
        return np.concatenate([rows(c(g.T)), rows(c(u.T)), rows(c(d.T))], 1)
    experts = [expert(i["L1_ffn_sg"], i["L1_ffn_su"], i["L1_ffn_sd"])] + [
        expert(i["L1_ffn_eg"][e], i["L1_ffn_eu"][e], i["L1_ffn_ed"][e]) for e in range(NEXP)]
    wqkv = i["L1_attn_Wqkv"]
    return {
        "xt": c(i["L0_attn_hidden_states"].reshape(T, E).T),
        "wqkv": c(np.stack([i[f"L0_attn_W{n}"].T for n in "qkv"])),
        "cols": c(np.stack([i["L0_attn_bq"], i["L0_attn_bk"], heads(rk[far]), heads(rk[0])], 1)),
        "rows": c(np.broadcast_to(np.stack([i["L0_attn_bv"], heads(rv[far]), heads(rv[0])]), (P, 3, E))),
        "rk": c(np.tile(rk[place(np.arange(TAB) - (W - 1 - PAD))].T, (NPT, 1))),
        "rkb": c(np.tile(np.stack([rk[far], rk[0]], 1), (NPT, 1))),
        "msk": masks,
        "rv": c(rv[place(m - w + PAD)]),
        "rvb": c(np.broadcast_to(np.stack([rv[far], rv[0]]), (P, 2, HD))),
        "wo": c(i["L0_attn_Wo"].T), "bo": halves(i["L0_attn_bo"]),
        "route0_w": c(i["L0_ffn_router_w"]), "route0_b": c(np.broadcast_to(i["L0_ffn_router_b"], (P, NEXP))),
        "route1_w": c(i["L1_ffn_router_w"].T), "route1_b": np.zeros((P, NEXP), np.float32),
        "iota": c(np.broadcast_to(np.arange(NEXP, dtype=np.float32), (P, NEXP))),
        "ident": np.eye(P, dtype=np.float32),
        "w1": c(i["L0_ffn_w1"].transpose(1, 0, 2).reshape(E, NEXP * RANK)),
        "w2": c(i["L0_ffn_w2"].reshape(NEXP * RANK, FF)),
        "w3": c(i["L0_ffn_lin2_w"]), "b3": halves(i["L0_ffn_lin2_b"]),
        "wkv": c(wqkv[:, INNER:]), "wq1": c(wqkv[:, :INNER]),
        "wout": c(i["L1_attn_Wout"]), "bout": halves(i["L1_attn_bout"]),
        "experts": c(np.stack(experts)),
    }


def kernel(**inputs):
    import concourse.bacc as bacc
    from concourse.bass_utils import run_bass_kernel_spmd

    nc = bacc.Bacc("TRN2", target_bir_lowering=False, num_devices=1)
    arrays = {f"in_{n}": a for n, a in layouts({n: np.asarray(a) for n, a in inputs.items()}).items()}
    t = {n[3:]: nc.dram_tensor(n, a.shape, mybir.dt.from_np(a.dtype), kind="ExternalInput").ap()
         for n, a in arrays.items()}
    out = nc.dram_tensor("out_t", [E, T], F32, kind="ExternalOutput").ap()
    transformer(nc, t, out)
    got = run_bass_kernel_spmd(nc, [arrays], core_ids=[0])
    return np.ascontiguousarray(got.results[0]["out_t"].T).reshape(B, S, E)
```

```python
from contextlib import ExitStack

import numpy as np

import concourse.bass as bass
from concourse import mybir

F32 = mybir.dt.float32
F32R = mybir.dt.float32r
BF16 = mybir.dt.bfloat16
ALU = mybir.AluOpType
ACT = mybir.ActivationFunctionType
AX = mybir.AxisListType
RMAX = bass.bass_isa.ReduceOp.max

P = 128
B, S, E = 2, 2048, 256
T = B * S
H, HD = 16, 16
REL = 20
NREL = 2 * REL + 1
EK2 = E // P
CH = 512
NCH = T // CH
CPB = S // CH
KT = S // P
PAD = REL - 1
W = P + 2 * PAD
HALF = 1024
NH = B * H
NHP = NH + 4
VC = 32
EPS = 1e-5
ONE = 1


class Semaphores:

    def __init__(self, nc, ctx, stage):
        self.nc, self.stage, self.mine = nc, stage, []
        ctx.callback(self.end)

    def __call__(self, name):
        self.mine.append(self.nc.alloc_semaphore(name=f"{self.stage}_{name}"))
        return self.mine[-1]

    def start(self):
        for one in self.mine:
            self.nc.sync.sem_inc(one, ONE)
        self.nc.all_engine_barrier()

    def end(self):
        self.nc.clear_and_free_semaphores(self.mine)
        self.nc.all_engine_barrier()


def project_qkv(nc, t, scratch):
    qs, kh, kl, vs = scratch
    with ExitStack() as ctx:
        sb = lambda n, s, d: ctx.enter_context(nc.sbuf_tensor("qkv_" + n, s, d))
        ps = lambda n, s: ctx.enter_context(nc.psum_tensor("qkv_" + n, s, F32))
        sem = Semaphores(nc, ctx, "qkv")
        wts = sb("wts", [P, 3, EK2, E], F32)
        cols = sb("cols", [P, EK2, 4], F32)
        kbias = sb("kbias", [P, EK2, 2], F32)
        rows = sb("rows", [P, E], F32)
        xc = [sb(f"xc{i}", [P, EK2, CH], F32) for i in range(2)]
        full = [sb(f"full{i}", [P, CH], F32) for i in range(2)]
        rest = [sb(f"rest{i}", [P, CH], F32) for i in range(2)]
        part = [sb(f"part{i}", [P, 3, CH], BF16) for i in range(4)]
        vst = sb("vst", [P, H, KT, HD], F32)
        acc = [ps(f"acc{i}", [P, CH]) for i in range(4)]
        vacc = ps("vacc", [P, 4 * E])
        w_in, x_in0, x_in1 = sem("w_in"), sem("x_in0"), sem("x_in1")
        x_in = [x_in0, x_in1]
        prep, qk_mm, v_mm = sem("prep"), sem("qk_mm"), sem("v_mm")
        f_rdy, p1_rdy, r_rdy, p2_rdy, p3_rdy = (sem(n) for n in ("f_rdy", "p1_rdy", "r_rdy", "p2_rdy", "p3_rdy"))
        v_rdy = sem("v_rdy")
        part_out = [sem(f"part_out{i}") for i in range(4)]
        v_out, pad_out = sem("v_out"), sem("pad_out")
        units = [(0, ("q", 0), qs, 0), (1, ("q", 1), qs, 1), (2, (0, 0), kh, 0), (2, (0, 1), kl, 0),
                 (3, (1, 0), kh, 1), (3, (1, 1), kl, 1)]
        NU = len(units)
        NUB = NU * CPB

        def bias_of(key):
            return cols[:, key[1], 0:1] if key[0] == "q" else kbias[:, key[0], key[1]:key[1] + 1]

        def s_slot(c, s):
            return (c * NU + s) % 4

        sem.start()
        with nc.Block() as block:
            @block.sync
            def _(sp):
                sp.dma_start(wts[:], t["wqkv"].rearrange("w (k p) n -> p w k n", p=P)).then_inc(w_in, 16)
                sp.dma_start(cols[:], t["cols"].rearrange("(k p) n -> p k n", p=P)).then_inc(w_in, 16)
                sp.dma_start(rows[:], t["rows"]).then_inc(w_in, 16)
                def load(n):
                    sp.dma_start(xc[n % 2][:], t["xt"].rearrange("(k p) n -> p k n", p=P)[
                        :, :, n * CH:(n + 1) * CH]).then_inc(x_in[n % 2], 16)
                load(0)
                for b in range(B):
                    for c in range(CPB):
                        n = b * CPB + c
                        if n + 1 < NCH:
                            sp.wait_ge(v_mm, n + ONE)
                            load(n + 1)
                        for s, (_, _, dst, e) in enumerate(units):
                            sp.wait_ge(p3_rdy, b * NUB + c * NU + s + 1 + ONE)
                            sp.dma_start(dst.rearrange("a r n -> r a n")[
                                bass.ds(b * E + e * P, P), :, c * CH:(c + 1) * CH],
                                part[s_slot(c, s)][:]).then_inc(part_out[s_slot(c, s)], 16)
                    sp.wait_ge(v_rdy, b * CPB + CPB + ONE)
                    sp.dma_start(vs.rearrange("h p c -> p h c")[:, b * H:(b + 1) * H],
                                 vst[:].rearrange("p h t c -> p h (t c)")).then_inc(v_out, 16)
                for i in range(4):
                    sp.wait_ge(part_out[i], 16 * B * NUB // 4 + ONE)
                sp.wait_ge(v_out, 16 * B + ONE)
                for dst in (qs, kh, kl):
                    sp.dma_start(dst[:, NH * HD:NHP * HD], dst[:, 0:4 * HD]).then_inc(pad_out, 16)
                sp.dma_start(vs[NH:NHP], vs[0:4]).then_inc(pad_out, 16)
                sp.wait_ge(pad_out, 64 + ONE)

            @block.tensor
            def _(pe):
                pe.wait_ge(w_in, 48 + ONE)
                with pe.Fori(0, B) as b:
                    for c in range(CPB):
                        x = xc[c % 2]
                        pe.wait_ge(x_in[c % 2], b * 32 + 16 * (c // 2) + 16 + ONE)
                        for a, (w, e) in enumerate(((0, 0), (0, 1), (1, 0), (1, 1))):
                            unread = [u[0] for u in units][::-1].index(a) if c else 0
                            pe.wait_ge(p1_rdy, b * NUB + c * NU - unread + ONE)
                            for k in range(EK2):
                                mm = nc.tensor.matmul(acc[a][:], wts[:, w, k, e * P:(e + 1) * P], x[:, k, :],
                                                      start=(k == 0), stop=(k == 1))
                            mm.then_inc(qk_mm, 1)
                        pe.wait_ge(v_rdy, b * CPB + c + ONE)
                        for i in range(4):
                            for k in range(EK2):
                                mm = nc.tensor.matmul(vacc[:, i * E:(i + 1) * E], x[:, k, i * P:(i + 1) * P],
                                                      wts[:, 2, k, :], start=(k == 0), stop=(k == 1))
                        mm.then_inc(v_mm, 1)

            @block.scalar
            def _(act):
                act.wait_ge(prep, 4 + ONE)
                with act.Fori(0, B) as b:
                    def first_part(n):
                        a, key, _, _ = units[n % NU]
                        act.wait_ge(qk_mm, b * 4 * CPB + 4 * (n // NU) + a + 1 + ONE)
                        act.wait_ge(r_rdy, b * NUB + max(n - 1, 0) + ONE)
                        nc.scalar.activation(full[n % 2][:], acc[a][:], ACT.Identity,
                                             bias=bias_of(key)).then_inc(f_rdy, 1)
                        act.wait_ge(part_out[n % 4], b * (16 * NUB // 4) + 16 * (n // 4) + ONE)
                        nc.scalar.activation(part[n % 4][:, 0, :], acc[a][:], ACT.Identity,
                                             bias=bias_of(key)).then_inc(p1_rdy, 1)

                    def second_part(n):
                        act.wait_ge(r_rdy, b * NUB + n + 1 + ONE)
                        nc.scalar.activation(part[n % 4][:, 1, :], rest[n % 2][:], ACT.Copy).then_inc(p2_rdy, 1)
                    for n in range(NUB):
                        first_part(n)
                        if n:
                            second_part(n - 1)
                    second_part(NUB - 1)

            @block.vector
            def _(dve):
                dve.wait_ge(w_in, 48 + ONE)
                for e in range(EK2):
                    for l in range(2):
                        nc.vector.tensor_tensor(kbias[:, e, l:l + 1], cols[:, e, 1:2], cols[:, e, 2 + l:3 + l],
                                                ALU.add).then_inc(prep, 1)
                with dve.Fori(0, B) as b:
                    def remainder(n):
                        dve.wait_ge(f_rdy, b * NUB + n + 1 + ONE)
                        dve.wait_ge(p1_rdy, b * NUB + n + 1 + ONE)
                        dve.wait_ge(p3_rdy, b * NUB + max(n - 1, 0) + ONE)
                        nc.vector.tensor_tensor(rest[n % 2][:], full[n % 2][:], part[n % 4][:, 0, :],
                                                ALU.subtract).then_inc(r_rdy, 1)

                    def third_part(n):
                        dve.wait_ge(p2_rdy, b * NUB + n + 1 + ONE)
                        dve.wait_ge(r_rdy, b * NUB + n + 1 + ONE)
                        nc.vector.tensor_tensor(part[n % 4][:, 2, :], rest[n % 2][:], part[n % 4][:, 1, :],
                                                ALU.subtract).then_inc(p3_rdy, 1)
                    for c in range(CPB):
                        for s in range(NU):
                            n = c * NU + s
                            remainder(n)
                            if n:
                                third_part(n - 1)
                        dve.wait_ge(v_mm, b * CPB + c + 1 + ONE)
                        if c == 0:
                            dve.wait_ge(v_out, b * 16 + ONE)
                        nc.vector.tensor_tensor(
                            vst[:, :, 4 * c:4 * c + 4, :].rearrange("p h t d -> p t h d"),
                            vacc[:].rearrange("p (t h d) -> p t h d", t=4, h=H),
                            rows[:].rearrange("p (h d) -> p h d", h=H).unsqueeze(1).to_broadcast([P, 4, H, HD]),
                            ALU.add).then_inc(v_rdy, 1)
                    third_part(NUB - 1)


NPT = 6
KS = NPT * HD
Q_PARTS, K_PARTS = (0, 0, 0, 1, 1, 2), (0, 1, 2, 0, 1, 0)
TAB = P + W - 1
HEADS = 4
STEPS = 2 * KT
WI = CH // (2 * KT)
GUARD_LAG = 8
STORE_LAG = 2
NPROB = 3
QG = HALF // 4
ZEROS = 2 + 3 * HEADS + 2
GUARD = KS


def window(a, b, kt):
    q0, q1 = max(P * kt - PAD, a), min(P * kt - PAD + W, b)
    return (q0, q1, q0 - (P * kt - PAD)) if q1 > q0 else None


def half_window(half, kt):
    return window(half * HALF, (half + 1) * HALF, kt)


def segments(a, b, step, kt):
    out = []
    for q0 in range(a, b, step):
        cut = min(max(P * kt, q0), q0 + step)
        out += [(c, d, early) for c, d, early in ((q0, cut, 0), (cut, q0 + step, 1)) if d > c]
    return out


BAND_ITEMS = [("band", w, min(w + WI, W)) for w in range(0, W, WI)]
VALUE_ITEMS = [("centre", w, w + WI) for w in range(PAD, PAD + P, WI)] + [
    ("side", a, min(a + WI, b)) for w0, b in ((0, PAD), (PAD + P, W)) for a in range(w0, b, WI)]
NCENTRE = P // WI


def attention_plan():
    steps = []
    first = STEPS // 2 - len(BAND_ITEMS)
    for u in range(HEADS):
        todo = VALUE_ITEMS[first:] if u % 2 else BAND_ITEMS + VALUE_ITEMS[:first]
        for s in range(STEPS):
            item = todo[s // 2] if s % 2 and s // 2 < len(todo) else None
            steps.append((u, s // KT, s % KT, item))
    return steps


def attention(nc, t, scratch, outs):
    qs, kh, kl, vs = scratch
    values, band_values, den = outs
    with ExitStack() as ctx:
        sb = lambda n, s, d: ctx.enter_context(nc.sbuf_tensor("att_" + n, s, d))
        sem = Semaphores(nc, ctx, "att")
        ktab = [sb(f"ktab{l}", [KS, TAB], BF16) for l in range(2)]
        vtab = sb("vtab", [P, W, HD], F32)
        rvb = sb("rvb", [P, 2, HD], F32)
        with ExitStack() as tctx:
            tb = lambda n, s, d: tctx.enter_context(nc.sbuf_tensor("tab_" + n, s, d))
            tsem = Semaphores(nc, tctx, "tab")
            rk, rkb, msk = tb("rk", [KS, TAB], F32), tb("rkb", [KS, 2], F32), tb("msk", [KS, 3], F32)
            kf, kr = tb("kf", [KS, TAB], F32), tb("kr", [KS, TAB], F32)
            kp = [tb(f"kp{i}", [KS, TAB], BF16) for i in range(3)]
            rv = tb("rv", [P, W, HD], F32)
            tin, step = tsem("in"), tsem("step")
            tsem.start()
            with nc.Block() as block:
                @block.sync
                def _(sp):
                    for dst, name in ((rk, "rk"), (rkb, "rkb"), (msk, "msk"), (rv, "rv"), (rvb, "rvb")):
                        sp.dma_start(dst[:], t[name]).then_inc(tin, 16)

                @block.vector
                def _(dve):
                    dve.wait_ge(tin, 80 + ONE)
                    n = 0
                    for l in range(2):
                        dve.wait_ge(step, n + ONE)
                        nc.vector.tensor_scalar(kf[:], rk[:], rkb[:, l:l + 1], None, ALU.subtract).then_inc(step, 1)
                        dve.wait_ge(step, n + 1 + ONE)
                        nc.vector.tensor_copy(kp[0][:], kf[:]).then_inc(step, 1)
                        dve.wait_ge(step, n + 2 + ONE)
                        nc.vector.tensor_tensor(kr[:], kf[:], kp[0][:], ALU.subtract).then_inc(step, 1)
                        dve.wait_ge(step, n + 3 + ONE)
                        nc.vector.tensor_copy(kp[1][:], kr[:]).then_inc(step, 1)
                        dve.wait_ge(step, n + 4 + ONE)
                        nc.vector.tensor_tensor(kp[2][:], kr[:], kp[1][:], ALU.subtract).then_inc(step, 1)
                        dve.wait_ge(step, n + 5 + ONE)
                        nc.vector.tensor_scalar(kf[:], kp[0][:], msk[:, 0:1], None, ALU.mult).then_inc(step, 1)
                        dve.wait_ge(step, n + 6 + ONE)
                        nc.vector.scalar_tensor_tensor(out=kr[:], in0=kp[1][:], scalar=msk[:, 1:2], in1=kf[:],
                                                       op0=ALU.mult, op1=ALU.add).then_inc(step, 1)
                        dve.wait_ge(step, n + 7 + ONE)
                        nc.vector.scalar_tensor_tensor(out=ktab[l][:], in0=kp[2][:], scalar=msk[:, 2:3], in1=kr[:],
                                                       op0=ALU.mult, op1=ALU.add).then_inc(step, 1)
                        n += 8
                    for l, (a, b) in enumerate(((0, PAD), (PAD, W))):
                        nc.vector.tensor_tensor(vtab[:, a:b, :], rv[:, a:b, :],
                                                rvb[:, l:l + 1, :].to_broadcast([P, b - a, HD]),
                                                ALU.subtract).then_inc(step, 1)
                    dve.wait_ge(step, n + 2 + ONE)

        q = [sb(f"q{u}", [P, S], BF16) for u in range(HEADS)]
        k = [[sb(f"k{l}{u}", [P, S], BF16) for u in range(HEADS)] for l in range(2)]
        vraw = [sb(f"vraw{i}", [P, KT * HD], F32) for i in range(2)]
        v = [sb(f"v{i}", [P, 2, KT * VC], F32) for i in range(2)]
        qband = sb("qband", [KS, 2, S + 2 * PAD], BF16)
        band = [sb(f"band{i}", [P, W * 2 * KT], F32) for i in range(2)]
        pwin = [sb(f"pwin{i}", [P, 2, KT, W], F32) for i in range(2)]
        prob = [sb(f"prob{i}", [P, HALF], F32) for i in range(NPROB)]
        kmax = [sb(f"kmax{i}", [P, HALF], F32) for i in range(2)]
        allmax = sb("allmax", [P, HALF], F32)
        ghi = sb("ghi", [1, HALF], BF16)
        glo = sb("glo", [1, HALF], BF16)
        oev = [sb(f"oev{i}", [P, QG], F32) for i in range(2)]
        rel = sb("rel", [HD, 2, S], F32)
        score = [ctx.enter_context(nc.psum_tensor(f"score{i}", [P, HALF], F32)) for i in range(2)]
        again = [ctx.enter_context(nc.psum_tensor(f"again{i}", [P, CH], F32)) for i in range(2)]
        item_acc = ctx.enter_context(nc.psum_tensor("item_acc", [P, CH], F32))
        oacc = ctx.enter_context(nc.psum_tensor("oacc", [P, CH], F32))

        zeroed, ones_set = sem("zeroed"), sem("ones_set")
        stack_in = [sem(f"stack_in{u}") for u in range(HEADS)]
        v_in = [sem(f"v_in{i}") for i in range(2)]
        qband_in = sem("qband_in")
        v_ones, v_half, v_rdy = sem("v_ones"), sem("v_half"), sem("v_rdy")
        score_rdy, band_added, exp_done = sem("score_rdy"), sem("band_added"), sem("exp_done")
        window_rdy, pv_done, o_read = sem("window_rdy"), sem("pv_done"), sem("o_read")
        again_rdy, again_added, again_read = sem("again_rdy"), sem("again_added"), sem("again_read")
        item_rdy, item_act, item_dve = sem("item_rdy"), sem("item_act"), sem("item_dve")
        all_max, ghi_rdy, glo_rdy = sem("all_max"), sem("ghi_rdy"), sem("glo_rdy")
        guard_in = [sem(f"guard_in{i}") for i in range(2)]
        o_out = [sem(f"o_out{i}") for i in range(2)]
        rel_out = sem("rel_out")

        plan = attention_plan()
        NS = len(plan)
        NW = sum(half_window(s // KT, s % KT) is not None for s in range(STEPS))
        chunks = [(half, kt, c) for half in range(2) for kt in range(KT) for c in range(2)]
        NC = len(chunks)

        def chunk_window(half, kt, c):
            q0 = half * HALF + c * CH
            return window(q0, q0 + CH, kt)
        NA = sum(chunk_window(*c) is not None for c in chunks)
        NB, NV = len(BAND_ITEMS), len(VALUE_ITEMS)
        NSIDE = NV - NCENTRE
        ITEMS, ITEMS_ACT, ITEMS_DVE = 2 * (NB + NV), 2 * (NB + NCENTRE), 2 * NSIDE

        def items_before(f):
            kinds = [st[3][0] for st in plan[:f] if st[3]]
            side = kinds.count("side")
            return len(kinds), len(kinds) - side, side

        def windows_before(f):
            return sum(half_window(st[1], st[2]) is not None for st in plan[:f])

        def load_stack(sp, u, head_row):
            for stack, src, parts in ((q[u], qs, Q_PARTS), (k[0][u], kh, K_PARTS), (k[1][u], kl, K_PARTS)):
                for r, p in enumerate(parts):
                    sp.dma_start(stack[r * HD:(r + 1) * HD, :], src[p, head_row, :]).then_inc(stack_in[u], 16)

        def load_qband(sp, rows):
            for hd in range(2):
                for r, p in enumerate(Q_PARTS):
                    sp.dma_start(qband[r * HD:(r + 1) * HD, hd, PAD:PAD + S], qs[p, rows[hd], :]).then_inc(qband_in, 16)
        STACK_INC, QBAND_INC = 18 * 16, 12 * 16

        sem.start()
        with nc.Block() as block:
            @block.sync
            def _(sp):
                sp.wait_ge(zeroed, 2 + ONE)
                load_qband(sp, [slice(0, HD), slice(HD, 2 * HD)])
                for u in range(HEADS):
                    load_stack(sp, u, slice(u * HD, (u + 1) * HD))
                    if u < 2:
                        sp.dma_start(vraw[u][:], vs[u]).then_inc(v_in[u], 16)

                def guard(half, seen, nxt):
                    sp.wait_ge(glo_rdy, seen + ONE)
                    cols = slice(half * HALF, (half + 1) * HALF)
                    sp.dma_start(q[nxt][GUARD:GUARD + 1, cols], ghi[:]).then_inc(guard_in[half], 16)
                    sp.dma_start(q[nxt][GUARD + 1:GUARD + 2, cols], glo[:]).then_inc(guard_in[half], 16)
                sp.wait_ge(zeroed, ZEROS + ONE)
                guard(0, 1, 0)
                sp.wait_ge(item_rdy, NB + ONE)
                load_qband(sp, [slice(2 * HD, 3 * HD), slice(3 * HD, 4 * HD)])

                def load_values(j, u):
                    sp.wait_ge(v_rdy, j * HEADS + u + 1 + ONE)
                    sp.dma_start(vraw[u % 2][:], vs.rearrange("h p c -> p h c")[
                        :, bass.ds(j * HEADS + u + 2, 1)].rearrange("p h c -> p (h c)")).then_inc(v_in[u % 2], 16)

                def store_values(n, head, half):
                    sp.wait_ge(o_read, n + ONE)
                    for g in range(HALF // QG):
                        sp.dma_start(values[bass.ds(head * HD, HD), half * HALF + g * QG:half * HALF + (g + 1) * QG],
                                     oev[half][g * VC:g * VC + HD, :]).then_inc(o_out[half], 16)
                        sp.dma_start(den[bass.ds(head, 1), half * HALF + g * QG:half * HALF + (g + 1) * QG],
                                     oev[half][g * VC + HD:g * VC + HD + 1, :]).then_inc(o_out[half], 16)

                def store_band_values(n, pair):
                    sp.wait_ge(item_dve, n + ONE)
                    sp.dma_start(band_values.rearrange("(h d) s -> d h s", d=HD)[:, bass.ds(pair * 2, 2), :],
                                 rel[:]).then_inc(rel_out, 16)

                with sp.Fori(0, NH // HEADS) as j:
                    for f, (u, half, kt, item) in enumerate(plan):
                        if kt == GUARD_LAG:
                            n = 2 * u + half
                            guard(1 - half, j * 2 * HEADS + 2 + n, (n + 1) // 2 % HEADS)
                        if kt == STORE_LAG and (u or half):
                            n = 2 * u + half
                            store_values(j * 2 * HEADS + n, j * HEADS + (n - 1) // 2, 1 - half)
                            if half == 0:
                                sp.wait_ge(pv_done, j * NS + u * STEPS + ONE)
                                load_stack(sp, u - 1, bass.ds(j * HEADS * HD + (u - 1 + HEADS) * HD, HD))
                                load_values(j, u - 1)
                        if item == BAND_ITEMS[-1]:
                            sp.wait_ge(item_rdy, j * ITEMS + NB + items_before(f + 1)[0] + ONE)
                            rows = j * HEADS * HD + (u + 4) * HD
                            load_qband(sp, [bass.ds(rows, HD), bass.ds(rows + HD, HD)])
                        if item == VALUE_ITEMS[-1]:
                            store_band_values(j * ITEMS_DVE + items_before(f + 1)[2], j * 2 + u // 2)
                    store_values(j * 2 * HEADS + 2 * HEADS, j * HEADS + HEADS - 1, 1)
                    sp.wait_ge(pv_done, j * NS + NS + ONE)
                    load_stack(sp, HEADS - 1, bass.ds(j * HEADS * HD + (2 * HEADS - 1) * HD, HD))
                    load_values(j, HEADS - 1)
                store_band_values(NH // HEADS * ITEMS_DVE + NSIDE, NH // 2)
                for i in range(2):
                    sp.wait_ge(o_out[i], 16 * 2 * (HALF // QG) * NH + ONE)
                    sp.wait_ge(v_in[i], 16 * (1 + NH // 2) + ONE)
                    sp.wait_ge(guard_in[i], 32 * (NH + 1 - i) + ONE)
                for u in range(HEADS):
                    sp.wait_ge(stack_in[u], STACK_INC * (1 + NH // HEADS) + ONE)
                sp.wait_ge(qband_in, QBAND_INC * (2 + NH // 2) + ONE)
                sp.wait_ge(rel_out, 16 * (1 + NH // 2) + ONE)

            def scores_of(out, a, b, u, kt, rows):
                for c, d, early in segments(a, b, CH, kt):
                    mm = nc.tensor.matmul(out[:, c - a:d - a], k[early][u][0:rows, kt * P:(kt + 1) * P],
                                          q[u][0:rows, c:d], start=True, stop=True)
                return mm

            def band_products(w0, w1):
                for w in range(w0, w1):
                    mm = nc.tensor.matmul(
                        item_acc[:, (w - w0) * 2 * KT:(w - w0 + 1) * 2 * KT].rearrange("p (h t) -> p h t", h=2),
                        ktab[0 if w < PAD else 1][:, W - 1 - w:W - 1 - w + P],
                        qband[:, :, w:w + (KT - 1) * P + 1:P], start=True, stop=True)
                return mm

            def value_band_products(w0, w1, pair):
                for w in range(w0, w1):
                    mm = nc.tensor.matmul(
                        item_acc[0:HD, (w - w0) * 2 * KT:(w - w0 + 1) * 2 * KT].rearrange("p (h t) -> p h t", h=2),
                        vtab[:, w, :], pwin[pair][:, :, :, w], start=True, stop=True)
                return mm

            @block.tensor
            def _(pe):
                pe.wait_ge(zeroed, 2 + ONE)
                pe.wait_ge(qband_in, QBAND_INC + ONE)
                for n, (_, w0, w1) in enumerate(BAND_ITEMS):
                    if n:
                        pe.wait_ge(item_act, n + ONE)
                    band_products(w0, w1).then_inc(item_rdy, 1)
                pe.wait_ge(stack_in[0], STACK_INC + ONE)
                for n, (half, kt, c) in enumerate(chunks):
                    if n >= 2:
                        pe.wait_ge(again_read, n - 1 + ONE)
                    a = half * HALF + c * CH
                    scores_of(again[c], a, a + CH, 0, kt, KS).then_inc(again_rdy, 1)

                def scores(f, j=None):
                    u, half, kt = plan[f % NS][:3]
                    if kt == 0:
                        n = 32 * (f // STEPS + 1)
                        pe.wait_ge(guard_in[half], (n if j is None else j * 32 * HEADS + n) + ONE)
                    if j is not None:
                        pe.wait_ge(exp_done, j * NS + max(f - 1, 0) + ONE)
                    scores_of(score[f % 2], half * HALF, (half + 1) * HALF, u, kt, P).then_inc(score_rdy, 1)
                pe.wait_ge(zeroed, ZEROS + ONE)
                pe.wait_ge(ones_set, 2 * HEADS + ONE)
                scores(0)
                with pe.Fori(0, NH // HEADS) as j:
                    def maximum_chunk(f, c):
                        u, half, kt = plan[f][:3]
                        nxt = (u + 1) % HEADS
                        if half == 0 and kt == 0 and c == 0:
                            pe.wait_ge(stack_in[nxt], (j * STACK_INC + (STACK_INC * 2 if nxt == 0 else STACK_INC)) + ONE)
                        pe.wait_ge(again_read, j * 2 * NS + NC + 2 * f + c - 1 + ONE)
                        a = half * HALF + c * CH
                        scores_of(again[c], a, a + CH, nxt, kt, KS).then_inc(again_rdy, 1)

                    def value_products(f):
                        u, half, kt = plan[f][:3]
                        if kt == 0:
                            pe.wait_ge(o_read, j * 2 * HEADS + 2 * u + half + ONE)
                            pe.wait_ge(v_rdy, j * HEADS + u + 1 + ONE)
                        pe.wait_ge(exp_done, j * NS + f + 1 + ONE)
                        for a, b, early in segments(half * HALF, (half + 1) * HALF, QG, kt):
                            a, b = a - half * HALF, b - half * HALF
                            g = a // QG
                            mm = nc.tensor.matmul(oacc[g * VC:(g + 1) * VC, a - g * QG:b - g * QG],
                                                  v[u % 2][:, early, kt * VC:(kt + 1) * VC], prob[f % NPROB][:, a:b],
                                                  start=(kt == 0), stop=(kt == KT - 1), skip_group_check=True)
                        mm.then_inc(pv_done, 1)

                    def item_products(f):
                        u, _, _, item = plan[f]
                        kind, w0, w1 = item
                        n, na, nd = items_before(f)
                        if n and plan[f - 2][3] and plan[f - 2][3][0] == "side":
                            pe.wait_ge(item_dve, j * ITEMS_DVE + nd + ONE)
                        elif n == 0:
                            pe.wait_ge(item_act, j * ITEMS_ACT + NB + ONE)
                            pe.wait_ge(item_dve, j * ITEMS_DVE + ONE)
                        else:
                            pe.wait_ge(item_act, j * ITEMS_ACT + NB + na + ONE)
                            pe.wait_ge(item_dve, j * ITEMS_DVE + nd + ONE)
                        if kind == "band":
                            if w0 == 0:
                                pe.wait_ge(qband_in, j * 2 * QBAND_INC + QBAND_INC * (2 + u // 2) + ONE)
                            mm = band_products(w0, w1)
                        else:
                            if item == VALUE_ITEMS[0]:
                                pe.wait_ge(window_rdy, j * HEADS * NW + (u // 2) * 2 * NW + ONE)
                            mm = value_band_products(w0, w1, (u // 2 + 1) % 2)
                        mm.then_inc(item_rdy, 1)

                    for f, st in enumerate(plan):
                        scores(f + 1, j)
                        maximum_chunk(f, 0)
                        if f:
                            value_products(f - 1)
                        maximum_chunk(f, 1)
                        if st[3]:
                            item_products(f)
                    value_products(NS - 1)
                passes = NH // HEADS
                pe.wait_ge(window_rdy, passes * HEADS * NW + ONE)
                pe.wait_ge(item_dve, passes * ITEMS_DVE + ONE)
                for n, (kind, w0, w1) in enumerate(VALUE_ITEMS):
                    if n <= NCENTRE:
                        pe.wait_ge(item_act, passes * ITEMS_ACT + NB + n + ONE)
                    else:
                        pe.wait_ge(item_dve, passes * ITEMS_DVE + n - NCENTRE + ONE)
                    value_band_products(w0, w1, 1).then_inc(item_rdy, 1)

            @block.scalar
            def _(act):
                for n, (_, w0, w1) in enumerate(BAND_ITEMS):
                    act.wait_ge(item_rdy, n + 1 + ONE)
                    nc.scalar.activation(band[0][:, w0 * 2 * KT:w1 * 2 * KT], item_acc[:, 0:(w1 - w0) * 2 * KT],
                                         ACT.Copy).then_inc(item_act, 1)

                def guard_high(n, j=None):
                    act.wait_ge(all_max, (n + 1 if j is None else j * 2 * HEADS + n + 1) + ONE)
                    if j is not None:
                        act.wait_ge(guard_in[(n - 1) % 2], j * 32 * HEADS + 32 * ((n - 1) // 2 + 1) + ONE)
                    nc.scalar.activation(ghi[:], allmax[0:1, :], ACT.Copy, scale=-1.0).then_inc(ghi_rdy, 1)
                guard_high(0)
                act.wait_ge(zeroed, ZEROS + ONE)

                def copy_centre(w0, w1, products):
                    act.wait_ge(item_rdy, products + ONE)
                    nc.scalar.activation(
                        rel[:].rearrange("p h (t q) -> p h t q", t=KT)[:, :, :, w0 - PAD:w1 - PAD],
                        item_acc[0:HD, :].rearrange("p (w h t) -> p h t w", h=2, t=KT), ACT.Copy).then_inc(item_act, 1)

                with act.Fori(0, NH // HEADS) as j:
                    nwin = 0

                    def copy_window(f):
                        u, half, kt, _ = plan[f]
                        win = half_window(half, kt)
                        if win is None:
                            return
                        q0, q1, w0 = win
                        if u % 2 == 0 and half == 0 and kt == 0:
                            act.wait_ge(item_rdy, j * ITEMS + NB + items_before(f)[0] + ONE)
                        act.wait_ge(exp_done, j * NS + f + 1 + ONE)
                        nc.scalar.activation(pwin[u // 2][:, u % 2, kt, w0:w0 + q1 - q0],
                                             prob[f % NPROB][:, q0 - half * HALF:q1 - half * HALF],
                                             ACT.Copy).then_inc(window_rdy, 1)

                    def copy_item(f):
                        u, _, _, item = plan[f]
                        if item is None or item[0] == "side":
                            return
                        kind, w0, w1 = item
                        n = items_before(f)[0]
                        if kind == "band":
                            act.wait_ge(item_rdy, j * ITEMS + NB + n + 1 + ONE)
                            nc.scalar.activation(band[(u // 2 + 1) % 2][:, w0 * 2 * KT:w1 * 2 * KT],
                                                 item_acc[:, 0:(w1 - w0) * 2 * KT], ACT.Copy).then_inc(item_act, 1)
                        else:
                            if item == VALUE_ITEMS[0]:
                                act.wait_ge(rel_out, j * 32 + 16 * (u // 2) + ONE)
                            copy_centre(w0, w1, j * ITEMS + NB + n + 1)

                    def evacuate(n):
                        act.wait_ge(pv_done, j * NS + (n + 1) * KT + ONE)
                        act.wait_ge(o_out[n % 2], (j * HEADS + n // 2) * (16 * 2 * (HALF // QG)) + ONE)
                        nc.scalar.activation(oev[n % 2][:], oacc[:, 0:QG], ACT.Copy).then_inc(o_read, 1)

                    for f, (u, half, kt, item) in enumerate(plan):
                        if half_window(half, kt) is not None:
                            nwin += 1
                            act.wait_ge(band_added, j * HEADS * NW + nwin + ONE)
                        else:
                            act.wait_ge(score_rdy, j * NS + f + 1 + ONE)
                        act.wait_ge(pv_done, j * NS + max(f - NPROB + 1, 0) + ONE)
                        act.wait_ge(window_rdy, j * HEADS * NW + windows_before(max(f - NPROB + 1, 0)) + ONE)
                        nc.scalar.activation(prob[f % NPROB][:], score[f % 2][:], ACT.Exp, scale=0.25).then_inc(exp_done, 1)
                        n = 2 * u + half
                        if n and kt == 0:
                            evacuate(n - 1)
                        if f:
                            copy_window(f - 1)
                            copy_item(f - 1)
                        if kt == GUARD_LAG:
                            guard_high(1 + n, j)
                    copy_window(NS - 1)
                    evacuate(2 * HEADS - 1)
                passes = NH // HEADS
                act.wait_ge(rel_out, 32 * passes + ONE)
                for n, (_, w0, w1) in enumerate(VALUE_ITEMS[:NCENTRE]):
                    copy_centre(w0, w1, passes * ITEMS + NB + n + 1)

            @block.gpsimd
            def _(pool):
                nc.gpsimd.memset(qband[:, :, 0:PAD], 0.0).then_inc(zeroed, 1)
                nc.gpsimd.memset(qband[:, :, PAD + S:S + 2 * PAD], 0.0).then_inc(zeroed, 1)
                operands = [k[l][u] for l in range(2) for u in range(HEADS)]
                for o in q + operands:
                    nc.gpsimd.memset(o[KS:P, :], 0.0).then_inc(zeroed, 1)
                for i in range(2):
                    pool.wait_ge(zeroed, ZEROS - 2 + i + ONE)
                    nc.gpsimd.memset(pwin[i][:], 0.0).then_inc(zeroed, 1)
                pool.wait_ge(zeroed, ZEROS + ONE)
                for o in operands:
                    nc.gpsimd.memset(o[GUARD:GUARD + 2, :], 1.0).then_inc(ones_set, 1)

                def all_reduce(n, j=None, made=None):
                    if j is None:
                        pool.wait_ge(zeroed, ZEROS + ONE)
                        pool.wait_ge(again_read, (n + 1) * NC // 2 + ONE)
                        if n:
                            pool.wait_ge(glo_rdy, n + ONE)
                    else:
                        maxes_in = pool.to_reg(j * 2 * NS + (n + 1) * (NC // 2) + ONE)
                        last_read = pool.to_reg(j * 2 * HEADS + n + ONE)
                        if made is not None:
                            values_made = pool.to_reg(j * HEADS + made + 1 + ONE)
                        pool.wait_ge(zeroed, ZEROS + ONE)
                        pool.wait_ge(again_read, maxes_in)
                        pool.wait_ge(glo_rdy, last_read)
                        if made is not None:
                            pool.wait_ge(v_rdy, values_made)
                    nc.gpsimd.partition_all_reduce(allmax[:], kmax[n % 2][:], P, RMAX).then_inc(all_max, 1)
                pool.wait_ge(ones_set, 2 * HEADS + ONE)
                for i in range(2):
                    nc.gpsimd.memset(v[i][:], 1.0).then_inc(v_ones, 1)
                pool.wait_ge(v_ones, 2 + ONE)

                def make_values(u, j=None):
                    g = lambda per_pass, n: n if j is None else j * per_pass + n
                    pool.wait_ge(v_in[u % 2], g(8 * HEADS, 16 * (u // 2) + 16) + ONE)
                    if j is not None:
                        pool.wait_ge(pv_done, j * NS + (u - 1) * STEPS + ONE)
                        pool.wait_ge(all_max, j * 2 * HEADS + 2 * u + ONE)
                    for l in range(2):
                        if l == 1:
                            pool.wait_ge(v_half, g(HEADS, u + 1) + ONE)
                        nc.gpsimd.tensor_tensor(
                            v[u % 2][:, l, :].rearrange("p (t c) -> p t c", c=VC)[:, :, 0:HD],
                            vraw[u % 2][:].rearrange("p (t d) -> p t d", d=HD),
                            rvb[:, l:l + 1, :].to_broadcast([P, KT, HD]), ALU.add).then_inc((v_half, v_rdy)[l], 1)
                make_values(0)
                pool.wait_ge(v_rdy, 1 + ONE)
                all_reduce(0)
                all_reduce(1)
                with pool.Fori(0, NH // HEADS) as j:
                    for u in range(HEADS):
                        make_values(u + 1, j)
                        all_reduce(2 + 2 * u, j, u + 1)
                        all_reduce(3 + 2 * u, j)

            @block.vector
            def _(dve):
                def band_of(pair, hd, kt, w0, w1):
                    return band[pair][:].rearrange("p (w h t) -> p w h t", h=2, t=KT)[:, w0:w1, hd, kt]

                def add_chunk_band(chunk, pair, hd, products):
                    half, kt, c = chunk
                    dve.wait_ge(again_rdy, products + ONE)
                    win = chunk_window(half, kt, c)
                    if win is not None:
                        q0, q1, w0 = win
                        a = half * HALF + c * CH
                        o = again[c][:, q0 - a:q1 - a]
                        nc.vector.tensor_tensor(o, o, band_of(pair, hd, kt, w0, w0 + q1 - q0),
                                                ALU.add).then_inc(again_added, 1)

                def chunk_maximum(chunk, added, before, reduced=None):
                    half, kt, c = chunk
                    if added is not None:
                        dve.wait_ge(again_added, added + ONE)
                    here = kmax[half][:, c * CH:(c + 1) * CH]
                    if kt == 0:
                        if reduced is not None:
                            dve.wait_ge(all_max, reduced + ONE)
                        nc.vector.tensor_copy(here, again[c][:]).then_inc(again_read, 1)
                    else:
                        dve.wait_ge(again_read, before)
                        nc.vector.tensor_tensor(here, here, again[c][:], ALU.max).then_inc(again_read, 1)

                def added_by(i):
                    if chunk_window(*chunks[i]) is None:
                        return None
                    return sum(chunk_window(*c) is not None for c in chunks[:i + 1])

                def guard_low(n, j=None):
                    dve.wait_ge(ghi_rdy, (n + 1 if j is None else j * 2 * HEADS + n + 1) + ONE)
                    if j is not None:
                        dve.wait_ge(guard_in[(n - 1) % 2], j * 32 * HEADS + 32 * ((n - 1) // 2 + 1) + ONE)
                    nc.vector.scalar_tensor_tensor(out=glo[:], in0=allmax[0:1, :], scalar=-1.0, in1=ghi[:],
                                                   op0=ALU.mult, op1=ALU.subtract).then_inc(glo_rdy, 1)

                def add_side(w0, w1, products, copied, mine):
                    dve.wait_ge(item_rdy, products + ONE)
                    dve.wait_ge(item_act, copied + ONE)
                    dve.wait_ge(item_dve, mine + ONE)
                    view = rel[:].rearrange("p h (t q) -> p h t q", t=KT)
                    new = item_acc[0:HD, 0:(w1 - w0) * 2 * KT].rearrange("p (w h t) -> p h t w", h=2, t=KT)
                    if w0 < PAD:
                        old, new = view[:, :, 0:KT - 1, P - PAD + w0:P - PAD + w1], new[:, :, 1:KT, :]
                    else:
                        old, new = view[:, :, 1:KT, w0 - PAD - P:w1 - PAD - P], new[:, :, 0:KT - 1, :]
                    for hd in range(2):
                        op = nc.vector.tensor_tensor(old[:, hd], old[:, hd], new[:, hd], ALU.add)
                    op.then_inc(item_dve, 1)

                dve.wait_ge(item_act, NB + ONE)
                for i, chunk in enumerate(chunks):
                    add_chunk_band(chunk, 0, 0, i + 1)
                    chunk_maximum(chunk, added_by(i), i - 1)
                    if i == NC // 2 + 24:
                        guard_low(0)

                def add_band(f, j=None):
                    u, half, kt, _ = plan[f % NS]
                    win = half_window(half, kt)
                    if win is None:
                        return
                    q0, q1, w0 = win
                    dve.wait_ge(score_rdy, (f + 1 if j is None else j * NS + f + 1) + ONE)
                    o = score[f % 2][:, q0 - half * HALF:q1 - half * HALF]
                    nc.vector.tensor_tensor(o, o, band_of(u // 2, u % 2, kt, w0, w0 + q1 - q0),
                                            ALU.add).then_inc(band_added, 1)
                add_band(0)
                with dve.Fori(0, NH // HEADS) as j:
                    for f, (u, half, kt, item) in enumerate(plan):
                        nxt = u + 1
                        for c in range(2):
                            i = 2 * (f % STEPS) + c
                            if i == 0 and nxt % 2 == 0:
                                dve.wait_ge(item_act, j * ITEMS_ACT + NB + items_before(f - STEPS)[1] + NB + ONE)
                            done = j * 2 * NS + NC + 2 * f + c
                            add_chunk_band(chunks[i], nxt // 2 % 2, nxt % 2, done + 1)
                            if c == 0:
                                add_band(f + 1, j)
                            added = added_by(i)
                            chunk_maximum(chunks[i], None if added is None else j * HEADS * NA + nxt * NA + added,
                                          done - 1, j * 2 * HEADS + 2 * u + half + 1)
                        if f and plan[f - 1][3] and plan[f - 1][3][0] == "side":
                            _, w0, w1 = plan[f - 1][3]
                            n, na, nd = items_before(f - 1)
                            add_side(w0, w1, j * ITEMS + NB + n + 1, j * ITEMS_ACT + NB + na, j * ITEMS_DVE + nd)
                        n = 2 * u + half
                        if kt == GUARD_LAG:
                            guard_low(1 + n, j)
                passes = NH // HEADS
                for n, (_, w0, w1) in enumerate(VALUE_ITEMS[NCENTRE:]):
                    add_side(w0, w1, passes * ITEMS + NB + NCENTRE + n + 1, passes * ITEMS_ACT + NB + NCENTRE,
                             passes * ITEMS_DVE + n)


class Names:

    def __init__(self, nc, ctx, stage):
        self.nc, self.ctx, self.stage = nc, ctx, stage
        self.sem = Semaphores(nc, ctx, stage)

    def sb(self, name, shape, dtype=F32):
        return self.ctx.enter_context(self.nc.sbuf_tensor(f"{self.stage}_{name}", shape, dtype))

    def ps(self, name, shape):
        return self.ctx.enter_context(self.nc.psum_tensor(f"{self.stage}_{name}", shape, F32))


def invert_denominators(nc, den, inverse):
    with ExitStack() as ctx:
        m = Names(nc, ctx, "inv")
        d, r_ = m.sb("den", [P, NH * S // P]), m.sb("inverse", [P, NH * S // P])
        d_in, r_rdy, r_out = m.sem("in"), m.sem("made"), m.sem("out")
        by_partition = lambda a: a.rearrange("h (g n) -> (h g) n", g=P // NH)
        m.sem.start()
        with nc.Block() as block:
            @block.sync
            def _(sp):
                sp.dma_start(d[:], by_partition(den)).then_inc(d_in, 16)
                sp.wait_ge(r_rdy, 1 + ONE)
                sp.dma_start(by_partition(inverse), r_[:]).then_inc(r_out, 16)
                sp.wait_ge(r_out, 16 + ONE)

            @block.vector
            def _(dve):
                dve.wait_ge(d_in, 16 + ONE)
                nc.vector.reciprocal(r_[:], d[:]).then_inc(r_rdy, 1)


def project_attention(nc, t, sums, inverse, x):
    values, band_values = sums
    with ExitStack() as ctx:
        m = Names(nc, ctx, "wo")
        w = m.sb("w", [P, EK2, E])
        bo = m.sb("bo", [P, EK2])
        xin = [m.sb(f"xin{i}", [P, EK2, CH]) for i in range(CPB)]
        parts = [m.sb(f"parts{i}", [P, EK2, 2, CH]) for i in range(CPB)]
        inv = [m.sb(f"inv{i}", [P, EK2, CH]) for i in range(CPB)]
        total = m.sb("total", [P, EK2, CH])
        att = [m.sb(f"att{i}", [P, EK2, CH]) for i in range(2)]
        out = [m.ps(f"out{i}", [P, EK2, CH]) for i in range(2)]
        w_in = m.sem("w_in")
        chunk_in = [m.sem(f"in{i}") for i in range(CPB)]
        summed, att_rdy, out_rdy, x_rdy = (m.sem(n) for n in ("summed", "att", "out", "x"))
        HK = P // HD
        ND = EK2 * (2 + HK) + 1
        m.sem.start()
        with nc.Block() as block:
            @block.sync
            def _(sp):
                sp.dma_start(w[:], t["wo"].rearrange("(k p) n -> p k n", p=P)).then_inc(w_in, 16)
                sp.dma_start(bo[:], t["bo"]).then_inc(w_in, 16)
                with sp.Fori(0, B) as b:
                    for c in range(CPB):
                        sp.wait_ge(x_rdy, b * (c + 1) + ONE)
                        cols = slice(c * CH, (c + 1) * CH)
                        s = chunk_in[c]
                        for e in range(EK2):
                            rows = bass.ds(b * E + e * P, P)
                            sp.dma_start(parts[c][:, e, 0, :], values[rows, cols]).then_inc(s, 16)
                            sp.dma_start(parts[c][:, e, 1, :],
                                         band_values[bass.ds(b * E + e * P + 2 * HD, P), cols]).then_inc(s, 16)
                            for h in range(HK):
                                sp.dma_start(inv[c][h * HD:(h + 1) * HD, e, :],
                                             inverse[bass.ds(b * H + e * HK + h, 1), cols].to_broadcast([HD, CH])).then_inc(s, 16)
                        sp.dma_start(xin[c][:], t["xt"].rearrange("(k p) n -> p k n", p=P)[
                            :, :, bass.ds(b * S + c * CH, CH)]).then_inc(s, 16)

            @block.vector
            def _(dve):
                dve.wait_ge(w_in, 32 + ONE)

                def normalised(n, b, c):
                    dve.wait_ge(chunk_in[c], b * (16 * ND) + 16 * ND + ONE)
                    dve.wait_ge(att_rdy, n + ONE)
                    nc.vector.tensor_tensor(total[:], parts[c][:, :, 0, :], parts[c][:, :, 1, :],
                                            ALU.add).then_inc(summed, 1)
                    dve.wait_ge(summed, n + 1 + ONE)
                    dve.wait_ge(out_rdy, b * CPB + max(c - 1, 0) + ONE)
                    nc.vector.tensor_tensor(att[c % 2][:], total[:], inv[c][:], ALU.mult).then_inc(att_rdy, 1)

                def add(n, b, c):
                    dve.wait_ge(out_rdy, n + 1 + ONE)
                    for e in range(EK2):
                        op = nc.vector.scalar_tensor_tensor(
                            out=x[:, e, bass.ds(b * S + c * CH, CH)], in0=out[c % 2][:, e, :], scalar=bo[:, e:e + 1],
                            in1=xin[c][:, e, :], op0=ALU.add, op1=ALU.add)
                    op.then_inc(x_rdy, 1)
                with dve.Fori(0, B) as b:
                    for c in range(CPB):
                        normalised(b * CPB + c, b, c)
                        if c:
                            add(b * CPB + c - 1, b, c - 1)
                    add(b * CPB + CPB - 1, b, CPB - 1)

            @block.tensor
            def _(pe):
                pe.wait_ge(w_in, 32 + ONE)
                with pe.Fori(0, B) as b:
                    for c in range(CPB):
                        pe.wait_ge(att_rdy, b * CPB + c + 1 + ONE)
                        pe.wait_ge(x_rdy, b * CPB + max(c - 1, 0) + ONE)
                        for e in range(EK2):
                            for k in range(EK2):
                                mm = nc.tensor.matmul(out[c % 2][:, e, :], w[:, k, e * P:(e + 1) * P], att[c % 2][:, k, :],
                                                      start=(k == 0), stop=(k == 1))
                        mm.then_inc(out_rdy, 1)


def layer_norm(nc, stage, x, out=None):
    with ExitStack() as ctx:
        m = Names(nc, ctx, stage)
        mean_of = m.sb("mean_of", [P, P])
        eps = m.sb("eps", [P, 1])
        dev = [m.sb(f"dev{i}", [P, EK2, CH]) for i in range(2)]
        sq = [m.sb(f"sq{i}", [P, EK2, CH]) for i in range(2)]
        sd = [m.sb(f"sd{i}", [P, CH]) for i in range(2)]
        rs = [m.sb(f"rs{i}", [P, CH]) for i in range(2)]
        mean = [m.ps(f"mean{i}", [P, CH]) for i in range(2)]
        var = [m.ps(f"var{i}", [P, CH]) for i in range(2)]
        ready, mean_rdy, dev_rdy, sq_rdy, var_rdy, sd_rdy, rs_rdy, x_rdy, x_out = (
            m.sem(n) for n in ("ready", "mean", "dev", "sq", "var", "sd", "rs", "x", "out"))
        m.sem.start()
        with nc.Block() as block:
            def chunk(n):
                return x[:, :, n * CH:(n + 1) * CH]

            @block.tensor
            def _(pe):
                def mean_of_chunk(n):
                    if n >= 2:
                        pe.wait_ge(dev_rdy, n - 1 + ONE)
                    for k in range(EK2):
                        mm = nc.tensor.matmul(mean[n % 2][:], mean_of[:], chunk(n)[:, k], start=(k == 0), stop=(k == 1))
                    mm.then_inc(mean_rdy, 1)
                pe.wait_ge(ready, 2 + ONE)
                mean_of_chunk(0)
                mean_of_chunk(1)
                for n in range(NCH):
                    pe.wait_ge(sq_rdy, n + 1 + ONE)
                    if n >= 2:
                        pe.wait_ge(sd_rdy, n - 1 + ONE)
                    for k in range(EK2):
                        mm = nc.tensor.matmul(var[n % 2][:], mean_of[:], sq[n % 2][:, k, :], start=(k == 0), stop=(k == 1))
                    mm.then_inc(var_rdy, 1)
                    if n + 2 < NCH:
                        mean_of_chunk(n + 2)

            @block.vector
            def _(dve):
                nc.vector.memset(mean_of[:], 1.0 / E).then_inc(ready, 1)
                nc.vector.memset(eps[:], EPS).then_inc(ready, 1)

                def deviations(n):
                    dve.wait_ge(mean_rdy, n + 1 + ONE)
                    if n >= 2:
                        dve.wait_ge(x_rdy, n - 1 + ONE)
                        dve.wait_ge(sq_rdy, n - 1 + ONE)
                    nc.vector.tensor_tensor(dev[n % 2][:], chunk(n), mean[n % 2][:].unsqueeze(1).to_broadcast([P, EK2, CH]),
                                            ALU.subtract).then_inc(dev_rdy, 1)
                deviations(0)
                for n in range(NCH):
                    if n + 1 < NCH:
                        deviations(n + 1)
                    dve.wait_ge(sd_rdy, n + 1 + ONE)
                    if n >= 2:
                        dve.wait_ge(x_rdy, n - 1 + ONE)
                    nc.vector.reciprocal(rs[n % 2][:], sd[n % 2][:]).then_inc(rs_rdy, 1)
                    dve.wait_ge(rs_rdy, n + 1 + ONE)
                    nc.vector.tensor_tensor(chunk(n), dev[n % 2][:], rs[n % 2][:].unsqueeze(1).to_broadcast([P, EK2, CH]),
                                            ALU.mult).then_inc(x_rdy, 1)

            @block.scalar
            def _(act):
                def squares(n):
                    act.wait_ge(dev_rdy, n + 1 + ONE)
                    if n >= 2:
                        act.wait_ge(var_rdy, n - 1 + ONE)
                    nc.scalar.activation(sq[n % 2][:], dev[n % 2][:], ACT.Square).then_inc(sq_rdy, 1)
                act.wait_ge(ready, 2 + ONE)
                squares(0)
                for n in range(NCH):
                    act.wait_ge(var_rdy, n + 1 + ONE)
                    if n >= 2:
                        act.wait_ge(rs_rdy, n - 1 + ONE)
                    nc.scalar.activation(sd[n % 2][:], var[n % 2][:], ACT.Sqrt, bias=eps[:]).then_inc(sd_rdy, 1)
                    if n + 1 < NCH:
                        squares(n + 1)

            if out is not None:
                @block.sync
                def _(sp):
                    with sp.Fori(0, NCH) as n:
                        sp.wait_ge(x_rdy, n + 1 + ONE)
                        sp.dma_start(out.rearrange("(k p) n -> p k n", p=P)[:, :, bass.ds(n * CH, CH)],
                                     x[:, :, bass.ds(n * CH, CH)]).then_inc(x_out, 16)
                    sp.wait_ge(x_out, 16 * NCH + ONE)


NEXP = 8
TILES = T // P


def route(nc, stage, t, x, weight, normalise):
    with ExitStack() as ctx:
        m = Names(nc, ctx, stage)
        rw = m.sb("rw", [P, EK2, NEXP])
        rb = m.sb("rb", [P, NEXP])
        iota = m.sb("iota", [P, NEXP])
        xs = [m.sb(f"xs{i}", [P, EK2, CH]) for i in range(2)]
        lg = [m.ps(f"lg{i}", [P, 4, NEXP]) for i in range(2)]
        names = ("logit", "shift", "ex", "prob", "mask1", "mask", "kept")
        logit, shift, ex, prob, mask1, mask, kept = (m.sb(n, [P, 4, NEXP]) for n in names)
        mx, tot, inv, tot2, inv2 = (m.sb(n, [P, 4]) for n in ("mx", "tot", "inv", "tot2", "inv2"))
        top = m.sb("top", [P, 4, 8])
        where = m.sb("where", [P, 4, 8], mybir.dt.uint32)
        wheref = m.sb("wheref", [P, 4, 8])
        w_in, xs_rdy, lg_rdy, ex_rdy, d = (m.sem(n) for n in ("w_in", "xs", "lg", "ex", "d"))
        m.sem.start()
        with nc.Block() as block:
            @block.sync
            def _(sp):
                sp.dma_start(rw[:], t[f"{stage}_w"].rearrange("(k p) n -> p k n", p=P)).then_inc(w_in, 16)
                sp.dma_start(rb[:], t[f"{stage}_b"]).then_inc(w_in, 16)
                sp.dma_start(iota[:], t["iota"]).then_inc(w_in, 16)

            ND = 5 + 2 * 4 + 5 + (4 if normalise else 1)

            @block.tensor
            def _(pe):
                pe.wait_ge(w_in, 48 + ONE)
                with pe.Fori(0, NCH // 2) as i:
                    for c in range(2):
                        pe.wait_ge(xs_rdy, i * 2 + c + 1 + ONE)
                        pe.wait_ge(d, i * 2 * ND + ONE)
                        for a in range(4):
                            for k in range(EK2):
                                mm = nc.tensor.matmul(lg[c][:, a, :], xs[c][:, k, a * P:(a + 1) * P], rw[:, k, :],
                                                      start=(k == 0), stop=(k == 1))
                        mm.then_inc(lg_rdy, 1)

            @block.scalar
            def _(act):
                with act.Fori(0, NCH // 2) as i:
                    for c in range(2):
                        act.wait_ge(lg_rdy, i * 2 + ONE)
                        nc.scalar.activation(xs[c][:], x[:, :, bass.ds(i * 2 * CH + c * CH, CH)], ACT.Copy).then_inc(xs_rdy, 1)
                    for c in range(2):
                        act.wait_ge(d, i * 2 * ND + c * ND + 3 + ONE)
                        nc.scalar.activation(ex[:], shift[:], ACT.Exp).then_inc(ex_rdy, 1)

            @block.vector
            def _(dve):
                dve.wait_ge(w_in, 48 + ONE)
                wide = [P, 4, NEXP]
                with dve.Fori(0, NCH // 2) as i:
                    for c in range(2):
                        n = c * ND

                        def then(op, last=True, constants=False):
                            nonlocal n
                            op.then_inc(d, 1)
                            n += 1
                            if last:
                                before = dve.to_reg(i * 2 * ND + n + ONE)
                                if constants:
                                    dve.wait_ge(w_in, 48 + ONE)
                                dve.wait_ge(d, before)
                        dve.wait_ge(lg_rdy, i * 2 + c + 1 + ONE)
                        then(nc.vector.tensor_tensor(logit[:], lg[c][:], rb[:].unsqueeze(1).to_broadcast(wide), ALU.add))
                        then(nc.vector.tensor_reduce(mx[:], logit[:], AX.X, ALU.max))
                        then(nc.vector.tensor_tensor(shift[:], logit[:], mx[:].unsqueeze(2).to_broadcast(wide), ALU.subtract))
                        dve.wait_ge(ex_rdy, i * 2 + c + 1 + ONE)
                        then(nc.vector.tensor_reduce(tot[:], ex[:], AX.X, ALU.add))
                        then(nc.vector.reciprocal(inv[:], tot[:]))
                        then(nc.vector.tensor_tensor(prob[:], ex[:], inv[:].unsqueeze(2).to_broadcast(wide), ALU.mult), constants=True)
                        for a in range(4):
                            then(nc.vector.max(top[:, a, :], prob[:, a, :]), a == 3, a == 3)
                        for a in range(4):
                            then(nc.vector.max_index(where[:, a, :], top[:, a, :], prob[:, a, :]), a == 3)
                        then(nc.vector.tensor_copy(wheref[:], where[:]))
                        it = iota[:].unsqueeze(1).to_broadcast(wide)
                        then(nc.vector.tensor_tensor(mask1[:], it, wheref[:, :, 0:1].to_broadcast(wide), ALU.is_equal))
                        then(nc.vector.tensor_tensor(mask[:], it, wheref[:, :, 1:2].to_broadcast(wide), ALU.is_equal))
                        then(nc.vector.tensor_tensor(mask[:], mask1[:], mask[:], ALU.add))
                        dst = weight[:, bass.ds(i * 8 + c * 4, 4), 0:NEXP]
                        if not normalise:
                            then(nc.vector.tensor_tensor(dst, prob[:], mask[:], ALU.mult))
                        else:
                            then(nc.vector.tensor_tensor(kept[:], prob[:], mask[:], ALU.mult))
                            then(nc.vector.tensor_reduce(tot2[:], kept[:], AX.X, ALU.add))
                            then(nc.vector.reciprocal(inv2[:], tot2[:]))
                            then(nc.vector.tensor_tensor(dst, kept[:], inv2[:].unsqueeze(2).to_broadcast(wide), ALU.mult))
                        assert n == (c + 1) * ND, (n, ND)


def load_split(nc, stage, jobs):
    with ExitStack() as ctx:
        m = Names(nc, ctx, stage)
        size = max(int(np.prod(hi.shape[1:])) for _, hi, _ in jobs)
        raw = [m.sb(f"raw{i}", [P, size]) for i in range(2)]
        ins = [m.sem(f"in{i}") for i in range(2)]
        hi_rdy, lo_rdy = m.sem("hi"), m.sem("lo")

        def view(n):
            hi = jobs[n][1]
            return raw[n % 2][:, 0:int(np.prod(hi.shape[1:]))].rearrange("p (k n) -> p k n", k=hi.shape[1])
        m.sem.start()
        with nc.Block() as block:
            @block.sync
            def _(sp):
                for n, (src, _, _) in enumerate(jobs):
                    if n >= 2:
                        sp.wait_ge(lo_rdy, n - 1 + ONE)
                    sp.dma_start(view(n), src).then_inc(ins[n % 2], 16)

            @block.scalar
            def _(act):
                for n, (_, hi, _) in enumerate(jobs):
                    act.wait_ge(ins[n % 2], 16 * (n // 2 + 1) + ONE)
                    nc.scalar.activation(hi[:], view(n), ACT.Copy).then_inc(hi_rdy, 1)

            @block.vector
            def _(dve):
                for n, (_, hi, lo) in enumerate(jobs):
                    dve.wait_ge(hi_rdy, n + 1 + ONE)
                    nc.vector.tensor_tensor(lo[:], view(n), hi[:].bitcast(F32), ALU.subtract).then_inc(lo_rdy, 1)


def product3(nc, out, left, right, start, stop):
    (lh, ll), (rh, rl) = left, right
    nc.tensor.matmul(out, ll, rh, start=start, stop=False)
    nc.tensor.matmul(out, lh, rl, start=False, stop=False)
    return nc.tensor.matmul(out, lh, rh, start=False, stop=stop)


RANK, FF = 64, 1024
ER = NEXP * RANK // P
FT = FF // P


def low_rank_ffn(nc, t, x, rows):
    with ExitStack() as ctx:
        m = Names(nc, ctx, "ffn0")
        pair = lambda n, s: (m.sb(n + "_hi", s, F32R), m.sb(n + "_lo", s, F32R))
        w1, w2, w3 = pair("w1", [P, EK2, NEXP * RANK]), pair("w2", [P, ER, FF]), pair("w3", [P, FT, E])
        load_split(nc, "ffn0w", [(t["w1"].rearrange("(k p) n -> p k n", p=P), *w1),
                                 (t["w2"].rearrange("(k p) n -> p k n", p=P), *w2),
                                 (t["w3"].rearrange("(k p) n -> p k n", p=P), *w3)])
        b3 = m.sb("b3", [P, EK2])
        wb = m.sb("wb", [P, ER, CH])
        xs = pair("xs", [P, EK2, CH])
        tt = m.sb("tt", [P, ER, CH])
        ts = pair("ts", [P, ER, CH])
        hf = [m.sb(f"hf{i}", [P, CH]) for i in range(2)]
        hs = pair("hs", [P, FT, CH])
        low = [m.ps(f"low{i}", [P, CH]) for i in range(2)]
        mid = [m.ps(f"mid{i}", [P, CH]) for i in range(2)]
        out = m.ps("out", [P, EK2, CH])
        b_in, wb_in, xh, xl, low_mm, tt_rdy, th, tl = (
            m.sem(n) for n in ("b_in", "wb_in", "xh", "xl", "low_mm", "tt", "th", "tl"))
        mid_mm, hf_rdy, hh, hl, out_mm, x_rdy = (m.sem(n) for n in ("mid_mm", "hf", "hh", "hl", "out_mm", "x"))
        m.sem.start()
        with nc.Block() as block:
            @block.sync
            def _(sp):
                sp.dma_start(b3[:], t["b3"]).then_inc(b_in, 16)
                experts = rows.rearrange("t (r h) n -> h r t n", h=P // RANK)
                with sp.Fori(0, NCH) as n:
                    sp.wait_ge(tt_rdy, n * ER + ONE)
                    for r in range(ER):
                        for h in range(P // RANK):
                            sp.dma_start(wb[h * RANK:(h + 1) * RANK, r, :].rearrange("p (t n) -> p t n", n=P),
                                         experts[h, r:r + 1, bass.ds(n * 4, 4), :].to_broadcast(
                                             [RANK, 4, P])).then_inc(wb_in, 16)

            @block.tensor
            def _(pe):
                def first(n):
                    pe.wait_ge(xl, n + 1 + ONE)
                    for r in range(ER):
                        pe.wait_ge(tt_rdy, n * ER + max(r - 1, 0) + ONE)
                        for k in range(EK2):
                            mm = product3(nc, low[r % 2][:], [w[:, k, r * P:(r + 1) * P] for w in w1],
                                          [a[:, k, :] for a in xs], k == 0, k == 1)
                        mm.then_inc(low_mm, 1)

                def second(n):
                    pe.wait_ge(tl, n * ER + ER + ONE)
                    for f in range(FT):
                        pe.wait_ge(hf_rdy, n * FT + max(f - 1, 0) + ONE)
                        for r in range(ER):
                            mm = product3(nc, mid[f % 2][:], [w[:, r, f * P:(f + 1) * P] for w in w2],
                                          [a[:, r, :] for a in ts], r == 0, r == ER - 1)
                        mm.then_inc(mid_mm, 1)

                def third(n):
                    pe.wait_ge(x_rdy, n + ONE)
                    for f in range(FT):
                        pe.wait_ge(hl, n * FT + f + 1 + ONE)
                        for e in range(EK2):
                            mm = product3(nc, out[:, e, :], [w[:, f, e * P:(e + 1) * P] for w in w3],
                                          [a[:, f, :] for a in hs], f == 0, f == FT - 1)
                    mm.then_inc(out_mm, 1)
                first(0)
                with pe.Fori(0, NCH - 1) as n:
                    second(n)
                    first(n + 1)
                    third(n)
                second(NCH - 1)
                third(NCH - 1)

            @block.scalar
            def _(act):
                def x_high(n):
                    act.wait_ge(low_mm, n * ER + ONE)
                    nc.scalar.activation(xs[0][:], x[:, :, bass.ds(n * CH, CH)], ACT.Copy).then_inc(xh, 1)

                def features_high(n):
                    act.wait_ge(mid_mm, n * FT + ONE)
                    for r in range(ER):
                        act.wait_ge(tt_rdy, n * ER + r + 1 + ONE)
                        nc.scalar.activation(ts[0][:, r, :], tt[:, r, :], ACT.Copy).then_inc(th, 1)

                def gelus(n):
                    for f in range(FT):
                        act.wait_ge(mid_mm, n * FT + f + 1 + ONE)
                        act.wait_ge(hl, n * FT + max(f - 1, 0) + ONE)
                        nc.scalar.activation(hf[f % 2][:], mid[f % 2][:], ACT.Gelu).then_inc(hf_rdy, 1)
                x_high(0)
                features_high(0)
                with act.Fori(0, NCH - 1) as n:
                    x_high(n + 1)
                    gelus(n)
                    features_high(n + 1)
                gelus(NCH - 1)

            @block.vector
            def _(dve):
                def x_low(n):
                    dve.wait_ge(xh, n + 1 + ONE)
                    nc.vector.tensor_tensor(xs[1][:], x[:, :, bass.ds(n * CH, CH)], xs[0][:].bitcast(F32),
                                            ALU.subtract).then_inc(xl, 1)

                def features(n):
                    dve.wait_ge(wb_in, n * (16 * NEXP) + 16 * NEXP + ONE)
                    dve.wait_ge(tl, n * ER + ONE)
                    for r in range(ER):
                        dve.wait_ge(low_mm, n * ER + r + 1 + ONE)
                        nc.vector.tensor_tensor(tt[:, r, :], low[r % 2][:], wb[:, r, :],
                                                ALU.mult).then_inc(tt_rdy, 1)
                    for r in range(ER):
                        dve.wait_ge(th, n * ER + r + 1 + ONE)
                        nc.vector.tensor_tensor(ts[1][:, r, :], tt[:, r, :], ts[0][:, r, :].bitcast(F32),
                                                ALU.subtract).then_inc(tl, 1)

                def splits(n):
                    dve.wait_ge(out_mm, n + ONE)
                    for f in range(FT):
                        dve.wait_ge(hf_rdy, n * FT + f + 1 + ONE)
                        nc.vector.tensor_copy(hs[0][:, f, :], hf[f % 2][:]).then_inc(hh, 1)
                        dve.wait_ge(hh, n * FT + f + 1 + ONE)
                        nc.vector.tensor_tensor(hs[1][:, f, :], hf[f % 2][:], hs[0][:, f, :].bitcast(F32),
                                                ALU.subtract).then_inc(hl, 1)

                def add(n):
                    dve.wait_ge(out_mm, n + 1 + ONE)
                    for e in range(EK2):
                        here = x[:, e, bass.ds(n * CH, CH)]
                        op = nc.vector.scalar_tensor_tensor(out=here, in0=out[:, e, :], scalar=b3[:, e:e + 1],
                                                            in1=here, op0=ALU.add, op1=ALU.add)
                    op.then_inc(x_rdy, 1)
                dve.wait_ge(b_in, 16 + ONE)
                x_low(0)
                features(0)
                with dve.Fori(0, NCH - 1) as n:
                    x_low(n + 1)
                    splits(n)
                    features(n + 1)
                    add(n)
                splits(NCH - 1)
                add(NCH - 1)


INNER, DH = 1024, 64
PAIRS = INNER // P
DQ = 32
VA = P + 2


def linear_keys(nc, t, x, kv, ks):
    with ExitStack() as ctx:
        m = Names(nc, ctx, "lk")
        w = (m.sb("w_hi", [P, EK2, 2 * INNER], F32R), m.sb("w_lo", [P, EK2, 2 * INNER], F32R))
        load_split(nc, "lkw", [(t["wkv"].rearrange("(k p) n -> p k n", p=P), *w)])
        xs = [(m.sb(f"xh{i}", [P, EK2, CH], F32R), m.sb(f"xl{i}", [P, EK2, CH], F32R)) for i in range(2)]
        ek = m.sb("ek", [P, INNER])
        em = m.sb("em", [P, INNER])
        kf = [m.sb(f"kf{i}", [P, INNER]) for i in range(2)]
        vn = [m.sb(f"vn{i}", [P, PAIRS, VA]) for i in range(2)]
        kacc = m.ps("kacc", [P, INNER])
        vacc = m.ps("vacc", [P, INNER])
        kvacc = [m.ps(f"kvacc{i}", [P, 3, VA]) for i in range(3)]
        ready, xh, xl, k_mm, v_mm, ek_rdy, em_rdy, kf_rdy, vn_rdy, kv_mm, kv_read = (
            m.sem(n) for n in ("ready", "xh", "xl", "k_mm", "v_mm", "ek", "em", "kf", "vn", "kv_mm", "kv_read"))
        NT = S // P
        m.sem.start()
        with nc.Block() as block:
            @block.tensor
            def _(pe):
                pe.wait_ge(ready, 4 + ONE)
                with pe.Fori(0, B) as b:
                    def sums(tile):
                        n = b * NT + tile
                        pe.wait_ge(kf_rdy, n + 1 + ONE)
                        pe.wait_ge(vn_rdy, n + 1 + ONE)
                        if tile == 0:
                            pe.wait_ge(kv_read, b * 4 + ONE)
                        for p in range(PAIRS):
                            mm = nc.tensor.matmul(kvacc[p // 3][:, p % 3, :], kf[tile % 2][:, p * P:(p + 1) * P],
                                                  vn[tile % 2][:, p, :], start=(tile == 0 and p % 3 == 0),
                                                  stop=(tile == NT - 1), skip_group_check=True)
                        mm.then_inc(kv_mm, 1)
                    for tile in range(NT):
                        n = b * NT + tile
                        c, a = tile // 4, tile % 4
                        if a == 0:
                            pe.wait_ge(xl, b * CPB + c + 1 + ONE)
                        for acc, done, mm_rdy, base in ((kacc, kf_rdy, k_mm, 0), (vacc, vn_rdy, v_mm, INNER)):
                            pe.wait_ge(done, n + ONE)
                            for h in range(2):
                                for k in range(EK2):
                                    cols = slice(base + h * CH, base + (h + 1) * CH)
                                    mm = product3(nc, acc[:, h * CH:(h + 1) * CH],
                                                  [s[:, k, a * P:(a + 1) * P] for s in xs[c % 2]],
                                                  [s[:, k, cols] for s in w], k == 0, k == 1)
                            mm.then_inc(mm_rdy, 1)
                        if tile:
                            sums(tile - 1)
                    sums(NT - 1)

            @block.scalar
            def _(act):
                act.wait_ge(ready, 4 + ONE)
                with act.Fori(0, B) as b:
                    for tile in range(NT):
                        n = b * NT + tile
                        if tile % 4 == 0:
                            act.wait_ge(v_mm, b * NT + max(tile - 4, 0) + ONE)
                            nc.scalar.activation(xs[tile // 4 % 2][0][:], x[:, :, bass.ds(b * S + tile * P, CH)],
                                                 ACT.Copy).then_inc(xh, 1)
                        act.wait_ge(k_mm, n + 1 + ONE)
                        act.wait_ge(em_rdy, n + ONE)
                        nc.scalar.activation(ek[:], kacc[:], ACT.Exp).then_inc(ek_rdy, 1)
                        act.wait_ge(v_mm, n + 1 + ONE)
                        act.wait_ge(kv_mm, b * NT + max(tile - 1, 0) + ONE)
                        nc.scalar.activation(vn[tile % 2][:, :, 0:P], vacc[:].rearrange("p (a n) -> p a n", a=PAIRS),
                                             ACT.Copy).then_inc(vn_rdy, 1)

            @block.vector
            def _(dve):
                for i in range(2):
                    nc.vector.memset(vn[i][:, :, P:VA], 1.0).then_inc(ready, 1)
                nc.vector.memset(kv[:], 0.0).then_inc(ready, 1)
                nc.vector.memset(ks[:], 0.0).then_inc(ready, 1)
                dve.wait_ge(ready, 4 + ONE)
                with dve.Fori(0, B) as b:
                    for tile in range(NT):
                        n = b * NT + tile
                        if tile % 4 == 0:
                            dve.wait_ge(xh, b * CPB + tile // 4 + 1 + ONE)
                            nc.vector.tensor_tensor(xs[tile // 4 % 2][1][:], x[:, :, bass.ds(b * S + tile * P, CH)],
                                                    xs[tile // 4 % 2][0][:].bitcast(F32), ALU.subtract).then_inc(xl, 1)
                        dve.wait_ge(ek_rdy, n + 1 + ONE)
                        dve.wait_ge(kf_rdy, n + ONE)
                        nc.vector.tensor_scalar(em[:], ek[:], 1.0, None, ALU.min).then_inc(em_rdy, 1)
                        dve.wait_ge(em_rdy, n + 1 + ONE)
                        dve.wait_ge(kv_mm, b * NT + max(tile - 1, 0) + ONE)
                        nc.vector.scalar_tensor_tensor(out=kf[tile % 2][:], in0=kacc[:], scalar=0.0, in1=em[:],
                                                       op0=ALU.max, op1=ALU.add).then_inc(kf_rdy, 1)
                    dve.wait_ge(kv_mm, b * NT + NT + ONE)
                    for h in range(2):
                        rows = slice(h * DH, (h + 1) * DH)
                        for g in range(3):
                            np_ = min(3, PAIRS - 3 * g)
                            op = nc.vector.tensor_copy(kv[rows, bass.ds(b * PAIRS + 3 * g, np_), rows],
                                                       kvacc[g][rows, 0:np_, rows])
                            for p in range(3 * g, 3 * g + np_):
                                op2 = nc.vector.tensor_copy(ks[rows, bass.ds(b * PAIRS + p, 1), 2 * p + h:2 * p + h + 1],
                                                            kvacc[g][rows, p % 3:p % 3 + 1, P:P + 1])
                        op.then_inc(kv_read, 1)
                        op2.then_inc(kv_read, 1)


def linear_attention(nc, t, x, kv, ks):
    with ExitStack() as ctx:
        m = Names(nc, ctx, "la")
        pair = lambda n, s: (m.sb(n + "_hi", s, F32R), m.sb(n + "_lo", s, F32R))
        wq, wo = pair("wq", [P, EK2, INNER]), pair("wo", [P, PAIRS, E])
        load_split(nc, "law", [(t["wq1"].rearrange("(k p) n -> p k n", p=P), *wq),
                               (t["wout"].rearrange("(k p) n -> p k n", p=P), *wo)])
        bo = m.sb("bo", [P, EK2])
        spread_in = m.sb("spread_in", [2 * DQ, PAIRS, P])
        spread = m.sb("spread", [2 * DQ, PAIRS, P], F32R)
        xs = pair("xs", [P, EK2, CH])
        eq, em, iv, of = ([m.sb(f"{n}{i}", [P, CH]) for i in range(2)] for n in ("eq", "em", "iv", "of"))
        qf = m.sb("qf", [P, PAIRS, CH])
        dn, rd = m.sb("dn", [2 * PAIRS, CH]), m.sb("rd", [2 * PAIRS, CH])
        rs = m.sb("rs", [2 * DQ, CH], F32R)
        os_ = pair("os", [P, PAIRS, CH])
        qacc = [m.ps(f"qacc{i}", [P, CH]) for i in range(2)]
        num = [m.ps(f"num{i}", [P, CH]) for i in range(2)]
        den, inv = m.ps("den", [P, CH]), m.ps("inv", [P, CH])
        out = m.ps("out", [P, EK2, CH])
        ready, b_in, xh, xl, q_mm, eq_rdy, em_rdy, qf_rdy = (
            m.sem(n) for n in ("ready", "b_in", "xh", "xl", "q_mm", "eq", "em", "qf"))
        iv_rdy = m.sem("iv")
        den_mm, dn_rdy, rd_rdy, rh_rdy, rl_rdy, num_mm, inv_mm, of_rdy, oh, ol, out_mm, x_rdy = (
            m.sem(n) for n in ("den_mm", "dn", "rd", "rh", "rl", "num_mm", "inv_mm", "of", "oh", "ol", "out_mm", "x"))
        m.sem.start()
        with nc.Block() as block:
            @block.sync
            def _(sp):
                sp.dma_start(bo[:], t["bout"]).then_inc(b_in, 16)
                sp.dma_start(spread_in[:], t["spread"]).then_inc(b_in, 16)

            @block.tensor
            def _(pe):
                pe.wait_ge(ready, 2 + ONE)

                def queries(n, b):
                    pe.wait_ge(xl, n + 1 + ONE)

                    def denominators(p):
                        pe.wait_ge(qf_rdy, n * PAIRS + p + 1 + ONE)
                        if p == 0:
                            pe.wait_ge(dn_rdy, n + ONE)
                        mm = nc.tensor.matmul(den[0:2 * PAIRS, :], ks[:, b * PAIRS + p, :], qf[:, p, :],
                                              start=(p == 0), stop=(p == PAIRS - 1))
                        if p == PAIRS - 1:
                            mm.then_inc(den_mm, 1)
                    for p in range(PAIRS):
                        pe.wait_ge(qf_rdy, n * PAIRS + max(p - 1, 0) + ONE)
                        for k in range(EK2):
                            mm = product3(nc, qacc[p % 2][:], [w[:, k, p * P:(p + 1) * P] for w in wq],
                                          [a[:, k, :] for a in xs], k == 0, k == 1)
                        mm.then_inc(q_mm, 1)
                        if p >= 2:
                            denominators(p - 2)
                    denominators(PAIRS - 2)
                    denominators(PAIRS - 1)

                def heads(n, b):
                    for p in range(PAIRS):
                        pe.wait_ge(of_rdy, n * PAIRS + max(p - 1, 0) + ONE)
                        nc.tensor.matmul(num[p % 2][:], kv[:, b * PAIRS + p, :], qf[:, p, :],
                                         start=True, stop=True).then_inc(num_mm, 1)
                        if p == 0:
                            pe.wait_ge(rl_rdy, n + 1 + ONE)
                        pe.wait_ge(iv_rdy, n * PAIRS + p + ONE)
                        nc.tensor.matmul(inv[:], spread[:, p, :], rs[:], start=True, stop=True).then_inc(inv_mm, 1)

                def project(n):
                    pe.wait_ge(x_rdy, n + ONE)
                    for p in range(PAIRS):
                        pe.wait_ge(ol, n * PAIRS + p + 1 + ONE)
                        for e in range(EK2):
                            mm = product3(nc, out[:, e, :], [w[:, p, e * P:(e + 1) * P] for w in wo],
                                          [a[:, p, :] for a in os_], p == 0, p == PAIRS - 1)
                    mm.then_inc(out_mm, 1)
                queries(0, 0)
                for b in range(B):
                    with pe.Fori(b * CPB, (b + 1) * CPB - 1) as n:
                        heads(n, b)
                        queries(n + 1, b)
                        project(n)
                    last = (b + 1) * CPB - 1
                    heads(last, b)
                    if b + 1 < B:
                        queries(last + 1, b + 1)
                    project(last)

            @block.scalar
            def _(act):
                def queries(n):
                    act.wait_ge(q_mm, n * PAIRS + ONE)
                    nc.scalar.activation(xs[0][:], x[:, :, bass.ds(n * CH, CH)], ACT.Copy).then_inc(xh, 1)
                    for p in range(PAIRS):
                        act.wait_ge(q_mm, n * PAIRS + p + 1 + ONE)
                        act.wait_ge(em_rdy, n * PAIRS + max(p - 1, 0) + ONE)
                        nc.scalar.activation(eq[p % 2][:], qacc[p % 2][:], ACT.Exp).then_inc(eq_rdy, 1)
                    act.wait_ge(rd_rdy, n + 1 + ONE)
                    act.wait_ge(inv_mm, n * PAIRS + ONE)
                    nc.scalar.activation(rs[0:2 * PAIRS, :], rd[:], ACT.Copy).then_inc(rh_rdy, 1)

                def heads(n):
                    act.wait_ge(out_mm, n + ONE)
                    def high(p):
                        act.wait_ge(of_rdy, n * PAIRS + p + 1 + ONE)
                        nc.scalar.activation(os_[0][:, p, :], of[p % 2][:], ACT.Copy).then_inc(oh, 1)
                    for p in range(PAIRS):
                        act.wait_ge(inv_mm, n * PAIRS + p + 1 + ONE)
                        act.wait_ge(of_rdy, n * PAIRS + max(p - 1, 0) + ONE)
                        nc.scalar.activation(iv[p % 2][:], inv[:], ACT.Copy).then_inc(iv_rdy, 1)
                        if p:
                            high(p - 1)
                    high(PAIRS - 1)
                act.wait_ge(b_in, 32 + ONE)
                nc.scalar.activation(spread[:], spread_in[:], ACT.Copy).then_inc(ready, 1)
                act.wait_ge(ready, 2 + ONE)
                queries(0)
                with act.Fori(0, NCH - 1) as n:
                    heads(n)
                    queries(n + 1)
                heads(NCH - 1)

            @block.vector
            def _(dve):
                def queries(n):
                    dve.wait_ge(xh, n + 1 + ONE)
                    nc.vector.tensor_tensor(xs[1][:], x[:, :, bass.ds(n * CH, CH)], xs[0][:].bitcast(F32),
                                            ALU.subtract).then_inc(xl, 1)
                    dve.wait_ge(num_mm, n * PAIRS + ONE)
                    for p in range(PAIRS):
                        dve.wait_ge(eq_rdy, n * PAIRS + p + 1 + ONE)
                        dve.wait_ge(qf_rdy, n * PAIRS + max(p - 1, 0) + ONE)
                        nc.vector.tensor_scalar(em[p % 2][:], eq[p % 2][:], 1.0, None, ALU.min).then_inc(em_rdy, 1)
                        dve.wait_ge(em_rdy, n * PAIRS + p + 1 + ONE)
                        nc.vector.scalar_tensor_tensor(out=qf[:, p, :], in0=qacc[p % 2][:], scalar=0.0, in1=em[p % 2][:],
                                                       op0=ALU.max, op1=ALU.add).then_inc(qf_rdy, 1)

                def reciprocals(n):
                    dve.wait_ge(den_mm, n + 1 + ONE)
                    dve.wait_ge(rd_rdy, n + ONE)
                    nc.vector.tensor_scalar(dn[:], den[0:2 * PAIRS, :], 1e-6, None, ALU.add).then_inc(dn_rdy, 1)
                    dve.wait_ge(dn_rdy, n + 1 + ONE)
                    dve.wait_ge(rl_rdy, n + ONE)
                    nc.vector.reciprocal(rd[:], dn[:]).then_inc(rd_rdy, 1)
                    dve.wait_ge(rh_rdy, n + 1 + ONE)
                    nc.vector.tensor_tensor(rs[DQ:DQ + 2 * PAIRS, :], rd[:], rs[0:2 * PAIRS, :].bitcast(F32),
                                            ALU.subtract).then_inc(rl_rdy, 1)

                def heads(n):
                    def low_of(p):
                        dve.wait_ge(oh, n * PAIRS + p + 1 + ONE)
                        nc.vector.tensor_tensor(os_[1][:, p, :], of[p % 2][:], os_[0][:, p, :].bitcast(F32),
                                                ALU.subtract).then_inc(ol, 1)
                    for p in range(PAIRS):
                        dve.wait_ge(num_mm, n * PAIRS + p + 1 + ONE)
                        dve.wait_ge(iv_rdy, n * PAIRS + p + 1 + ONE)
                        dve.wait_ge(ol, n * PAIRS + max(p - 1, 0) + ONE)
                        nc.vector.tensor_tensor(of[p % 2][:], num[p % 2][:], iv[p % 2][:], ALU.mult).then_inc(of_rdy, 1)
                        if p:
                            low_of(p - 1)
                    low_of(PAIRS - 1)

                def add(n):
                    dve.wait_ge(out_mm, n + 1 + ONE)
                    for e in range(EK2):
                        here = x[:, e, bass.ds(n * CH, CH)]
                        op = nc.vector.scalar_tensor_tensor(out=here, in0=out[:, e, :], scalar=bo[:, e:e + 1],
                                                            in1=here, op0=ALU.add, op1=ALU.add)
                    op.then_inc(x_rdy, 1)
                nc.vector.memset(rs[:].bitcast(F32), 0.0).then_inc(ready, 1)
                dve.wait_ge(b_in, 32 + ONE)
                dve.wait_ge(ready, 2 + ONE)
                queries(0)
                reciprocals(0)
                with dve.Fori(0, NCH - 1) as n:
                    heads(n)
                    queries(n + 1)
                    reciprocals(n + 1)
                    add(n)
                heads(NCH - 1)
                add(NCH - 1)


HF = 512
HT = HF // P


def router_weights(nc, stage, t, weight, rows):
    with ExitStack() as ctx:
        m = Names(nc, ctx, stage)
        ident = m.sb("ident", [P, P])
        turned = m.sb("turned", [P, 2, P])
        acc = m.ps("acc", [P, 2, P])
        ident_in, acc_rdy, turned_rdy, out_done = (m.sem(n) for n in ("ident", "acc", "turned", "out"))
        m.sem.start()
        with nc.Block() as block:
            @block.sync
            def _(sp):
                sp.dma_start(ident[:], t["ident"]).then_inc(ident_in, 16)
                sp.wait_ge(turned_rdy, 1 + ONE)
                sp.dma_start(rows.rearrange("(a t) e n -> (t e) a n", a=2), turned[:]).then_inc(out_done, 16)
                sp.wait_ge(out_done, 16 + ONE)

            @block.tensor
            def _(pe):
                pe.wait_ge(ident_in, 16 + ONE)
                for a in range(2):
                    mm = nc.tensor.matmul(acc[:, a, :], weight[:, a * TILES // 2:(a + 1) * TILES // 2, :].rearrange(
                        "p t e -> p (t e)"), ident[:], start=True, stop=True)
                mm.then_inc(acc_rdy, 1)

            @block.scalar
            def _(act):
                act.wait_ge(acc_rdy, 1 + ONE)
                nc.scalar.activation(turned[:], acc[:], ACT.Copy).then_inc(turned_rdy, 1)


def routed_ffn(nc, t, x, rows):
    with ExitStack() as ctx:
        m = Names(nc, ctx, "ffn1")
        xh, xl = m.sb("xh", [P, EK2, T], F32R), m.sb("xl", [P, EK2, T], F32R)
        raw = m.sb("raw", [P, 3, HT * E])
        wh = [m.sb(f"wh{i}", [P, 3, HT * E], F32R) for i in range(2)]
        wl = [m.sb(f"wl{i}", [P, 3, HT * E], F32R) for i in range(2)]
        wb = [m.sb(f"wb{i}", [P, CH]) for i in range(2)]
        sg = [m.sb(f"sg{i}", [P, CH]) for i in range(2)]
        su = m.sb("su", [P, CH])
        hw = [m.sb(f"hw{i}", [P, CH]) for i in range(2)]
        hh = [m.sb(f"hh{i}", [P, HT, CH], F32R) for i in range(2)]
        hl = [m.sb(f"hl{i}", [P, HT, CH], F32R) for i in range(2)]
        gate = [m.ps(f"gate{i}", [P, CH]) for i in range(2)]
        up = [m.ps(f"up{i}", [P, CH]) for i in range(2)]
        out = m.ps("out", [P, EK2, CH])
        xh_rdy, xl_rdy, raw_in, wh_rdy, wl_rdy, one_rdy = (m.sem(n) for n in ("xh", "xl", "raw_in", "wh", "wl", "one"))
        wb_in = [m.sem(f"wb_in{i}") for i in range(2)]
        gu_mm, sg_rdy, su_rdy, hw_rdy, hh_rdy, hl_rdy, out_mm, x_rdy = (
            m.sem(n) for n in ("gu_mm", "sg", "su", "hw", "hh", "hl", "out_mm", "x"))
        NE = NEXP + 1
        assert NCH % 2 == 0 and NEXP % 2 == 0

        def operand(i, which, k, a, b):
            n = HF if which < 2 else E
            return [w[i][:, which, k * n + a:k * n + b] for w in (wh, wl)]

        def every_expert(eng, expert):
            expert(0, 0)
            with eng.Fori(0, NEXP // 2 - 1) as pair:
                expert(pair * 2 + 1, 1)
                expert(pair * 2 + 2, 0)
            expert(NE - 2, 1)
            expert(NE - 1, 0, True)

        def every_chunk(eng, g, body):
            for c in range(2):
                body(g * NCH + c, c, c, c)
            with eng.Fori(1, NCH // 2) as pair:
                for i in range(2):
                    body(g * NCH + pair * 2 + i, pair * 2 + i, i, None)

        m.sem.start()
        with nc.Block() as block:
            @block.sync
            def _(sp):
                def load_weights(g):
                    sp.wait_ge(wl_rdy, g + ONE)
                    sp.dma_start(raw[:].rearrange("p a n -> p (a n)"), t["experts"].rearrange("e p n -> p e n")[
                        :, bass.ds(g, 1)].rearrange("p e n -> p (e n)")).then_inc(raw_in, 16)

                def expert(g, i, final=False):
                    if type(g) is int and g == 0:
                        load_weights(0)
                        load_weights(1)
                        return
                    if not final:
                        load_weights(g + 1)
                    with sp.Fori(0, NCH // 2) as pair:
                        for b in range(2):
                            sp.wait_ge(hw_rdy, (g * NCH + pair * 2 + b - 1) * HT + ONE)
                            sp.dma_start(wb[b][:].rearrange("p (t n) -> p t n", n=P), rows.rearrange("t e n -> e t n")[
                                bass.ds(g - 1, 1), bass.ds(pair * 8 + b * 4, 4)].to_broadcast([P, 4, P])).then_inc(wb_in[b], 16)
                every_expert(sp, expert)

            @block.tensor
            def _(pe):
                pe.wait_ge(xl_rdy, NCH + ONE)

                def down(n, b, i):
                    pe.wait_ge(x_rdy, n + ONE)
                    for h in range(HT):
                        pe.wait_ge(hl_rdy, n * HT + h + 1 + ONE)
                        for e in range(EK2):
                            mm = product3(nc, out[:, e, :], operand(i, 2, h, e * P, (e + 1) * P),
                                          [hh[b][:, h, :], hl[b][:, h, :]], h == 0, h == HT - 1)
                    mm.then_inc(out_mm, 1)

                def expert(g, i, final=False):
                    pe.wait_ge(wl_rdy, g + 1 + ONE)

                    def chunk(n, c, b, first):
                        for h in range(HT):
                            pe.wait_ge(su_rdy, n * HT + max(h - 1, 0) + ONE)
                            for which, acc in ((0, gate), (1, up)):
                                for k in range(EK2):
                                    mm = product3(nc, acc[h % 2][:], operand(i, which, k, h * P, (h + 1) * P),
                                                  [s[:, k, bass.ds(c * CH, CH)] for s in (xh, xl)], k == 0, k == 1)
                            mm.then_inc(gu_mm, 1)
                        if first != 0:
                            down(n - 1, 1 - b, i)
                        elif not (type(g) is int and g == 0):
                            down(n - 1, 1 - b, 1 - i)
                    every_chunk(pe, g, chunk)
                    if final:
                        down(NE * NCH - 1, 1, i)
                every_expert(pe, expert)

            @block.scalar
            def _(act):
                with act.Fori(0, NCH) as n:
                    nc.scalar.activation(xh[:, :, bass.ds(n * CH, CH)], x[:, :, bass.ds(n * CH, CH)],
                                         ACT.Copy).then_inc(xh_rdy, 1)

                def split_high(g, i):
                    act.wait_ge(raw_in, g * 16 + 16 + ONE)
                    nc.scalar.activation(wh[i][:], raw[:], ACT.Copy).then_inc(wh_rdy, 1)
                split_high(0, 0)

                def expert(g, i, final=False):
                    def chunk(n, c, b, first):
                        def high(h):
                            act.wait_ge(hw_rdy, n * HT + h + 1 + ONE)
                            if not (type(n) is int and n == 0):
                                act.wait_ge(out_mm, n - 1 + ONE)
                            nc.scalar.activation(hh[b][:, h, :], hw[h % 2][:], ACT.Copy).then_inc(hh_rdy, 1)
                        for h in range(HT):
                            act.wait_ge(gu_mm, n * HT + h + 1 + ONE)
                            act.wait_ge(su_rdy, n * HT + max(h - 1, 0) + ONE)
                            nc.scalar.activation(sg[h % 2][:], gate[h % 2][:], ACT.Silu).then_inc(sg_rdy, 1)
                            if h:
                                high(h - 1)
                        high(HT - 1)
                        if first == 1 and not final:
                            act.wait_ge(out_mm, g * NCH + ONE)
                            split_high(g + 1, 1 - i)
                    every_chunk(act, g, chunk)
                every_expert(act, expert)

            @block.vector
            def _(dve):
                for i in range(2):
                    nc.vector.memset(wb[i][:], 1.0).then_inc(one_rdy, 1)
                dve.wait_ge(one_rdy, 2 + ONE)
                with dve.Fori(0, NCH) as n:
                    dve.wait_ge(xh_rdy, n + 1 + ONE)
                    nc.vector.tensor_tensor(xl[:, :, bass.ds(n * CH, CH)], x[:, :, bass.ds(n * CH, CH)],
                                            xh[:, :, bass.ds(n * CH, CH)].bitcast(F32), ALU.subtract).then_inc(xl_rdy, 1)

                def split_low(g, i):
                    dve.wait_ge(wh_rdy, g + 1 + ONE)
                    nc.vector.tensor_tensor(wl[i][:], raw[:], wh[i][:].bitcast(F32), ALU.subtract).then_inc(wl_rdy, 1)
                split_low(0, 0)

                def add(n, c):
                    dve.wait_ge(out_mm, n + 1 + ONE)
                    dve.wait_ge(x_rdy, n + ONE)
                    here = x[:, :, bass.ds(c * CH, CH)]
                    nc.vector.tensor_tensor(here, here, out[:], ALU.add).then_inc(x_rdy, 1)

                def expert(g, i, final=False):
                    shared = type(g) is int and g == 0

                    def chunk(n, c, b, first):
                        def low(h):
                            dve.wait_ge(hh_rdy, n * HT + h + 1 + ONE)
                            nc.vector.tensor_tensor(hl[b][:, h, :], hw[h % 2][:], hh[b][:, h, :].bitcast(F32),
                                                    ALU.subtract).then_inc(hl_rdy, 1)
                        if not shared:
                            loads = (n - NCH - b) * 8 + 16
                            dve.wait_ge(wb_in[b], loads + ONE)
                        for h in range(HT):
                            dve.wait_ge(sg_rdy, n * HT + h + 1 + ONE)
                            dve.wait_ge(hw_rdy, n * HT + h + ONE)
                            nc.vector.tensor_tensor(su[:], sg[h % 2][:], up[h % 2][:], ALU.mult).then_inc(su_rdy, 1)
                            dve.wait_ge(su_rdy, n * HT + h + 1 + ONE)
                            dve.wait_ge(hl_rdy, n * HT + max(h - 1, 0) + ONE)
                            nc.vector.tensor_tensor(hw[h % 2][:], su[:], wb[b][:], ALU.mult).then_inc(hw_rdy, 1)
                            if h:
                                low(h - 1)
                            if h == 0 and not (shared and first is not None):
                                add(n - 2, c - 2 if first is None else NCH - 2 + c)
                        low(HT - 1)
                        if first == 1 and not final:
                            split_low(g + 1, 1 - i)
                    every_chunk(dve, g, chunk)
                    if final:
                        for c in (NCH - 2, NCH - 1):
                            add(NEXP * NCH + c, c)
                every_expert(dve, expert)


def transformer(nc, t, out):
    dram = lambda n, s, d: nc.dram_tensor(n, s, d, kind="Internal").ap()
    scratch = (dram("q_parts", [3, NHP * HD, S], BF16), dram("k_late", [3, NHP * HD, S], BF16),
               dram("k_early", [3, NHP * HD, S], BF16), dram("v_heads", [NHP, P, KT * HD], F32))
    sums = (dram("value_sums", [NH * HD, S], F32), dram("band_sums", [(NH + 2) * HD, S], F32),
            dram("denominators", [NH, S], F32))
    inverse = dram("inverse_denominators", [NH, S], F32)
    project_qkv(nc, t, scratch)
    attention(nc, t, scratch, sums)
    rows = dram("router_rows", [TILES, NEXP, P], F32)
    with nc.sbuf_tensor("x", [P, EK2, T], F32) as x, nc.sbuf_tensor("weight", [P, TILES, NEXP], F32) as weight:
        invert_denominators(nc, sums[2], inverse)
        project_attention(nc, t, sums[:2], inverse, x)
        layer_norm(nc, "ln0", x)
        route(nc, "route0", t, x, weight, False)
        router_weights(nc, "rows0", t, weight, rows)
        low_rank_ffn(nc, t, x, rows)
        layer_norm(nc, "ln1", x)
        with nc.sbuf_tensor("kv", [P, B * PAIRS, P], F32) as kv, nc.sbuf_tensor("ks", [P, B * PAIRS, 2 * PAIRS], F32) as ks:
            linear_keys(nc, t, x, kv, ks)
            linear_attention(nc, t, x, kv, ks)
        layer_norm(nc, "ln2", x)
        route(nc, "route1", t, x, weight, True)
        router_weights(nc, "rows1", t, weight, rows)
        routed_ffn(nc, t, x, rows)
        layer_norm(nc, "ln3", x, out)


def layouts(i):
    c = np.ascontiguousarray
    heads = lambda v: np.tile(v, H)
    halves = lambda v: c(v.reshape(EK2, P).T)
    rk, rv = i["L0_attn_rel_k"], i["L0_attn_rel_v"]
    far = 2 * REL
    place = lambda d: np.clip(d, -REL, REL) + REL
    masks = np.zeros((KS, 3), np.float32)
    for r, p in enumerate(K_PARTS):
        masks[r * HD:(r + 1) * HD, p] = 1
    m, w = np.meshgrid(np.arange(P), np.arange(W), indexing="ij")

    def expert(g, u, d):
        rows = lambda a: a.reshape(-1, P, a.shape[1]).transpose(1, 0, 2).reshape(P, -1)
        return np.concatenate([rows(c(g.T)), rows(c(u.T)), rows(c(d.T))], 1)
    experts = [expert(i["L1_ffn_sg"], i["L1_ffn_su"], i["L1_ffn_sd"])] + [
        expert(i["L1_ffn_eg"][e], i["L1_ffn_eu"][e], i["L1_ffn_ed"][e]) for e in range(NEXP)]
    wqkv = i["L1_attn_Wqkv"]
    spread = np.zeros((2 * DQ, PAIRS, P), np.float32)
    for head in range(2 * PAIRS):
        spread[[head, DQ + head], head // 2, head % 2 * DH:(head % 2 + 1) * DH] = 1
    return {
        "xt": c(i["L0_attn_hidden_states"].reshape(T, E).T),
        "wqkv": c(np.stack([i[f"L0_attn_W{n}"].T for n in "qkv"])),
        "cols": c(np.stack([i["L0_attn_bq"], i["L0_attn_bk"], heads(rk[far]), heads(rk[0])], 1)),
        "rows": c(np.broadcast_to(i["L0_attn_bv"], (P, E))),
        "rk": c(np.tile(rk[place(np.arange(TAB) - (W - 1 - PAD))].T, (NPT, 1))),
        "rkb": c(np.tile(np.stack([rk[far], rk[0]], 1), (NPT, 1))),
        "msk": masks,
        "rv": c(rv[place(m - w + PAD)]),
        "rvb": c(np.broadcast_to(np.stack([rv[far], rv[0]]), (P, 2, HD))),
        "wo": c(i["L0_attn_Wo"].T), "bo": halves(i["L0_attn_bo"]),
        "route0_w": c(i["L0_ffn_router_w"]), "route0_b": c(np.broadcast_to(i["L0_ffn_router_b"], (P, NEXP))),
        "route1_w": c(i["L1_ffn_router_w"].T), "route1_b": np.zeros((P, NEXP), np.float32),
        "iota": c(np.broadcast_to(np.arange(NEXP, dtype=np.float32), (P, NEXP))),
        "ident": np.eye(P, dtype=np.float32),
        "w1": c(i["L0_ffn_w1"].transpose(1, 0, 2).reshape(E, NEXP * RANK)),
        "w2": c(i["L0_ffn_w2"].reshape(NEXP * RANK, FF)),
        "w3": c(i["L0_ffn_lin2_w"]), "b3": halves(i["L0_ffn_lin2_b"]),
        "wkv": c(wqkv[:, INNER:]), "wq1": c(wqkv[:, :INNER]),
        "wout": c(i["L1_attn_Wout"]), "bout": halves(i["L1_attn_bout"]),
        "spread": spread,
        "experts": c(np.stack(experts)),
    }


def kernel(**inputs):
    import concourse.bacc as bacc
    from concourse.bass_utils import run_bass_kernel_spmd

    nc = bacc.Bacc("TRN2", target_bir_lowering=False, num_devices=1)
    arrays = {f"in_{n}": a for n, a in layouts({n: np.asarray(a) for n, a in inputs.items()}).items()}
    t = {n[3:]: nc.dram_tensor(n, a.shape, mybir.dt.from_np(a.dtype), kind="ExternalInput").ap()
         for n, a in arrays.items()}
    out = nc.dram_tensor("out_t", [E, T], F32, kind="ExternalOutput").ap()
    transformer(nc, t, out)
    got = run_bass_kernel_spmd(nc, [arrays], core_ids=[0])
    return np.ascontiguousarray(got.results[0]["out_t"].T).reshape(B, S, E)
```
